# Optimizing a Trainium2 kernel written in Bass

```python
import numpy as np
import jax
import jax.numpy as jnp

def _softmax(x, axis=-1):
    return jax.nn.softmax(x, axis=axis)

def _gelu(x):
    return jax.nn.gelu(x, approximate=True)

def _silu(x):
    return jax.nn.silu(x)

def _sigmoid(x):
    return jax.nn.sigmoid(x)

def _layernorm(x, axis=-1, eps=1e-05):
    m = jnp.mean(x, axis=axis, keepdims=True)
    v = jnp.var(x, axis=axis, keepdims=True)
    return (x - m) / jnp.sqrt(v + eps)

def _scatter_add(tgt, idx, src, axis=0):
    return tgt.at[idx].add(src)

def _segment_sum(src, seg, n):
    return jax.ops.segment_sum(src, seg, n)
kernel_name = 'mk_metaformer_d1_conv_nhwc256_r2_6b6798'

def setup_inputs(seed: int=0):
    np.random.seed(seed)
    _w = jnp.asarray

    def _rec_inputs():
        import jax
        import jax.numpy as jnp
        _gk = jax.random.key(seed)
        x = -0.000125 + 0.9999 * jax.random.normal(jax.random.fold_in(_gk, 1), (32, 32, 32, 128), jnp.float32)
        return x
    x = _rec_inputs()

    def _L0_conv_setup():
        import jax, jax.numpy as jnp
        import numpy as np
        M, H, W, D = (32, 32, 32, 128)
        WH, WW = (8, 8)
        SH, SW = (4, 4)
        NH = 8
        NEG = -1000000000.0
        NW = H // WH * (W // WW)
        WS = WH * WW

        def _window_partition(x):
            m, d = (x.shape[0], x.shape[-1])
            x = x.reshape(m, H // WH, WH, W // WW, WW, d)
            x = x.transpose(0, 1, 3, 2, 4, 5)
            return x.reshape(m * NW, WS, d)

        def _window_reverse(x):
            d = x.shape[-1]
            m = x.shape[0] // NW
            x = x.reshape(m, H // WH, W // WW, WH, WW, d)
            x = x.transpose(0, 1, 3, 2, 4, 5)
            return x.reshape(m, H, W, d)

        def _shift_mask():
            img = np.zeros((H, W), np.int32)
            cnt = 0
            for hs in (slice(0, -WH), slice(-WH, -SH), slice(-SH, None)):
                for ws_ in (slice(0, -WW), slice(-WW, -SW), slice(-SW, None)):
                    img[hs, ws_] = cnt
                    cnt += 1
            mw = img.reshape(H // WH, WH, W // WW, WW).transpose(0, 2, 1, 3).reshape(NW, WS)
            diff = mw[:, None, :] - mw[:, :, None]
            return jnp.asarray(np.where(diff != 0, NEG, 0.0).astype(np.float32))

        def _mhsa(x, w_qkv, b_qkv, w_o, b_o, mask):
            B, S, _ = x.shape
            hd = D // NH
            qkv = x @ w_qkv + b_qkv
            q, k, v = jnp.split(qkv, 3, axis=-1)
            q = q.reshape(B, S, NH, hd)
            k = k.reshape(B, S, NH, hd)
            v = v.reshape(B, S, NH, hd)
            scores = jnp.einsum('bqhd,bkhd->bhqk', q, k) / jnp.sqrt(jnp.float32(hd))
            if mask is not None:
                scores = scores + mask[:, None, :, :]
            attn = jax.nn.softmax(scores, axis=-1)
            out = jnp.einsum('bhqk,bkhd->bqhd', attn, v).reshape(B, S, D)
            return out @ w_o + b_o
        key = jax.random.key(seed)
        ks = jax.random.split(key, 4)
        return {'x': jax.random.normal(ks[0], (M, H, W, D), jnp.float32), 'w_qkv': 0.02 * jax.random.normal(ks[1], (D, 3 * D), jnp.float32), 'b_qkv': jnp.zeros((3 * D,), jnp.float32), 'w_o': 0.02 * jax.random.normal(ks[2], (D, D), jnp.float32), 'b_o': jnp.zeros((D,), jnp.float32)}
    _L0_conv_all = _L0_conv_setup()
    _L0_conv_in = {k: v for k, v in _L0_conv_all.items() if k in ('w_qkv', 'b_qkv', 'w_o', 'b_o')}
    del _L0_conv_all

    def _L0_ffn_setup():
        import jax, jax.numpy as jnp
        import numpy as np
        B, N, D = (16, 2048, 128)
        NUM_EXPERTS, TOP_K, HEADS = (4, 2, 4)
        N_EDGES = 524288
        LN_EPS = 1e-05

        def _layernorm(x, g, b):
            mu = x.mean(-1, keepdims=True)
            var = ((x - mu) ** 2).mean(-1, keepdims=True)
            return (x - mu) * jax.lax.rsqrt(var + LN_EPS) * g + b

        def _forward(x, edge_index, W_gat, att_src, att_dst, b_gat, ln_gamma, ln_beta, W1, b1, W2, b2):
            Bc, Nc, Dc = x.shape
            M = Bc * Nc
            x_flat = x.reshape(M, Dc)
            h = (x_flat @ W_gat).reshape(M, HEADS, NUM_EXPERTS)
            loops = jnp.arange(M, dtype=edge_index.dtype)
            src = jnp.concatenate([edge_index[0], loops])
            dst = jnp.concatenate([edge_index[1], loops])
            a_src = (h * att_src).sum(-1)
            a_dst = (h * att_dst).sum(-1)
            e = jax.nn.leaky_relu(a_src[src] + a_dst[dst], negative_slope=0.2)
            e_max = jax.ops.segment_max(e, dst, num_segments=M)
            ee = jnp.exp(e - e_max[dst])
            denom = jax.ops.segment_sum(ee, dst, num_segments=M)
            alpha = ee / (denom[dst] + 1e-16)
            msg = h[src] * alpha[:, :, None]
            agg = jax.ops.segment_sum(msg, dst, num_segments=M).reshape(M, HEADS * NUM_EXPERTS) + b_gat
            scores = _layernorm(agg, ln_gamma, ln_beta).reshape(M, HEADS, NUM_EXPERTS).mean(1)
            scores = scores.reshape(Bc, Nc, NUM_EXPERTS)
            topk_s, topk_i = jax.lax.top_k(scores, TOP_K)
            w = jax.nn.softmax(topk_s, axis=-1)
            out = jnp.zeros_like(x)
            for ei in range(NUM_EXPERTS):
                g = jnp.where(topk_i == ei, w, 0.0).sum(-1)
                hh = jax.nn.gelu(x @ W1[ei] + b1[ei], approximate=False)
                out = out + g[..., None] * (hh @ W2[ei] + b2[ei])
            return out
        key = jax.random.key(seed)
        ks = jax.random.split(key, 8)
        s = 0.05
        return {'x': jax.random.normal(ks[0], (B, N, D), jnp.float32), 'W_gat': jax.random.normal(ks[1], (D, HEADS * NUM_EXPERTS), jnp.float32) * s, 'att_src': jax.random.normal(ks[2], (HEADS, NUM_EXPERTS), jnp.float32) * s, 'att_dst': jax.random.normal(ks[3], (HEADS, NUM_EXPERTS), jnp.float32) * s, 'b_gat': jnp.zeros((HEADS * NUM_EXPERTS,), jnp.float32), 'ln_gamma': jnp.ones((HEADS * NUM_EXPERTS,), jnp.float32), 'ln_beta': jnp.zeros((HEADS * NUM_EXPERTS,), jnp.float32), 'W1': jax.random.normal(ks[4], (NUM_EXPERTS, D, 2 * D), jnp.float32) * s, 'b1': jnp.zeros((NUM_EXPERTS, 2 * D), jnp.float32), 'W2': jax.random.normal(ks[5], (NUM_EXPERTS, 2 * D, D), jnp.float32) * s, 'b2': jnp.zeros((NUM_EXPERTS, D), jnp.float32), 'edge_index': jax.random.randint(ks[6], (2, N_EDGES), 0, B * N, jnp.int32)}
    _L0_ffn_all = _L0_ffn_setup()
    _L0_ffn_in = {k: v for k, v in _L0_ffn_all.items() if k in ('W_gat', 'att_src', 'att_dst', 'b_gat', 'ln_gamma', 'ln_beta', 'W1', 'b1', 'W2', 'b2', 'edge_index')}
    del _L0_ffn_all
    return {'x': x, 'L0_conv_w_qkv': _L0_conv_in['w_qkv'], 'L0_conv_b_qkv': _L0_conv_in['b_qkv'], 'L0_conv_w_o': _L0_conv_in['w_o'], 'L0_conv_b_o': _L0_conv_in['b_o'], 'L0_ffn_W_gat': _L0_ffn_in['W_gat'], 'L0_ffn_att_src': _L0_ffn_in['att_src'], 'L0_ffn_att_dst': _L0_ffn_in['att_dst'], 'L0_ffn_b_gat': _L0_ffn_in['b_gat'], 'L0_ffn_ln_gamma': _L0_ffn_in['ln_gamma'], 'L0_ffn_ln_beta': _L0_ffn_in['ln_beta'], 'L0_ffn_W1': _L0_ffn_in['W1'], 'L0_ffn_b1': _L0_ffn_in['b1'], 'L0_ffn_W2': _L0_ffn_in['W2'], 'L0_ffn_b2': _L0_ffn_in['b2'], 'L0_ffn_edge_index': _L0_ffn_in['edge_index']}

def reference(x, L0_conv_w_qkv, L0_conv_b_qkv, L0_conv_w_o, L0_conv_b_o, L0_ffn_W_gat, L0_ffn_att_src, L0_ffn_att_dst, L0_ffn_b_gat, L0_ffn_ln_gamma, L0_ffn_ln_beta, L0_ffn_W1, L0_ffn_b1, L0_ffn_W2, L0_ffn_b2, L0_ffn_edge_index):
    import jax
    import jax.numpy as jnp

    def _L0_conv_ref(x, w_qkv, b_qkv, w_o, b_o):
        import jax, jax.numpy as jnp
        import numpy as np
        M, H, W, D = (32, 32, 32, 128)
        WH, WW = (8, 8)
        SH, SW = (4, 4)
        NH = 8
        NEG = -1000000000.0
        NW = H // WH * (W // WW)
        WS = WH * WW

        def _window_partition(x):
            m, d = (x.shape[0], x.shape[-1])
            x = x.reshape(m, H // WH, WH, W // WW, WW, d)
            x = x.transpose(0, 1, 3, 2, 4, 5)
            return x.reshape(m * NW, WS, d)

        def _window_reverse(x):
            d = x.shape[-1]
            m = x.shape[0] // NW
            x = x.reshape(m, H // WH, W // WW, WH, WW, d)
            x = x.transpose(0, 1, 3, 2, 4, 5)
            return x.reshape(m, H, W, d)

        def _shift_mask():
            img = np.zeros((H, W), np.int32)
            cnt = 0
            for hs in (slice(0, -WH), slice(-WH, -SH), slice(-SH, None)):
                for ws_ in (slice(0, -WW), slice(-WW, -SW), slice(-SW, None)):
                    img[hs, ws_] = cnt
                    cnt += 1
            mw = img.reshape(H // WH, WH, W // WW, WW).transpose(0, 2, 1, 3).reshape(NW, WS)
            diff = mw[:, None, :] - mw[:, :, None]
            return jnp.asarray(np.where(diff != 0, NEG, 0.0).astype(np.float32))

        def _mhsa(x, w_qkv, b_qkv, w_o, b_o, mask):
            B, S, _ = x.shape
            hd = D // NH
            qkv = x @ w_qkv + b_qkv
            q, k, v = jnp.split(qkv, 3, axis=-1)
            q = q.reshape(B, S, NH, hd)
            k = k.reshape(B, S, NH, hd)
            v = v.reshape(B, S, NH, hd)
            scores = jnp.einsum('bqhd,bkhd->bhqk', q, k) / jnp.sqrt(jnp.float32(hd))
            if mask is not None:
                scores = scores + mask[:, None, :, :]
            attn = jax.nn.softmax(scores, axis=-1)
            out = jnp.einsum('bhqk,bkhd->bqhd', attn, v).reshape(B, S, D)
            return out @ w_o + b_o
        m = x.shape[0]
        y = _mhsa(_window_partition(x), w_qkv, b_qkv, w_o, b_o, None)
        y = _window_reverse(y)
        ys = jnp.roll(y, shift=(-SH, -SW), axis=(1, 2))
        mask = jnp.broadcast_to(_shift_mask()[None], (m, NW, WS, WS)).reshape(m * NW, WS, WS)
        ys = _mhsa(_window_partition(ys), w_qkv, b_qkv, w_o, b_o, mask)
        ys = _window_reverse(ys)
        return jnp.roll(ys, shift=(SH, SW), axis=(1, 2))

    def _L0_ffn_ref(x, W_gat, att_src, att_dst, b_gat, ln_gamma, ln_beta, W1, b1, W2, b2, edge_index):
        import jax, jax.numpy as jnp
        import numpy as np
        B, N, D = (16, 2048, 128)
        NUM_EXPERTS, TOP_K, HEADS = (4, 2, 4)
        N_EDGES = 524288
        LN_EPS = 1e-05

        def _layernorm(x, g, b):
            mu = x.mean(-1, keepdims=True)
            var = ((x - mu) ** 2).mean(-1, keepdims=True)
            return (x - mu) * jax.lax.rsqrt(var + LN_EPS) * g + b

        def _forward(x, edge_index, W_gat, att_src, att_dst, b_gat, ln_gamma, ln_beta, W1, b1, W2, b2):
            Bc, Nc, Dc = x.shape
            M = Bc * Nc
            x_flat = x.reshape(M, Dc)
            h = (x_flat @ W_gat).reshape(M, HEADS, NUM_EXPERTS)
            loops = jnp.arange(M, dtype=edge_index.dtype)
            src = jnp.concatenate([edge_index[0], loops])
            dst = jnp.concatenate([edge_index[1], loops])
            a_src = (h * att_src).sum(-1)
            a_dst = (h * att_dst).sum(-1)
            e = jax.nn.leaky_relu(a_src[src] + a_dst[dst], negative_slope=0.2)
            e_max = jax.ops.segment_max(e, dst, num_segments=M)
            ee = jnp.exp(e - e_max[dst])
            denom = jax.ops.segment_sum(ee, dst, num_segments=M)
            alpha = ee / (denom[dst] + 1e-16)
            msg = h[src] * alpha[:, :, None]
            agg = jax.ops.segment_sum(msg, dst, num_segments=M).reshape(M, HEADS * NUM_EXPERTS) + b_gat
            scores = _layernorm(agg, ln_gamma, ln_beta).reshape(M, HEADS, NUM_EXPERTS).mean(1)
            scores = scores.reshape(Bc, Nc, NUM_EXPERTS)
            topk_s, topk_i = jax.lax.top_k(scores, TOP_K)
            w = jax.nn.softmax(topk_s, axis=-1)
            out = jnp.zeros_like(x)
            for ei in range(NUM_EXPERTS):
                g = jnp.where(topk_i == ei, w, 0.0).sum(-1)
                hh = jax.nn.gelu(x @ W1[ei] + b1[ei], approximate=False)
                out = out + g[..., None] * (hh @ W2[ei] + b2[ei])
            return out
        return _forward(x, edge_index, W_gat, att_src, att_dst, b_gat, ln_gamma, ln_beta, W1, b1, W2, b2)

    def _gn(v, G=32, eps=1e-05):
        B_, H_, W_, C_ = v.shape
        g = v.reshape(B_, H_, W_, G, C_ // G)
        m = jnp.mean(g, axis=(1, 2, 4), keepdims=True)
        s = jnp.var(g, axis=(1, 2, 4), keepdims=True)
        return ((g - m) / jnp.sqrt(s + eps)).reshape(v.shape)

    def _ln_c(v, eps=1e-06):
        m = jnp.mean(v, axis=-1, keepdims=True)
        s = jnp.var(v, axis=-1, keepdims=True)
        return (v - m) / jnp.sqrt(s + eps)

    def _ln_t(v, eps=1e-05):
        m = jnp.mean(v, axis=-1, keepdims=True)
        s = jnp.var(v, axis=-1, keepdims=True)
        return (v - m) / jnp.sqrt(s + eps)

    def _to_tokens(v):
        B_, H_, W_, C_ = v.shape
        return v.reshape(B_, H_ * W_, C_)

    def _from_tokens(t, like):
        return t.reshape(like.shape)
    x = x + _L0_conv_ref(_ln_c(x), L0_conv_w_qkv, L0_conv_b_qkv, L0_conv_w_o, L0_conv_b_o)
    t = _to_tokens(x)
    t = t + _L0_ffn_ref(_ln_t(t), L0_ffn_W_gat, L0_ffn_att_src, L0_ffn_att_dst, L0_ffn_b_gat, L0_ffn_ln_gamma, L0_ffn_ln_beta, L0_ffn_W1, L0_ffn_b1, L0_ffn_W2, L0_ffn_b2, L0_ffn_edge_index)
    x = _from_tokens(t, x)
    return x

_drawn_inputs = setup_inputs


def setup_inputs(seed=0):
    import zlib

    import numpy as np

    out = dict(_drawn_inputs(seed))
    spreads = {'L0_conv_b_qkv': (0.0, 0.1),
     'L0_conv_b_o': (0.0, 0.1),
     'L0_ffn_b_gat': (0.0, 0.1),
     'L0_ffn_ln_gamma': (1.0, 0.2),
     'L0_ffn_ln_beta': (0.0, 0.1),
     'L0_ffn_b1': (0.0, 0.1),
     'L0_ffn_b2': (0.0, 0.1)}
    factors = {'L0_conv_w_qkv': 2.95, 'L0_ffn_att_dst': 3.839}
    for name, (base, spread) in spreads.items():
        noise = np.random.default_rng([zlib.crc32(name.encode()), seed]).standard_normal(out[name].shape)
        drawn = base * np.exp(spread * noise) if base else spread * noise
        out[name] = jnp.asarray(drawn.astype(out[name].dtype))
    for name, factor in factors.items():
        out[name] = (out[name] * factor).astype(out[name].dtype)
    return out
```

```python
from contextlib import ExitStack
import concourse.bass as bass
from concourse import mybir

F32 = mybir.dt.float32
I32 = mybir.dt.int32
BF16 = mybir.dt.bfloat16
ALU = mybir.AluOpType
ACT = mybir.ActivationFunctionType
AX_X = mybir.AxisListType.X

P = 128
BANK = 512
NODES = 32768
EDGES = 524288
NODE_BITS = 15
SORTED = EDGES + NODES
ROWS = SORTED // P
KEY_BASE = (1 << 23) >> NODE_BITS


def pair_views(tile, bit, direction=None):
    n = tile.shape[1].bit_length() - 1
    if direction is None:
        v = tile.rearrange("p (o b i) -> p o b i", b=2, i=1 << bit)
        return [(v[:, :, 0, :], v[:, :, 1, :])]
    hi, lo = max(bit, direction), min(bit, direction)
    v = tile.rearrange("p (o h m l i) -> p o h m l i", h=2, m=1 << (hi - lo - 1), l=2, i=1 << lo)
    out = []
    for d in range(2):
        if bit > direction:
            out.append((v[:, :, 0, :, d, :], v[:, :, 1, :, d, :]))
        else:
            out.append((v[:, :, d, :, 0, :], v[:, :, d, :, 1, :]))
    return out


def sort_edges(nc, edge_index, sorted_keys):
    COLS = EDGES // P
    CB = COLS.bit_length() - 1
    LB = 7
    BLOCKS = COLS // P
    LEVELS = EDGES.bit_length() - 1
    UCOLS = NODES // P

    with ExitStack() as ctx:
        def sb(name, shape, dt):
            return ctx.enter_context(nc.sbuf_tensor("sort_" + name, shape, dt))

        def sem(name):
            return ctx.enter_context(nc.semaphore("sort_" + name))

        keys = [sb(f"keys{i}", [P, COLS], F32) for i in range(2)]
        loops = sb("loops", [P, COLS], F32)
        upper = [sb(f"upper{i}", [P, UCOLS], F32) for i in range(2)]
        umax = sb("umax", [P, COLS], F32)
        ident = sb("ident", [P, P], F32)
        sign = sb("sign", [P, CB], F32)
        signi = sb("signi", [P, CB], I32)
        zero = sb("zero", [P, 1], F32)
        mark = sb("mark", [P, 1], F32)
        banks = [ctx.enter_context(nc.psum_tensor(f"sort_bank{i}", [P, BANK], F32)) for i in range(8)]

        s_dst = sem("s_dst")
        s_src = sem("s_src")
        s_const = sem("s_const")
        s_stage = sem("s_stage")
        s_turn = sem("s_turn")
        s_evac_a = sem("s_evac_a")
        s_evac_v = sem("s_evac_v")
        s_upout = sem("s_upout")
        s_upin = sem("s_upin")
        s_out = sem("s_out")
        s_out2 = sem("s_out2")
        s_out3 = sem("s_out3")

        plan = []
        stages = []

        step = [3]
        cur = [0]

        def compare(tiles, which, bit, direction):
            stages.append(("cmp", tiles, which, bit, direction))
            step[0] += 1
            return 1 - which

        def turn(tiles, which, blocks, col):
            plan.append((step[0], tiles[which], tiles[1 - which], blocks, col))
            stages.append(("turn", len(plan) - 1))
            step[0] += 1
            return 1 - which

        def scale(tiles, which, col):
            stages.append(("sign", tiles, which, col))
            step[0] += 1
            return 1 - which

        w = 1
        for level in range(1, CB + 1):
            if level == CB:
                w = scale(keys, w, 0)
            for j in range(level - 1, -1, -1):
                w = compare(keys, w, j, level if level < CB else None)
            if level == CB:
                w = scale(keys, w, 0)

        def column_bit(j):
            return j - CB if j >= CB else j - LB + LB
        for level in range(CB + 1, LEVELS + 1):
            w = turn(keys, w, BLOCKS, None)
            for j in range(level - 1, LB - 1, -1):
                w = compare(keys, w, column_bit(j), level - CB if level < LEVELS else None)
            w = turn(keys, w, BLOCKS, level - CB if level < LEVELS else None)
            for j in range(LB - 1, -1, -1):
                w = compare(keys, w, j, None)
            if level < LEVELS:
                w = scale(keys, w, level - CB)
        stages.append(("join", w))
        step[0] += 2
        join_step = step[0]
        w = 1 - w
        w = turn(keys, w, BLOCKS, None)
        for j in range(LEVELS - 1, LB - 1, -1):
            w = compare(keys, w, column_bit(j), None)
        w = turn(keys, w, BLOCKS, None)
        for j in range(LB - 1, -1, -1):
            w = compare(keys, w, j, None)
        final = w
        final_step = step[0]
        UL = UCOLS.bit_length() - 1
        stages.append(("upin",))
        u = turn(upper, 0, UCOLS // P, None)
        for j in range(NODE_BITS - 1, LB - 1, -1):
            u = compare(upper, u, j - UL if j >= UL else j, None)
        u = turn(upper, u, UCOLS // P, None)
        for j in range(LB - 1, -1, -1):
            u = compare(upper, u, j, None)
        ufinal = u
        last_step = step[0]

        def bank_count(blocks):
            return max(1, blocks // 4)
        before = []
        total = 0
        for (_, _, _, blocks, _) in plan:
            before.append(total)
            total += bank_count(blocks)

        def turned(n, b):
            return before[n] + b + 1

        def emptied_a(n):
            return sum((bank_count(pl[3]) + 1) // 2 for pl in plan[:n])

        def emptied_v(n):
            return sum(bank_count(pl[3]) // 2 for pl in plan[:n])

        block = ctx.enter_context(nc.Block())

        @block.sync
        def _(sp):
            sp.dma_start(keys[0][:, :].bitcast(I32), edge_index[1, :].rearrange("(p c) -> p c", p=P)).then_inc(s_dst, 16)
            sp.dma_start(keys[1][:, :].bitcast(I32), edge_index[0, :].rearrange("(p c) -> p c", p=P)).then_inc(s_src, 16)
            sp.wait_ge(s_const, 4)
            sp.dma_start(sorted_keys[0:1, :], zero[0:1, :]).then_inc(s_out3, 16)
            sp.wait_ge(s_stage, join_step)
            first = P - NODES // COLS
            sp.dma_start(sorted_keys[1 + EDGES:1 + SORTED, :].rearrange("(p c) o -> p (c o)", c=COLS),
                         umax[first:P, :]).then_inc(s_upout, 16)
            sp.wait_ge(s_upout, 16)
            sp.dma_start(upper[0][:, :], sorted_keys[1 + EDGES:1 + SORTED, :].rearrange("(p c) o -> p (c o)", c=UCOLS)
                         ).then_inc(s_upin, 16)
            sp.wait_ge(s_stage, final_step)
            sp.dma_start(sorted_keys[1:1 + EDGES, :].rearrange("(p c) o -> p (c o)", c=COLS),
                         keys[final][:, :]).then_inc(s_out, 16)
            sp.wait_ge(s_stage, last_step)
            sp.dma_start(sorted_keys[1 + EDGES:1 + SORTED, :].rearrange("(p c) o -> p (c o)", c=UCOLS),
                         upper[ufinal][:, :]).then_inc(s_out2, 16)
            sp.wait_ge(s_out, 16)
            sp.wait_ge(s_out2, 16)
            sp.wait_ge(s_out3, 16)

        @block.gpsimd
        def _(pool):
            pool.memset(ident[:, :], 0.0).then_inc(s_const, 1)
            pool.memset(zero[:, :], 0.0).then_inc(s_const, 1)
            pool.wait_ge(s_const, 2)
            pool.affine_select(out=ident[:, :], in_=ident[:, :], compare_op=ALU.not_equal, fill=1.0,
                               base=0, pattern=[[-1, P]], channel_multiplier=1).then_inc(s_const, 1)
            pool.iota(signi[:, :], pattern=[[0, CB]], base=0, channel_multiplier=1).then_inc(s_const, 1)
            lo = P - 32
            pool.wait_ge(s_const, 4)
            pool.iota(loops[lo:P, :].bitcast(I32), pattern=[[-1, COLS]], base=EDGES - 1 - lo * COLS,
                      channel_multiplier=-COLS).then_inc(s_const, 1)

        @block.scalar
        def _(act):
            used = 0
            for n, (need, src, dst, blocks, col) in enumerate(plan):
                for b in range(0, bank_count(blocks), 2):
                    width = min(BANK, blocks * P)
                    act.wait_ge(s_turn, turned(n, b))
                    out = dst[:, b * BANK:b * BANK + width]
                    if col is None:
                        act.activation(out, banks[b][:, 0:width], ACT.Copy).then_inc(s_evac_a, 1)
                    else:
                        act.activation(out, banks[b][:, 0:width], ACT.Copy, scale=sign[:, col:col + 1]).then_inc(s_evac_a, 1)

        @block.tensor
        def _(pe):
            pe.wait_ge(s_const, 5)
            for n, (need, src, dst, blocks, col) in enumerate(plan):
                if src is upper[0] and n == len(plan) - 2:
                    pe.wait_ge(s_upin, 16)
                pe.wait_ge(s_stage, need)
                pe.wait_ge(s_evac_a, emptied_a(n)) if n else None
                pe.wait_ge(s_evac_v, emptied_v(n)) if n else None
                for b in range(bank_count(blocks)):
                    for k in range(min(4, blocks)):
                        c = (4 * b + k) * P
                        last = pe.transpose(banks[b][:, k * P:(k + 1) * P], src[:, c:c + P], ident[:, :])
                    last.then_inc(s_turn, 1)

        @block.vector
        def _(dve):
            done = [0]

            def step_done(ins):
                ins.then_inc(s_stage, 1)
                done[0] += 1
                dve.wait_ge(s_stage, done[0])

            dve.wait_ge(s_const, 5)
            for c in range(CB):
                last = dve.tensor_scalar(signi[:, c:c + 1], signi[:, c:c + 1], c, 1, ALU.logical_shift_right, ALU.bitwise_and)
            dve.wait_ge(s_dst, 16)
            dve.wait_ge(s_src, 16)
            step_done(dve.tensor_tensor(keys[1][:, :].bitcast(I32), keys[0][:, :].bitcast(I32), keys[1][:, :].bitcast(I32),
                                        ALU.bitwise_xor))
            dve.tensor_scalar(sign[:, :], signi[:, :], -2.0, 1.0, ALU.mult, ALU.add)
            dve.tensor_scalar(loops[P - 32:P, :].bitcast(I32), loops[P - 32:P, :].bitcast(I32), float(NODES), float(KEY_BASE),
                              ALU.min, ALU.add)
            step_done(dve.tensor_scalar(keys[0][:, :].bitcast(I32), keys[0][:, :].bitcast(I32), float(KEY_BASE), None, ALU.add))
            dve.tensor_scalar(loops[P - 32:P, :].bitcast(I32), loops[P - 32:P, :].bitcast(I32), NODE_BITS, None,
                              ALU.logical_shift_left)
            step_done(dve.scalar_tensor_tensor(out=keys[1][:, :].bitcast(I32), in0=keys[0][:, :].bitcast(I32),
                                               scalar=NODE_BITS, in1=keys[1][:, :].bitcast(I32),
                                               op0=ALU.logical_shift_left, op1=ALU.bitwise_or))
            nturn = 0
            for st in stages:
                if st[0] == "cmp":
                    _, tiles, which, bit, direction = st
                    src, dst = tiles[which][:, :], tiles[1 - which][:, :]
                    ops = (ALU.min, ALU.max)
                    for d, ((a, b), (x, y)) in enumerate(zip(pair_views(src, bit, direction), pair_views(dst, bit, direction))):
                        dve.tensor_tensor(x, a, b, ops[d])
                        last = dve.tensor_tensor(y, a, b, ops[1 - d])
                    step_done(last)
                elif st[0] == "sign":
                    _, tiles, which, col = st
                    step_done(dve.tensor_scalar(tiles[1 - which][:, :], tiles[which][:, :], sign[:, col:col + 1], None, ALU.mult))
                elif st[0] == "turn":
                    n = st[1]
                    _, src, dst, blocks, col = plan[n]
                    for b in range(1, bank_count(blocks), 2):
                        dve.wait_ge(s_turn, turned(n, b))
                        out = dst[:, b * BANK:(b + 1) * BANK]
                        if col is None:
                            last = dve.tensor_copy(out, banks[b][:, :])
                        else:
                            last = dve.tensor_scalar(out, banks[b][:, :], sign[:, col:col + 1], None, ALU.mult)
                        last.then_inc(s_evac_v, 1)
                    dve.wait_ge(s_evac_a, emptied_a(n + 1))
                    if emptied_v(n + 1):
                        dve.wait_ge(s_evac_v, emptied_v(n + 1))
                    step_done(dve.memset(mark[:, :], 0.0))
                elif st[0] == "join":
                    src, dst = keys[st[1]], keys[1 - st[1]]
                    dve.tensor_copy(dst[0:P - 32, :], src[0:P - 32, :])
                    step_done(dve.tensor_tensor(dst[P - 32:P, :], src[P - 32:P, :], loops[P - 32:P, :], ALU.min))
                    step_done(dve.tensor_tensor(umax[P - 32:P, :], src[P - 32:P, :], loops[P - 32:P, :], ALU.max))
                elif st[0] == "upin":
                    dve.wait_ge(s_upin, 16)
            assert done[0] == last_step, (done[0], last_step)


IMAGES = 32
SIDE = 32
TOKENS = SIDE * SIDE
TILES = TOKENS // P
WIN = 8
WTOK = WIN * WIN
WGRID = SIDE // WIN
SHIFT = 4
PAD = SIDE + SHIFT
HEADS = 8
HDIM = P // HEADS
PAIRS = WGRID * WGRID // 2
GROUPS = HEADS // 2
VW = 2 * (HDIM + 1)
GHEADS = 4
GDIM = 16
NROW = GDIM + 2 * GHEADS
NEG = -1.0e9
SCALE = HDIM ** -0.5
EPS_LN = 1e-6
EPS_TOKEN = 1e-5


class Chain:

    def __init__(self, sem):
        self.sem, self.per, self.k = sem, None, 0

    def start(self, m):
        self.m, self.k = m, 0

    def value(self):
        return self.k if self.per is None else self.m * self.per + self.k

    def link(self, eng, ins):
        ins.then_inc(self.sem, 1)
        self.k += 1
        eng.wait_ge(self.sem, self.value())

    def end(self):
        if self.per is None:
            self.per = self.k
        assert self.per == self.k


def attention(nc, x, w_qkv, b_qkv, w_o, b_o, w_gat, att_src, att_dst, x2_out, tnT_out, node_rows):
    with ExitStack() as ctx:
        def sb(name, shape, dt=F32):
            return ctx.enter_context(nc.sbuf_tensor("attn_" + name, shape, dt))

        def ps(name):
            return ctx.enter_context(nc.psum_tensor("attn_" + name, [P, BANK], F32))

        def sem(name):
            return ctx.enter_context(nc.semaphore("attn_" + name))

        wqkv = sb("wqkv", [P, 3 * P])
        wo = sb("wo", [P, P])
        wgat = sb("wgat", [P, GDIM])
        bias = sb("bias", [P, 4])
        attv = sb("attv", [P, 2, GDIM])
        ident = sb("ident", [P, P])
        ones = sb("ones", [P, 1])
        hm = sb("hm", [P, HEADS])
        hmi = sb("hmi", [P, 2, HEADS], I32)
        mi = sb("mi", [P, 4, WTOK], I32)
        masks = sb("masks", [P, 3, WTOK])
        eps = sb("eps", [P, 2])
        xin = sb("xin", [P, TILES, P])
        xn = sb("xn", [P, TILES, P])
        xres = sb("xres", [P, TILES, P])
        x2 = sb("x2", [P, TILES, P])
        tn = sb("tn", [P, TILES, P])
        tnT = sb("tnT", [P, TOKENS])
        hrow = sb("hrow", [P, TILES, NROW])
        hprod = sb("hprod", [P, 2, TILES, GDIM])
        wmaj = sb("wmaj", [P, WGRID, WGRID, WTOK])
        ypad = sb("ypad", [P, PAD, PAD])
        ywin = sb("ywin", [P, WGRID, WGRID, WTOK])
        zmaj = sb("zmaj", [P, SIDE, SIDE])
        zrow = sb("zrow", [P, SIDE, SIDE])
        qT = [[sb(f"qT{s}{h}", [P, BANK]) for h in range(2)] for s in range(2)]
        kT = [[sb(f"kT{s}{h}", [P, BANK]) for h in range(2)] for s in range(2)]
        km = [[sb(f"km{s}{h}", [P, PAIRS, HEADS, WTOK]) for h in range(2)] for s in range(2)]
        vx = [sb(f"vx{s}", [P, 2 * PAIRS, GROUPS, VW]) for s in range(2)]
        S = [[sb(f"S{s}{i}", [P, HEADS, WTOK]) for i in range(2)] for s in range(2)]
        mx = [sb(f"mx{s}", [P, PAIRS, HEADS]) for s in range(2)]
        pT = [sb(f"pT{s}", [P, GROUPS, P]) for s in range(2)]
        att = [sb(f"att{h}", [P, PAIRS // 2, 2, P]) for h in range(2)]
        rsum = [sb(f"rsum{i}", [P, 2, HEADS]) for i in range(2)]
        attT = [sb(f"attT{s}", [P, BANK]) for s in range(2)]
        st6 = [sb(f"st6{i}", [P, TILES, 6]) for i in range(2)]
        mv = [sb(f"mv{i}", [P, TILES, 2]) for i in range(2)]
        nw = [sb(f"nw{i}", [P, 4, TILES]) for i in range(2)]

        score_bank = [ps("score0"), ps("score1")]
        turn_bank = [ps("turn0"), ps("turn1")]
        out_bank = [ps("out0"), ps("out1")]
        misc = [ps("misc0"), ps("misc1")]

        s_w = sem("s_w")
        s_c = sem("s_c")
        s_cv = sem("s_cv")
        s_full = [sem("s_full0"), sem("s_full1")]
        s_free = [sem("s_free0"), sem("s_free1")]
        s_xin = sem("s_xin")
        s_xres = sem("s_xres")
        s_xn = sem("s_xn")
        s_wmaj = sem("s_wmaj")
        s_q = [sem("s_qa"), sem("s_qb")]
        s_k = [sem("s_ka"), sem("s_kb")]
        s_km = [sem("s_kma"), sem("s_kmb")]
        s_v = [sem("s_va"), sem("s_vb")]
        s_sc = [sem("s_sca"), sem("s_scb")]
        s_S = [sem("s_Sa"), sem("s_Sb")]
        s_mx = [sem("s_mxa"), sem("s_mxb")]
        s_sub = [sem("s_suba"), sem("s_subb")]
        s_exp = [sem("s_expa"), sem("s_expb")]
        s_pt = [sem("s_pta"), sem("s_ptb")]
        s_pte = [sem("s_ptea"), sem("s_pteb")]
        s_pv = sem("s_pv")
        s_nrm = sem("s_nrm")
        s_oT = [sem("s_oTa"), sem("s_oTb")]
        s_y = [sem("s_y"), sem("s_z")]
        s_roll = [sem("s_yroll"), sem("s_zroll")]
        YC, ZC = 2 + WGRID, 4
        s_x2 = sem("s_x2")
        s_tn = sem("s_tn")
        s_ct = sem("s_ct")
        s_h = sem("s_h")
        s_x2st = sem("s_x2st")
        s_tst = sem("s_tst")
        s_hst = sem("s_hst")
        s_passed = [sem("s_passed_v"), sem("s_passed_p")]
        ch_f = Chain(sem("ch_f"))
        ch_c = Chain(sem("ch_c"))
        ch_m = Chain(sem("ch_m"))
        ch_n = Chain(sem("ch_n"))

        ORDER = ["Aq0", "Ak0", "Av0", "Bq0", "Bk0", "Bv0", "Aq1", "Ak1", "Av1", "Bq1", "Bk1", "Bv1", "CZ0", "CZ1",
                 "CT0", "CT1", "Ao0", "Bo0", "Ap0", "Bp0", "CH0", "FT0", "FT1", "Ao1", "Bo1", "Ap1", "Bp1"]
        LAG = {"A": 0, "B": 1, "C": 2, "F": -1}
        ITERS = IMAGES + 2

        def active(n):
            return "ABCF" if n is None else [s for s in "ABCF" if 0 <= n - LAG[s] < IMAGES]

        def bank_of(task):
            return ORDER.index(task) % 2

        def count(n, task):
            b = bank_of(task)
            before = ORDER[:ORDER.index(task) + 1]
            total = 0
            for s in "ABCF":
                per = sum(1 for t in ORDER if t[0] == s and bank_of(t) == b)
                here = sum(1 for t in before if t[0] == s and bank_of(t) == b)
                m = n - LAG[s]
                if isinstance(n, int):
                    total = total + min(max(m, 0), IMAGES) * per + (here if 0 <= m < IMAGES else 0)
                else:
                    total = total + m * per + here
            return total

        def steps(eng, body):
            body(-1, active(-1))
            body(0, active(0))
            body(1, active(1))
            body(2, active(2))
            with eng.Fori(3, IMAGES - 1) as n:
                body(n, "ABCF")
            for n in range(IMAGES - 1, ITERS):
                body(n, active(n))

        STREAM = {"A": 0, "B": 1}
        block = ctx.enter_context(nc.Block())

        @block.sync
        def _(sp):
            sp.dma_start(wqkv[:, :], w_qkv).then_inc(s_w, 16)
            sp.dma_start(wo[:, :], w_o).then_inc(s_w, 16)
            sp.dma_start(wgat[:, :], w_gat).then_inc(s_w, 16)
            sp.dma_start(bias[:, 0:3], b_qkv.rearrange("(c p) -> p c", p=P),
                         allow_slow_non_contiguous=True).then_inc(s_w, 16)
            sp.dma_start(bias[:, 3:4], b_o.rearrange("(p o) -> p o", o=1), allow_slow_non_contiguous=True).then_inc(s_w, 16)
            sp.dma_start(attv[:, 0, :], att_src.rearrange("(o h) e -> o (h e)", o=1).to_broadcast([P, GDIM])).then_inc(s_w, 16)
            sp.dma_start(attv[:, 1, :], att_dst.rearrange("(o h) e -> o (h e)", o=1).to_broadcast([P, GDIM])).then_inc(s_w, 16)

            def body(n, on):
                if "F" in on:
                    if not (isinstance(n, int) and n + 1 == 0):
                        sp.wait_ge(s_xn, n + 1)
                    sp.dma_start(xin[:, :, :], x[n + 1].rearrange("(j r) c d -> (r c) j d", j=TILES)).then_inc(s_xin, 16)
                if "C" in on:
                    if not (isinstance(n, int) and n == 2):
                        sp.wait_ge(s_x2, n - 2)
                    sp.dma_start(xres[:, :, :], x[n - 2].rearrange("(j r) c d -> (r c) j d", j=TILES)).then_inc(s_xres, 16)
                    sp.wait_ge(s_x2, n - 1)
                    sp.dma_start(x2_out[n - 2].rearrange("(j p) d -> p j d", p=P), x2[:, :, :]).then_inc(s_x2st, 16)
                    sp.wait_ge(s_ct, 2 * (n - 1))
                    sp.dma_start(tnT_out[n - 2], tnT[:, :]).then_inc(s_tst, 16)
                    sp.wait_ge(s_h, n - 1)
                    sp.dma_start(node_rows[n - 2].rearrange("(j p) d -> p j d", p=P), hrow[:, :, :]).then_inc(s_hst, 16)

            steps(sp, body)
            sp.wait_ge(s_x2st, 16 * IMAGES)
            sp.wait_ge(s_tst, 16 * IMAGES)
            sp.wait_ge(s_hst, 16 * IMAGES)

        @block.gpsimd
        def _(pool):
            pool.memset(ident[:, :], 0.0).then_inc(s_c, 1)
            pool.memset(eps[:, 0:1], EPS_LN)
            pool.memset(eps[:, 1:2], EPS_TOKEN)
            for s in range(2):
                v = vx[s][:, :, :, :].rearrange("p w g c -> p (w g c)")
                pool.memset(v, 0.0).then_inc(s_c, 1)
            pool.wait_ge(s_c, 3)
            pool.affine_select(out=ident[:, :], in_=ident[:, :], compare_op=ALU.not_equal, fill=1.0,
                               base=0, pattern=[[-1, P]], channel_multiplier=1).then_inc(s_c, 1)
            for s in range(2):
                pool.wait_ge(s_c, 4 + 2 * s)
                pool.memset(vx[s][0:WTOK, :, :, HDIM:HDIM + 1], 1.0).then_inc(s_c, 1)
                pool.wait_ge(s_c, 5 + 2 * s)
                pool.memset(vx[s][WTOK:P, :, :, VW - 1:VW], 1.0).then_inc(s_c, 1)
            pool.wait_ge(s_c, 8)
            pool.iota(hmi[:, 0, :], pattern=[[0, HEADS]], base=0, channel_multiplier=1).then_inc(s_c, 1)
            pool.wait_ge(s_c, 9)
            pool.iota(hmi[:, 1, :], pattern=[[1, HEADS]], base=0, channel_multiplier=0).then_inc(s_c, 1)
            pool.wait_ge(s_c, 10)
            pool.iota(mi[:, 0, :], pattern=[[0, WTOK]], base=0, channel_multiplier=1).then_inc(s_c, 1)
            pool.wait_ge(s_c, 11)
            pool.iota(mi[:, 1, :], pattern=[[1, WTOK]], base=0, channel_multiplier=0).then_inc(s_c, 1)

            def wrap(st, m):
                pool.wait_ge(s_y[st], 2 * m + 2)
                pool.sem_inc(s_passed[1], 1)
                if st == 0:
                    pool.tensor_copy(ypad[:, 0:SIDE, SIDE:PAD], ypad[:, 0:SIDE, 0:SHIFT]).then_inc(s_roll[0], 1)
                    pool.wait_ge(s_roll[0], YC * m + 1)
                    pool.sem_inc(s_passed[1], 1)
                    pool.tensor_copy(ypad[:, SIDE:PAD, :], ypad[:, 0:SHIFT, :]).then_inc(s_roll[0], 1)
                    pool.wait_ge(s_roll[0], YC * m + 2)
                    pool.sem_inc(s_passed[1], 1)
                    for a in range(WGRID):
                        r = a * WIN + SHIFT
                        pool.tensor_copy(ywin[:, a, :, :].rearrange("p b (h c) -> p h b c", h=WIN),
                                         ypad[:, r:r + WIN, SHIFT:PAD].rearrange("p h (b c) -> p h b c", b=WGRID)
                                         ).then_inc(s_roll[0], 1)
                else:
                    e = SIDE - SHIFT
                    for to, of in (((SHIFT, SIDE), (0, e)), ((0, SHIFT), (e, SIDE))):
                        for to2, of2 in (((SHIFT, SIDE), (0, e)), ((0, SHIFT), (e, SIDE))):
                            pool.tensor_copy(zrow[:, to[0]:to[1], to2[0]:to2[1]], zmaj[:, of[0]:of[1], of2[0]:of2[1]]
                                             ).then_inc(s_roll[1], 1)

            def body(n, on):
                for j in range(PAIRS):
                    for s in "AB":
                        if s in on:
                            st, m = STREAM[s], n - LAG[s]
                            t = S[st][j % 2]
                            pool.wait_ge(s_mx[st], m * PAIRS + j + 1)
                            pool.tensor_tensor(t[:, :, :], t[:, :, :],
                                               mx[st][:, j, :].unsqueeze(2).to_broadcast([P, HEADS, WTOK]),
                                               ALU.subtract).then_inc(s_sub[st], 1)
                for s in "AB":
                    if s in on:
                        wrap(STREAM[s], n - LAG[s])

            steps(pool, body)

        @block.scalar
        def _(act):
            act.wait_ge(s_w, 16 * 7)
            act.wait_ge(s_c, 8)

            def take(n, task, f):
                b = bank_of(task)
                act.wait_ge(s_full[b], count(n, task))
                f(misc[b]).then_inc(s_free[b], 1)

            def qk(n, s, h, which):
                st, m = STREAM[s], n - LAG[s]
                dst, col, done = ((qT, 0, s_q), (kT, 1, s_k))[which == "k"]
                b = bank_of(f"{s}{which}{h}")
                act.wait_ge(s_full[b], count(n, f"{s}{which}{h}"))
                act.activation(dst[st][h][:, :], misc[b][:, :], ACT.Identity, bias=bias[:, col:col + 1]).then_inc(s_free[b], 1)
                return b

            def vals(eng, n, s, h):
                st = STREAM[s]
                b = bank_of(f"{s}v{h}")
                eng.wait_ge(s_full[b], count(n, f"{s}v{h}"))
                if not (isinstance(n, int) and n - LAG[s] == 0):
                    eng.wait_ge(s_pv, (n - 1) * PAIRS + 4 * h + 4)
                w = slice(PAIRS * h, PAIRS * h + PAIRS)
                src = misc[b][:, :].rearrange("p (w g d) -> p w g d", w=PAIRS, g=GROUPS)
                eng.activation(vx[st][0:WTOK, w, :, 0:HDIM], src[0:WTOK], ACT.Copy)
                eng.activation(vx[st][WTOK:P, w, :, HDIM + 1:VW - 1], src[WTOK:P], ACT.Copy).then_inc(s_free[b], 1)

            def qkv(n, s, h):
                qk(n, s, h, "q")
                qk(n, s, h, "k")
                if s == "A":
                    vals(act, n, s, h)

            def outT(n, s, h):
                st = STREAM[s]
                take(n, f"{s}o{h}", lambda t: act.activation(attT[st][:, :], t[:, :], ACT.Identity, bias=bias[:, 2:3]))

            def project(n, s, h):
                st, b = STREAM[s], bank_of(f"{s}p{h}")
                t = (ypad, zmaj)[st]
                act.wait_ge(s_full[b], count(n, f"{s}p{h}"))
                for i in range(2):
                    r = (2 * h + i) * WIN
                    src = misc[b][:, i * 256:(i + 1) * 256].rearrange("p (b h c) -> p h b c", b=WGRID, h=WIN)
                    out = t[:, r:r + WIN, 0:SIDE].rearrange("p h (b c) -> p h b c", b=WGRID)
                    last = act.activation(out, src, ACT.Identity, bias=bias[:, 3:4])
                last.then_inc(s_free[b], 1)
                act.wait_ge(s_free[b], count(n, f"{s}p{h}"))
                act.sem_inc(s_y[st], 1)

            def body(n, on):
                AB = [s for s in "AB" if s in on]
                for s in AB:
                    qkv(n, s, 0)
                for j in range(PAIRS + 1):
                    if j < PAIRS:
                        for s in AB:
                            st, m = STREAM[s], n - LAG[s]
                            act.wait_ge(s_sc[st], m * PAIRS + j + 1)
                            if j >= 2 or not (isinstance(m, int) and m == 0):
                                act.wait_ge(s_pt[st], m * PAIRS + j - 1)
                            act.activation(S[st][j % 2][:, :, :], score_bank[st][:, :].rearrange("p (h k) -> p h k", h=HEADS),
                                           ACT.Copy).then_inc(s_S[st], 1)
                    if j >= 1:
                        for s in AB:
                            st, m = STREAM[s], n - LAG[s]
                            act.wait_ge(s_pt[st], m * PAIRS + j)
                            if j > 1 or not (isinstance(n, int) and n - LAG[s] == 0):
                                act.wait_ge(s_pv, n * PAIRS + j - 1)
                            act.activation(pT[st][:, :, :], turn_bank[st][:, :].rearrange("p (g q) -> p g q", g=GROUPS),
                                           ACT.Copy).then_inc(s_pte[st], 1)
                    if j < PAIRS:
                        for s in AB:
                            st, m = STREAM[s], n - LAG[s]
                            act.wait_ge(s_sub[st], m * PAIRS + j + 1)
                            act.activation(S[st][j % 2][:, :, :], S[st][j % 2][:, :, :], ACT.Exp, scale=SCALE).then_inc(s_exp[st], 1)
                    if j == 0 and "A" in on:
                        qkv(n, "A", 1)
                    if j == 1 and "B" in on:
                        qkv(n, "B", 1)
                    if j == 4 and "C" in on:
                        m = n - 2
                        for i in range(2):
                            if i == 0 and not (isinstance(m, int) and m == 0):
                                act.wait_ge(s_tst, 16 * m)
                            b = bank_of(f"CT{i}")
                            act.wait_ge(s_full[b], count(n, f"CT{i}"))
                            act.activation(tnT[:, i * BANK:(i + 1) * BANK], misc[b][:, :], ACT.Copy).then_inc(s_free[b], 1)
                            act.wait_ge(s_free[b], count(n, f"CT{i}"))
                            act.sem_inc(s_ct, 1)
                    if j == 5:
                        for s in AB:
                            outT(n, s, 0)
                    if j == 6:
                        for s in AB:
                            project(n, s, 0)
                if "F" in on:
                    for i in range(2):
                        b = bank_of(f"FT{i}")
                        act.wait_ge(s_full[b], count(n, f"FT{i}"))
                        for a in range(2):
                            src = misc[b][:, a * 256:(a + 1) * 256].rearrange("p (h b c) -> p h b c", h=WIN, b=WGRID)
                            out = wmaj[:, 2 * i + a, :, :].rearrange("p b (h c) -> p h b c", h=WIN)
                            last = act.activation(out, src, ACT.Copy)
                        last.then_inc(s_free[b], 1)
                for s in AB:
                    outT(n, s, 1)
                for s in AB:
                    project(n, s, 1)

            steps(act, body)

        @block.tensor
        def _(pe):
            pe.wait_ge(s_w, 16 * 7)
            pe.wait_ge(s_c, 8)

            def take(n, task):
                b = bank_of(task)
                c = count(n, task) - 1
                if not (isinstance(c, int) and c == 0):
                    pe.wait_ge(s_free[b], c)
                return misc[b], s_full[b]

            def window(s, w):
                a, b = w // WGRID, w % WGRID
                return (wmaj if s == "A" else ywin)[:, a, b, :]

            def qkv(n, s, h):
                m = n - LAG[s]
                if h == 0:
                    if s == "A":
                        for i in range(2):
                            pe.wait_ge(s_free[bank_of(f"FT{i}")], count(n - 1, f"FT{i}"))
                    else:
                        pe.wait_ge(s_roll[0], YC * m + YC)
                for which in "qk":
                    t, full = take(n, f"{s}{which}{h}")
                    wt = wqkv[:, 0:P] if which == "q" else wqkv[:, P:2 * P]
                    src = (wmaj if s == "A" else ywin)[:, 2 * h:2 * h + 2].rearrange("p a b k -> p (a b k)")
                    last = pe.matmul(t[:, :], wt, src, start=True, stop=True)
                    last.then_inc(full, 1)
                t, full = take(n, f"{s}v{h}")
                wv = wqkv[:, 2 * P:3 * P].rearrange("p (g e d) -> p e g d", g=GROUPS, e=2)
                for i in range(PAIRS):
                    for e in range(2):
                        last = pe.matmul(t[e * WTOK:(e + 1) * WTOK, i * WTOK:(i + 1) * WTOK], window(s, PAIRS * h + i), wv[:, e],
                                         start=True, stop=True)
                last.then_inc(full, 1)

            def scores(n, s, j):
                st, m, h = STREAM[s], n - LAG[s], j // 4
                if j % 4 == 0:
                    pe.wait_ge(s_free[bank_of(f"{s}q{h}")], count(n, f"{s}q{h}"))
                    pe.wait_ge(s_km[st], 2 * m + h + 1)
                if j > 0 or not (isinstance(m, int) and m == 0):
                    pe.wait_ge(s_S[st], m * PAIRS + j)
                for e in range(2):
                    w = (2 * j + e) % PAIRS
                    last = pe.matmul(score_bank[st][e * WTOK:(e + 1) * WTOK, :], qT[st][h][:, w * WTOK:(w + 1) * WTOK],
                                     km[st][h][:, w].rearrange("p h k -> p (h k)"), start=True, stop=True)
                last.then_inc(s_sc[st], 1)

            def turn(n, s, j):
                st, m = STREAM[s], n - LAG[s]
                pe.wait_ge(s_exp[st], m * PAIRS + j + 1)
                if j > 0 or not (isinstance(m, int) and m == 0):
                    pe.wait_ge(s_pte[st], m * PAIRS + j)
                src = S[st][j % 2][:, :, :].rearrange("p h k -> p (h k)")
                for g in range(GROUPS):
                    last = pe.transpose(turn_bank[st][:, g * P:(g + 1) * P], src[:, g * P:(g + 1) * P], ident[:, :])
                last.then_inc(s_pt[st], 1)

            def values(n, AB, j):
                if j >= 2 or not (isinstance(n, int) and n == 0):
                    pe.wait_ge(s_nrm, n * PAIRS + j - 1)
                for s in AB:
                    st, m = STREAM[s], n - LAG[s]
                    if j % 4 == 0:
                        b = bank_of(f"{s}v{j // 4}")
                        pe.wait_ge(s_free[b], count(n, f"{s}v{j // 4}"))
                    pe.wait_ge(s_pte[st], m * PAIRS + j + 1)
                    for g in range(GROUPS):
                        for e in range(2):
                            c = st * GROUPS * VW + g * VW
                            last = pe.matmul(out_bank[j % 2][e * WTOK:(e + 1) * WTOK, c:c + VW],
                                             pT[st][:, g, e * WTOK:(e + 1) * WTOK], vx[st][:, 2 * j + e, g, :],
                                             start=True, stop=True)
                last.then_inc(s_pv, 1)

            def outT(n, s, h):
                st = STREAM[s]
                t, full = take(n, f"{s}o{h}")
                pe.wait_ge(s_nrm, n * PAIRS + 4 * h + 4)
                for i in range(PAIRS // 2):
                    last = pe.transpose(t[:, i * P:(i + 1) * P], att[h][:, i, st, :], ident[:, :])
                last.then_inc(full, 1)

            def project(n, s, h):
                st = STREAM[s]
                t, full = take(n, f"{s}p{h}")
                pe.wait_ge(s_free[bank_of(f"{s}o{h}")], count(n, f"{s}o{h}"))
                pe.matmul(t[:, :], wo[:, :], attT[st][:, :], start=True, stop=True).then_inc(full, 1)

            def body(n, on):
                AB = [s for s in "AB" if s in on]
                for s in AB:
                    qkv(n, s, 0)
                for j in range(PAIRS + 1):
                    if j < PAIRS:
                        for s in AB:
                            scores(n, s, j)
                    if j >= 1:
                        for s in AB:
                            turn(n, s, j - 1)
                    if j == 0 and "A" in on:
                        qkv(n, "A", 1)
                    if j == 1 and "B" in on:
                        qkv(n, "B", 1)
                    if j == 2 and "C" in on:
                        m = n - 2
                        pe.wait_ge(s_roll[1], ZC * m + ZC)
                        for i in range(2):
                            t, full = take(n, f"CZ{i}")
                            for k in range(4):
                                r = (4 * i + k) * (P // SIDE)
                                last = pe.transpose(t[:, k * P:(k + 1) * P],
                                                    zrow[:, r:r + P // SIDE, :].rearrange("p h w -> p (h w)"), ident[:, :])
                            last.then_inc(full, 1)
                    if j == 4 and "C" in on:
                        pe.wait_ge(s_tn, n - 1)
                        for i in range(2):
                            t, full = take(n, f"CT{i}")
                            for k in range(4):
                                last = pe.transpose(t[:, k * P:(k + 1) * P], tn[:, 4 * i + k, :], ident[:, :])
                            last.then_inc(full, 1)
                    if j == 5:
                        for s in AB:
                            outT(n, s, 0)
                    if j == 6:
                        for s in AB:
                            project(n, s, 0)
                    if j == 7 and "C" in on:
                        t, full = take(n, "CH0")
                        pe.wait_ge(s_ct, 2 * (n - 1))
                        for k in range(TILES):
                            last = pe.matmul(t[:, k * GDIM:(k + 1) * GDIM], tnT[:, k * P:(k + 1) * P], wgat[:, :],
                                             start=True, stop=True)
                        last.then_inc(full, 1)
                    if j == PAIRS and "F" in on:
                        pe.wait_ge(s_xn, n + 2)
                        for i in range(2):
                            t, full = take(n, f"FT{i}")
                            for k in range(4):
                                last = pe.transpose(t[:, k * P:(k + 1) * P], xn[:, 4 * i + k, :], ident[:, :])
                            last.then_inc(full, 1)
                    if j >= 1 and AB:
                        values(n, AB, j - 1)
                for s in AB:
                    outT(n, s, 1)
                for s in AB:
                    project(n, s, 1)

            steps(pe, body)

        @block.vector
        def _(dve):
            dve.wait_ge(s_c, 12)
            cv = [0]

            def link(ins):
                ins.then_inc(s_cv, 1)
                cv[0] += 1
                dve.wait_ge(s_cv, cv[0])

            link(dve.tensor_scalar(hmi[:, 0, :], hmi[:, 0, :], 4, None, ALU.logical_shift_right))
            link(dve.tensor_tensor(hm[:, :], hmi[:, 0, :], hmi[:, 1, :], ALU.is_equal))
            link(dve.tensor_tensor(mi[:, 1, :], mi[:, 0, :], mi[:, 1, :], ALU.bitwise_xor))
            link(dve.tensor_scalar(mi[:, 2, :], mi[:, 1, :], 5, 1, ALU.logical_shift_right, ALU.bitwise_and))
            link(dve.tensor_scalar(mi[:, 3, :], mi[:, 1, :], 2, 1, ALU.logical_shift_right, ALU.bitwise_and))
            link(dve.tensor_scalar(mi[:, 0, :], mi[:, 0, :], 6, None, ALU.logical_shift_right))
            link(dve.tensor_tensor(mi[:, 3, :], mi[:, 3, :], mi[:, 0, :], ALU.mult))
            link(dve.tensor_tensor(mi[:, 0, :], mi[:, 2, :], mi[:, 3, :], ALU.max))
            big = NEG / SCALE
            link(dve.tensor_scalar(masks[:, 0, :], mi[:, 3, :], big, None, ALU.mult))
            link(dve.tensor_scalar(masks[:, 1, :], mi[:, 2, :], big, None, ALU.mult))
            link(dve.tensor_scalar(masks[:, 2, :], mi[:, 0, :], big, None, ALU.mult))

            def mask_of(j):
                row, right = j // 2 == WGRID - 1, j % 2 == 1
                return {(False, False): None, (False, True): 0, (True, False): 1, (True, True): 2}[(row, right)]

            def normalise(ch, k, src, dst, eps_col):
                for j in range(TILES):
                    last = dve.bn_stats(st6[k][:, j, :], src[:, j, :])
                ch.link(dve, last)
                dve.sem_inc(s_passed[0], 1)
                for j in range(TILES):
                    last = dve.bn_aggr(mv[k][:, j, :], st6[k][:, j, :])
                ch.link(dve, last)
                v, h, y, t = (nw[k][:, i, :] for i in range(4))
                ch.link(dve, dve.tensor_scalar(v, mv[k][:, :, 1], eps[:, eps_col:eps_col + 1], None, ALU.add))
                ch.link(dve, dve.tensor_scalar(h.bitcast(I32), v.bitcast(I32), 1, None, ALU.logical_shift_right))
                ch.link(dve, dve.tensor_scalar(y.bitcast(I32), h.bitcast(I32), -1.0, float(0x5F3759DF), ALU.mult, ALU.add))
                for _ in range(4):
                    ch.link(dve, dve.tensor_tensor(t, y, y, ALU.mult))
                    ch.link(dve, dve.scalar_tensor_tensor(out=h, in0=t, scalar=-0.5, in1=v, op0=ALU.mult, op1=ALU.mult))
                    ch.link(dve, dve.scalar_tensor_tensor(out=y, in0=h, scalar=1.5, in1=y, op0=ALU.add, op1=ALU.mult))
                for j in range(TILES):
                    last = dve.tensor_scalar(dst[:, j, :], src[:, j, :], mv[k][:, j, 0:1], y[:, j:j + 1],
                                             ALU.subtract, ALU.mult)
                return last

            def head(n):
                m = n + 1
                ch_f.start(m)
                dve.wait_ge(s_xin, 16 * m + 16)
                if not (isinstance(m, int) and m == 0):
                    for i in range(2):
                        dve.wait_ge(s_free[bank_of(f"FT{i}")], count(n - 1, f"FT{i}"))
                normalise(ch_f, 0, xin, xn, 0).then_inc(s_xn, 1)
                ch_f.end()

            def residual(n):
                m = n - 2
                dve.wait_ge(s_xres, 16 * m + 16)
                if not (isinstance(m, int) and m == 0):
                    dve.wait_ge(s_x2st, 16 * m)
                for i in range(2):
                    b = bank_of(f"CZ{i}")
                    dve.wait_ge(s_full[b], count(n, f"CZ{i}"))
                    z = misc[b][:, :].rearrange("p (j d) -> p j d", d=P)
                    dve.tensor_tensor(x2[:, 4 * i:4 * i + 4, :], z, xres[:, 4 * i:4 * i + 4, :], ALU.add).then_inc(s_free[b], 1)
                for i in range(2):
                    b = bank_of(f"CZ{i}")
                    dve.wait_ge(s_free[b], count(n, f"CZ{i}"))
                dve.sem_inc(s_x2, 1)

            def tail(n):
                m = n - 2
                ch_c.start(m)
                if not (isinstance(m, int) and m == 0):
                    dve.wait_ge(s_ct, 2 * m)
                normalise(ch_c, 1, x2, tn, 1).then_inc(s_tn, 1)

            def node_row(n):
                m = n - 2
                b = bank_of("CH0")
                dve.wait_ge(s_full[b], count(n, "CH0"))
                if not (isinstance(m, int) and m == 0):
                    dve.wait_ge(s_hst, 16 * m)
                dve.tensor_copy(hrow[:, :, 0:GDIM], misc[b][:, 0:TILES * GDIM].rearrange("p (j e) -> p j e", e=GDIM)
                                ).then_inc(s_free[b], 1)
                dve.wait_ge(s_free[b], count(n, "CH0"))
                for k in range(2):
                    last = dve.tensor_tensor(hprod[:, k], hrow[:, :, 0:GDIM],
                                             attv[:, k, :].unsqueeze(1).to_broadcast([P, TILES, GDIM]), ALU.mult)
                ch_c.link(dve, last)
                for k in range(2):
                    c = GDIM + k * GHEADS
                    last = dve.tensor_reduce(hrow[:, :, c:c + GHEADS],
                                             hprod[:, k].rearrange("p j (h e) -> p j h e", h=GHEADS), AX_X, ALU.add)
                last.then_inc(s_h, 1)
                ch_c.end()

            def masked_keys(n, s, h):
                st, m = STREAM[s], n - LAG[s]
                b = bank_of(f"{s}k{h}")
                dve.wait_ge(s_free[b], count(n, f"{s}k{h}"))
                if not (isinstance(m, int) and m == 0):
                    dve.wait_ge(s_sc[st], (m - 1) * PAIRS + 4 * h + 4)
                k = kT[st][h][:, :].rearrange("p (w k) -> p w k", w=PAIRS)
                for i in range(HEADS):
                    last = dve.tensor_scalar(km[st][h][:, :, i, :], k, hm[:, i:i + 1], None, ALU.mult)
                last.then_inc(s_km[st], 1)

            def b_values(n, h):
                b = bank_of(f"Bv{h}")
                dve.wait_ge(s_full[b], count(n, f"Bv{h}"))
                if not (isinstance(n, int) and n == 1):
                    dve.wait_ge(s_pv, (n - 1) * PAIRS + 4 * h + 4)
                w = slice(PAIRS * h, PAIRS * h + PAIRS)
                src = misc[b][:, :].rearrange("p (w g d) -> p w g d", w=PAIRS, g=GROUPS)
                dve.tensor_copy(vx[1][0:WTOK, w, :, 0:HDIM], src[0:WTOK])
                dve.tensor_copy(vx[1][WTOK:P, w, :, HDIM + 1:VW - 1], src[WTOK:P]).then_inc(s_free[b], 1)

            def body(n, on):
                AB = [s for s in "AB" if s in on]
                if AB:
                    ch_n.start(n)
                if "B" in on:
                    ch_m.start(n - 1)
                for s in AB:
                    masked_keys(n, s, 0)
                if "B" in on:
                    b_values(n, 0)
                for j in range(PAIRS + 1):
                    if j < PAIRS:
                        for s in AB:
                            st, m = STREAM[s], n - LAG[s]
                            t = S[st][j % 2][:, :, :]
                            dve.wait_ge(s_S[st], m * PAIRS + j + 1)
                            if s == "B" and mask_of(j) is not None:
                                ch_m.link(dve, dve.tensor_tensor(
                                    t, t, masks[:, mask_of(j), :].unsqueeze(1).to_broadcast([P, HEADS, WTOK]), ALU.add))
                            dve.tensor_reduce(mx[st][:, j, :], t, AX_X, ALU.max).then_inc(s_mx[st], 1)
                    if j == 0 and "A" in on:
                        masked_keys(n, "A", 1)
                    if j == 1 and "B" in on:
                        masked_keys(n, "B", 1)
                        b_values(n, 1)
                    if j == 2 and "C" in on:
                        residual(n)
                    if j == 3 and "C" in on:
                        tail(n)
                    if j == 6 and "F" in on:
                        head(n)
                    if j == 7 and "C" in on:
                        node_row(n)
                    if j >= 1 and AB:
                        i = j - 1
                        dve.wait_ge(s_pv, n * PAIRS + i + 1)
                        lo, hi = STREAM[AB[0]], STREAM[AB[-1]] + 1
                        o = out_bank[i % 2][:, 0:2 * GROUPS * VW].rearrange("p (s h d) -> p s h d", s=2, d=HDIM + 1)[:, lo:hi]
                        r = rsum[i % 2][:, lo:hi, :]
                        if i % 4 == 0 and not (isinstance(n, int) and n == 0):
                            for s in AB:
                                if not (isinstance(n, int) and n - LAG[s] == 0):
                                    c = f"{s}o{i // 4}"
                                    dve.wait_ge(s_full[bank_of(c)], count(n - 1, c))
                        ch_n.link(dve, dve.reciprocal(r, o[:, :, :, HDIM]))
                        dve.tensor_tensor(att[i // 4][:, i % 4, lo:hi, :].rearrange("p s (h d) -> p s h d", h=HEADS),
                                          o[:, :, :, 0:HDIM], r.unsqueeze(3).to_broadcast([P, hi - lo, HEADS, HDIM]),
                                          ALU.mult).then_inc(s_nrm, 1)
                if AB:
                    ch_n.end()
                if "B" in on:
                    ch_m.end()

            def dbody(n, on):
                if isinstance(n, int) and n == -1:
                    head(n)
                else:
                    body(n, on)

            steps(dve, dbody)


CHUNKS = 64
TC = ROWS // CHUNKS
HC = EDGES // P // CHUNKS
EXPERTS = 4
HIDDEN = 256
HB = HIDDEN // P
UNIT = NODES // CHUNKS
UTILES = UNIT // P
LOW = -1.0e38
HI = NODES // P
MCH, LCH, ACH = 0, GHEADS, 2 * GHEADS
RING = 8


def edges(nc, sorted_keys, node_rows, edge_index, tnT, W1, b1, W2, b2, state_rows, expert_out, last_state, first_start, hist_out):
    with ExitStack() as ctx:
        def sb(name, shape, dt=F32):
            return ctx.enter_context(nc.sbuf_tensor("edge_" + name, shape, dt))

        def ps(name):
            return ctx.enter_context(nc.psum_tensor("edge_" + name, [P, BANK], F32))

        def sem(name):
            return ctx.enter_context(nc.semaphore("edge_" + name))

        key = [sb(f"key{b}", [P, 2, TC], I32) for b in range(2)]
        dst = sb("dst", [P, 2, TC], I32)
        low = sb("low", [P, TC], I32)
        node = sb("node", [P, TC], I32)
        src = [sb(f"src{b}", [P, TC], I32) for b in range(2)]
        start = [sb(f"start{b}", [P, TC]) for b in range(2)]
        keep = [sb(f"keep{b}", [P, TC]) for b in range(2)]
        neg = [sb(f"neg{b}", [P, TC]) for b in range(2)]
        pos = sb("pos", [P, TC])
        posi = sb("posi", [P, TC], I32)
        posv = sb("posv", [P, TC])
        base = sb("base", [P, 1])
        cmin = sb("cmin", [P, 1])
        fmin = sb("fmin", [P, 1])
        G = [sb(f"G{b}", [P, TC, NROW]) for b in range(2)]
        O = [sb(f"O{b}", [P, TC + 1, NROW]) for b in range(2)]
        adm = sb("adm", [P, GHEADS, TC])
        adp = [sb(f"adp{b}", [P, GHEADS, TC]) for b in range(2)]
        ad0 = sb("ad0", [P, NROW])
        first = sb("first", [P, 1], I32)
        e = sb("e", [P, GHEADS, TC])
        w = sb("w", [P, 2, GHEADS, TC])
        msg = sb("msg", [P, GHEADS, GDIM // GHEADS, TC])
        dx = [sb(f"dx{b}", [P, HC], I32) for b in range(2)]
        dlo = sb("dlo", [P, 2, HC], I32)
        dlf = sb("dlf", [P, 2, HC])
        io = sb("io", [P, HI], I32)
        iob = sb("iob", [P, HI], BF16)
        ohl = sb("ohl", [P, RING, P], BF16)
        ohh = sb("ohh", [P, RING, HI], BF16)
        hist = sb("hist", [P, HI])
        w1 = sb("w1", [P, EXPERTS, HIDDEN])
        w2 = sb("w2", [P, EXPERTS, HB, P])
        b1c = sb("b1c", [P, EXPERTS * HB])
        b2r = sb("b2r", [P, EXPERTS * P])
        xt = [sb(f"xt{b}", [P, UNIT]) for b in range(2)]
        hid = sb("hid", [P, EXPERTS * HB, UNIT])
        yo = [sb(f"yo{b}", [P, UTILES, EXPERTS * P]) for b in range(2)]
        hbank = [ps("hbank0"), ps("hbank1")]
        ybank = [ps("ybank0"), ps("ybank1")]
        cbank = [ps("cbank0"), ps("cbank1")]

        s_w = sem("s_w")
        s_c = sem("s_c")
        s_cv = sem("s_cv")
        s_key = [sem("s_key0"), sem("s_key1")]
        s_dec = sem("s_dec")
        s_g = [[sem(f"s_g{b}{i}") for i in range(2)] for b in range(2)]
        s_ad = sem("s_ad")
        s_lo = sem("s_lo")
        s_ex = sem("s_ex")
        s_math = sem("s_math")
        s_st = [sem("s_st0"), sem("s_st1")]
        s_dx = [sem("s_dx0"), sem("s_dx1")]
        s_dxr = sem("s_dxr")
        s_oh = sem("s_oh")
        s_ohp = sem("s_ohp")
        s_hs = sem("s_hs")
        s_xt = [sem("s_xt0"), sem("s_xt1")]
        s_l1 = sem("s_l1")
        s_ge = sem("s_ge")
        s_l2 = sem("s_l2")
        s_y = sem("s_y")
        s_yst = [sem("s_yst0"), sem("s_yst1")]
        s_end = sem("s_end")
        s_passed = sem("s_passed")

        keys_prev = sorted_keys[0:SORTED, :].rearrange("(p r) o -> p (r o)", p=P)
        keys_here = sorted_keys[1:1 + SORTED, :].rearrange("(p r) o -> p (r o)", p=P)
        raw_dst = edge_index[1, :].rearrange("(p c) -> p c", p=P)
        st_rows = state_rows[0:SORTED, :].rearrange("(p r) d -> p r d", p=P)
        halves = NODES // CHUNKS
        per_img = 1024 // UNIT

        def chunks(eng, body):
            body(0, 0)
            body(1, 0)
            with eng.Fori(1, CHUNKS // 2 - 1) as i:
                for b in range(2):
                    body(b, i)
            for b in range(2):
                body(b, CHUNKS // 2 - 1)

        def first_of(b, i, n=1):
            return isinstance(i, int) and 2 * i + b < n

        def last_of(b, i, n=1):
            return isinstance(i, int) and 2 * i + b >= CHUNKS - n

        block = ctx.enter_context(nc.Block())

        @block.sync
        def _(sp):
            sp.dma_start(w1[:, :, :], W1.rearrange("e p f -> p e f")).then_inc(s_w, 16)
            sp.dma_start(w2[:, :, :, :].rearrange("p e h d -> p (e h) d"), W2.rearrange("e (h p) d -> p (e h) d", p=P)).then_inc(s_w, 16)
            sp.dma_start(b1c[:, :], b1.rearrange("e (h p) -> p (e h)", p=P), allow_slow_non_contiguous=True).then_inc(s_w, 16)
            sp.dma_start(b2r[:, :], b2.rearrange("(o e) d -> o (e d)", o=1).to_broadcast([P, EXPERTS * P])).then_inc(s_w, 16)

            def load_keys(b, c):
                sp.dma_start(key[b][:, 0, :], keys_prev[:, bass.ds(c * TC, TC)]).then_inc(s_key[b], 16)
                sp.dma_start(key[b][:, 1, :], keys_here[:, bass.ds(c * TC, TC)]).then_inc(s_key[b], 16)

            def load_raw(b, c):
                sp.dma_start(dx[b][:, :], raw_dst[:, bass.ds(c * HC, HC)]).then_inc(s_dx[b], 16)

            def load_x(b, i):
                sp.dma_start(xt[b][:, :], tnT[i][:, b * UNIT:(b + 1) * UNIT]).then_inc(s_xt[b], 16)

            load_keys(0, 0)
            load_keys(1, 1)
            load_raw(0, 0)
            load_x(0, 0)

            def body(b, i):
                c = 2 * i + b
                if not last_of(b, i, 2):
                    sp.wait_ge(s_dec, c + 1)
                    load_keys(b, c + 2)
                if not last_of(b, i):
                    if not first_of(b, i):
                        sp.wait_ge(s_w, 64)
                        sp.wait_ge(s_dxr, c)
                        sp.wait_ge(s_l1, c * EXPERTS * HB)
                    load_raw(1 - b, c + 1)
                    load_x(1 - b, i + b)
                sp.wait_ge(s_math, c + 1)
                sp.dma_start(st_rows[:, bass.ds(c * TC, TC), :], O[b][:, 1:, :]).then_inc(s_st[b], 16)
                sp.wait_ge(s_y, (c + 1) * UTILES)
                sp.dma_start(expert_out[i][b].rearrange("(t p) d -> p t d", p=P), yo[b][:, :, :]).then_inc(s_yst[b], 16)

            chunks(sp, body)
            sp.dma_start(last_state, O[1][:, TC, :]).then_inc(s_end, 16)
            sp.dma_start(first_start, fmin[:, :]).then_inc(s_end, 16)
            sp.wait_ge(s_hs, CHUNKS)
            sp.dma_start(hist_out, hist[:, :]).then_inc(s_end, 16)
            sp.wait_ge(s_end, 48)
            for b in range(2):
                sp.wait_ge(s_st[b], 16 * CHUNKS // 2)
                sp.wait_ge(s_yst[b], 16 * CHUNKS // 2)

        @block.gpsimd
        def _(pool):
            pool.iota(posi[:, :], pattern=[[1, TC]], base=0, channel_multiplier=0).then_inc(s_c, 1)
            pool.iota(io[:, :], pattern=[[1, HI]], base=0, channel_multiplier=0).then_inc(s_c, 1)
            pool.wait_ge(s_dec, 1)
            pool.indirect_dma_start(ad0[:, :], None, node_rows, bass.IndirectOffsetOnAxis(ap=first[:, :], axis=0)).then_inc(s_ad, 16)

            def body(b, i):
                c = 2 * i + b
                pool.wait_ge(s_dec, c + 1)
                if not first_of(b, i, 2):
                    pool.wait_ge(s_math, c - 1)
                pool.sem_inc(s_passed, 1)
                for t in range(TC):
                    pool.indirect_dma_start(G[b][:, t, :], None, node_rows,
                                            bass.IndirectOffsetOnAxis(ap=src[b][:, t:t + 1], axis=0)
                                            ).then_inc(s_g[b][2 * t // TC], 16)

            chunks(pool, body)

        @block.scalar
        def _(act):
            act.wait_ge(s_w, 64)

            def body(b, i):
                c = 2 * i + b
                act.wait_ge(s_lo, c + 1)
                act.activation(w[:, :, :, :], w[:, :, :, :], ACT.Exp).then_inc(s_ex, 1)
                for k in range(EXPERTS * HB):
                    act.wait_ge(s_l1, c * EXPERTS * HB + k + 1)
                    if k == 0 and not first_of(b, i):
                        act.wait_ge(s_l2, c * UTILES)
                    act.activation(hid[:, k, :], hbank[k % 2][:, :], ACT.Gelu, bias=b1c[:, k:k + 1]).then_inc(s_ge, 1)

            chunks(act, body)

        @block.tensor
        def _(pe):
            pe.wait_ge(s_w, 64)

            def body(b, i):
                c = 2 * i + b
                if not first_of(b, i, 2):
                    pe.wait_ge(s_hs, c - 1)
                for t in range(HC):
                    pe.wait_ge(s_oh, c * HC + t + 1)
                    pe.matmul(cbank[b][:, 0:HI], ohl[:, t % RING, :], ohh[:, t % RING, :],
                              start=(t == 0), stop=(t == HC - 1)).then_inc(s_ohp, 1)
                pe.wait_ge(s_xt[b], 16 * i + 16)
                for k in range(EXPERTS * HB):
                    if k >= 2 or not first_of(b, i):
                        pe.wait_ge(s_ge, c * EXPERTS * HB + k - 1)
                    pe.matmul(hbank[k % 2][:, :], w1[:, k // HB, (k % HB) * P:(k % HB + 1) * P], xt[b][:, :],
                              start=True, stop=True).then_inc(s_l1, 1)
                pe.wait_ge(s_ge, (c + 1) * EXPERTS * HB)
                for t in range(UTILES):
                    if t >= 2 or not first_of(b, i):
                        pe.wait_ge(s_y, c * UTILES + t - 1)
                    for x in range(EXPERTS):
                        for h in range(HB):
                            last = pe.matmul(ybank[t % 2][:, x * P:(x + 1) * P], hid[:, x * HB + h, t * P:(t + 1) * P],
                                             w2[:, x, h, :], start=(h == 0), stop=(h == HB - 1))
                    last.then_inc(s_l2, 1)

            chunks(pe, body)

        @block.vector
        def _(dve):
            s_step = sem("s_step")
            per = {}

            class Steps:
                k = 0

            st = Steps()

            def link(ins, at):
                ins.then_inc(s_step, 1)
                st.k += 1
                dve.wait_ge(s_step, at + st.k)

            dve.wait_ge(s_c, 2)
            dve.wait_ge(s_w, 64)
            dve.tensor_copy(pos[:, :], posi[:, :])
            dve.tensor_copy(iob[:, :], io[:, :])
            dve.memset(hist[:, :], 0.0)
            dve.memset(fmin[:, :], 0.0)
            dve.memset(base[:, :], float(-ROWS))
            dve.memset(O[1][:, TC, MCH:LCH], LOW)
            dve.memset(O[1][:, TC, LCH:], 0.0).then_inc(s_cv, 1)
            dve.wait_ge(s_cv, 1)

            def decode(b, i, at):
                c = 2 * i + b
                dve.wait_ge(s_key[b], 32 * i + 32)
                if not first_of(b, i, 2):
                    for h in range(2):
                        dve.wait_ge(s_g[b][h], 16 * (TC // 2) * i)
                st.k = 0
                link(dve.tensor_scalar(dst[:, :, :], key[b][:, :, :], NODE_BITS, None, ALU.logical_shift_right), at)
                dve.tensor_tensor(start[b][:, :], dst[:, 0, :], dst[:, 1, :], ALU.not_equal)
                dve.tensor_scalar(low[:, :], key[b][:, 1, :], NODES - 1, None, ALU.bitwise_and)
                link(dve.tensor_scalar(node[:, :], dst[:, 1, :], float(KEY_BASE), None, ALU.subtract), at)
                dve.tensor_scalar(keep[b][:, :], start[b][:, :], -1.0, 1.0, ALU.mult, ALU.add)
                dve.tensor_scalar(neg[b][:, :], start[b][:, :], LOW, None, ALU.mult)
                dve.tensor_scalar(posv[:, :], pos[:, :], base[:, :], None, ALU.add)
                if first_of(b, i):
                    dve.tensor_copy(first[:, :], node[:, 0:1])
                link(dve.tensor_tensor(src[b][:, :], low[:, :], node[:, :], ALU.bitwise_xor), at)
                link(dve.tensor_tensor(posv[:, :], posv[:, :], start[b][:, :], ALU.mult), at)
                dve.tensor_scalar(base[:, :], base[:, :], float(TC), None, ALU.add)
                link(dve.tensor_reduce(cmin[:, :], posv[:, :], AX_X, ALU.min), at)
                link(dve.tensor_tensor(fmin[:, :], fmin[:, :], cmin[:, :], ALU.min), at)
                dve.sem_inc(s_dec, 1)

            def math(b, i, at):
                c = 2 * i + b
                o, g, before = O[b], G[b], O[1 - b]
                for h in range(2):
                    dve.wait_ge(s_g[b][h], 16 * (TC // 2) * (i + 1))
                if first_of(b, i):
                    dve.wait_ge(s_ad, 16)
                if not first_of(b, i, 2):
                    dve.wait_ge(s_st[b], 16 * i)
                G2 = GDIM + GHEADS

                def by_head(t):
                    return t.rearrange("p t h -> p h t")

                bc = [P, GHEADS, TC]
                dve.tensor_copy(o[:, 0, :], before[:, TC, :])
                link(dve.tensor_tensor(adm[:, :, :], by_head(g[:, :, G2:]), start[b][:, :].unsqueeze(1).to_broadcast(bc), ALU.mult), at)
                for h in range(GHEADS):
                    init = ad0[:, G2 + h:G2 + h + 1] if first_of(b, i) else adp[1 - b][:, h, TC - 1:TC]
                    last = dve.tensor_tensor_scan(adp[b][:, h, :], keep[b][:, :], adm[:, h, :], init, ALU.mult, ALU.add)
                link(last, at)
                link(dve.tensor_tensor(e[:, :, :], by_head(g[:, :, GDIM:G2]), adp[b][:, :, :], ALU.add), at)
                link(dve.scalar_tensor_tensor(out=e[:, :, :], in0=e[:, :, :], scalar=0.2, in1=e[:, :, :], op0=ALU.mult, op1=ALU.max), at)
                for h in range(GHEADS):
                    last = dve.tensor_tensor_scan(o[:, 1:, h], neg[b][:, :], e[:, h, :], o[:, 0, h:h + 1], ALU.add, ALU.max)
                link(last, at)
                dve.tensor_tensor(w[:, 1], e[:, :, :], by_head(o[:, 1:, MCH:LCH]), ALU.subtract)
                link(dve.tensor_tensor(w[:, 0], by_head(o[:, 0:TC, MCH:LCH]), by_head(o[:, 1:, MCH:LCH]), ALU.subtract), at)
                dve.scalar_tensor_tensor(out=w[:, 0], in0=w[:, 0], scalar=0.0, in1=neg[b][:, :].unsqueeze(1).to_broadcast(bc),
                                         op0=ALU.min, op1=ALU.add).then_inc(s_lo, 1)
                dve.wait_ge(s_ex, c + 1)
                for h in range(GHEADS):
                    dve.tensor_tensor_scan(o[:, 1:, LCH + h], w[:, 0, h, :], w[:, 1, h, :], o[:, 0, LCH + h:LCH + h + 1], ALU.mult, ALU.add)
                link(dve.tensor_tensor(msg[:, :, :, :], g[:, :, 0:GDIM].rearrange("p t (h e) -> p h e t", h=GHEADS),
                                       w[:, 1].unsqueeze(2).to_broadcast([P, GHEADS, GDIM // GHEADS, TC]), ALU.mult), at)
                for h in range(GHEADS):
                    for x in range(GDIM // GHEADS):
                        k = ACH + h * (GDIM // GHEADS) + x
                        last = dve.tensor_tensor_scan(o[:, 1:, k], w[:, 0, h, :], msg[:, h, x, :], o[:, 0, k:k + 1], ALU.mult, ALU.add)
                last.then_inc(s_math, 1)
                dve.wait_ge(s_math, c + 1)

            def counts(b, i, at):
                c = 2 * i + b
                dve.wait_ge(s_dx[b], 16 * i + 16)
                dve.tensor_scalar(dlo[:, 0, :], dx[b][:, :], P - 1, None, ALU.bitwise_and)
                link(dve.tensor_scalar(dlo[:, 1, :], dx[b][:, :], 7, None, ALU.logical_shift_right), at)
                link(dve.tensor_copy(dlf[:, :, :], dlo[:, :, :]), at)
                dve.sem_inc(s_dxr, 1)
                for t in range(HC):
                    if t >= RING or not first_of(b, i):
                        dve.wait_ge(s_ohp, c * HC + t - RING + 1)
                    dve.tensor_scalar(ohl[:, t % RING, :], iob[:, 0:P], dlf[:, 0, t:t + 1], None, ALU.is_equal)
                    dve.tensor_scalar(ohh[:, t % RING, :], iob[:, :], dlf[:, 1, t:t + 1], None, ALU.is_equal).then_inc(s_oh, 1)
                dve.wait_ge(s_ohp, (c + 1) * HC)
                dve.tensor_tensor(hist[:, :], cbank[b][:, 0:HI], hist[:, :], ALU.add).then_inc(s_hs, 1)

            def outputs(b, i):
                c = 2 * i + b
                if not first_of(b, i, 2):
                    dve.wait_ge(s_yst[b], 16 * i)
                for t in range(UTILES):
                    dve.wait_ge(s_l2, c * UTILES + t + 1)
                    dve.tensor_tensor(yo[b][:, t, :], ybank[t % 2][:, :], b2r[:, :], ALU.add).then_inc(s_y, 1)

            D, M = 6, 7
            C = 2
            decode(0, 0, 0)

            def body(b, i):
                c = 2 * i + b
                at = D + c * (D + M + C)
                if not last_of(b, i):
                    decode(1 - b, i + b, at)
                    assert st.k == D
                    at = at + D
                elif True:
                    at = at + 0
                st.k = 0
                math(b, i, at)
                assert st.k == M, st.k
                st.k = 0
                counts(b, i, at + M)
                assert st.k == C
                outputs(b, i)

            chunks(dve, body)


EH = GDIM // GHEADS
VCH = NROW - LCH


def ends(nc, state_rows, last_state, first_start, hist_in, end_rows):
    with ExitStack() as ctx:
        def sb(name, shape, dt=F32):
            return ctx.enter_context(nc.sbuf_tensor("ends_" + name, shape, dt))

        def sem(name):
            return ctx.enter_context(nc.semaphore("ends_" + name))

        hist = sb("hist", [P, HI])
        tri = sb("tri", [P, P])
        ones = sb("ones", [P, P])
        ident = sb("ident", [P, P])
        rowi = sb("rowi", [P, HI], I32)
        rowf = sb("rowf", [P, HI])
        pref = sb("pref", [P, HI])
        tot = sb("tot", [P, HI])
        zero = sb("zero", [P, HI])
        endi = sb("endi", [P, HI], I32)
        ls = sb("ls", [P, NROW])
        fs = sb("fs", [P, 1])
        nost = sb("nost", [P, 1])
        x3 = sb("x3", [P, 3, VCH])
        xt = sb("xt", [VCH, 3, P])
        M = sb("M", [VCH, P + 1])
        V = sb("V", [VCH, P + 1])
        w2 = sb("w2", [VCH, 2, P])
        car = sb("car", [P, 2, VCH])
        old = sb("old", [P, NROW])
        new = sb("new", [P, NROW])
        mm = sb("mm", [P, VCH])
        mo = sb("mo", [P, VCH])
        wc = sb("wc", [P, 2, VCH])
        has = sb("has", [P, 1])
        ri = sb("ri", [P, 2], I32)
        rf = sb("rf", [P, 4])
        bp = ctx.enter_context(nc.psum_tensor("bp", [P, BANK], F32))
        bt = ctx.enter_context(nc.psum_tensor("bt", [P, BANK], F32))
        bx = ctx.enter_context(nc.psum_tensor("bx", [P, BANK], F32))
        bc = ctx.enter_context(nc.psum_tensor("bc", [P, BANK], F32))

        s_in = sem("s_in")
        s_c = sem("s_c")
        s_step = sem("s_step")
        s_pe = sem("s_pe")
        s_act = sem("s_act")
        s_z = sem("s_z")
        s_old = sem("s_old")
        s_new = sem("s_new")
        s_out = sem("s_out")
        mark = {}
        block = ctx.enter_context(nc.Block())

        @block.vector
        def _(dve):
            n = [0]

            def link(ins, name=None):
                ins.then_inc(s_step, 1)
                n[0] += 1
                dve.wait_ge(s_step, n[0])
                mark[name] = n[0]

            dve.wait_ge(s_c, 7)
            dve.wait_ge(s_in, 48)
            dve.tensor_scalar(nost[:, :], fs[:, :], 0.0, LOW, ALU.is_lt, ALU.mult)
            dve.tensor_copy(x3[:, 0, 0:GHEADS], ls[:, MCH:LCH])
            dve.tensor_copy(x3[:, 0, GHEADS:].rearrange("p (h e) -> p h e", e=EH), ls[:, MCH:LCH].unsqueeze(2).to_broadcast([P, GHEADS, EH]))
            link(dve.tensor_copy(x3[:, 1, :], ls[:, LCH:]))
            link(dve.tensor_copy(x3[:, 2, :], nost[:, :].to_broadcast([P, VCH])), "x3")
            dve.tensor_scalar(rf[:, 0:1], fs[:, :], float(ROWS - 1), None, ALU.add)
            link(dve.tensor_scalar(has[:, :], fs[:, :], float(-ROWS), None, ALU.is_gt))
            dve.tensor_copy(rf[:, 1:2], ri[:, 0:1])
            link(dve.tensor_copy(rf[:, 2:3], ri[:, 1:2]))
            link(dve.tensor_tensor(rf[:, 0:1], rf[:, 0:1], rf[:, 1:2], ALU.add))
            link(dve.tensor_tensor(rf[:, 0:1], rf[:, 0:1], rf[:, 2:3], ALU.subtract))
            link(dve.scalar_tensor_tensor(out=rf[:, 3:4], in0=rf[:, 0:1], scalar=has[:, 0:1], in1=rf[:, 2:3], op0=ALU.mult, op1=ALU.add))
            link(dve.tensor_copy(ri[:, 0:1], rf[:, 3:4]), "row")
            dve.wait_ge(s_pe, 1)
            link(dve.tensor_copy(tot[:, :], bt[:, 0:HI]))
            link(dve.tensor_tensor_scan(pref[:, :], tot[:, :], zero[:, :], 0.0, ALU.add, ALU.add))
            link(dve.tensor_tensor(pref[:, :], pref[:, :], tot[:, :], ALU.subtract))
            link(dve.tensor_tensor(pref[:, :], bp[:, 0:HI], pref[:, :], ALU.add))
            link(dve.tensor_copy(rowf[:, :], rowi[:, :]))
            link(dve.tensor_tensor(pref[:, :], pref[:, :], rowf[:, :], ALU.add))
            link(dve.tensor_copy(endi[:, :], pref[:, :]), "ends")
            dve.wait_ge(s_pe, 2)
            link(dve.tensor_copy(xt[:, :, :], bx[0:VCH, 0:3 * P].rearrange("p (a b) -> p a b", a=3)))
            dve.memset(M[:, 0:1], LOW)
            link(dve.memset(V[:, 0:1], 0.0))
            link(dve.tensor_tensor_scan(M[:, 1:], xt[:, 2, :], xt[:, 0, :], M[:, 0:1], ALU.add, ALU.max))
            dve.tensor_tensor(w2[:, 1, :], xt[:, 0, :], M[:, 1:], ALU.subtract)
            link(dve.tensor_tensor(w2[:, 0, :], M[:, 0:P], M[:, 1:], ALU.subtract))
            link(dve.scalar_tensor_tensor(out=w2[:, 0, :], in0=w2[:, 0, :], scalar=0.0, in1=xt[:, 2, :], op0=ALU.min, op1=ALU.add), "w2")
            dve.wait_ge(s_act, 1)
            link(dve.tensor_tensor(xt[:, 1, :], xt[:, 1, :], w2[:, 1, :], ALU.mult))
            link(dve.tensor_tensor_scan(V[:, 1:], w2[:, 0, :], xt[:, 1, :], V[:, 0:1], ALU.mult, ALU.add), "V")
            dve.wait_ge(s_pe, 3)
            link(dve.tensor_copy(car[:, :, :], bc[:, 0:2 * VCH].rearrange("p (a b) -> p a b", a=2)))
            dve.wait_ge(s_old, 16)
            dve.tensor_copy(mo[:, 0:GHEADS], old[:, MCH:LCH])
            link(dve.tensor_copy(mo[:, GHEADS:].rearrange("p (h e) -> p h e", e=EH), old[:, MCH:LCH].unsqueeze(2).to_broadcast([P, GHEADS, EH])))
            link(dve.tensor_tensor(mm[:, :], mo[:, :], car[:, 0, :], ALU.max))
            dve.tensor_tensor(wc[:, 0, :], car[:, 0, :], mm[:, :], ALU.subtract)
            link(dve.tensor_tensor(wc[:, 1, :], mo[:, :], mm[:, :], ALU.subtract), "wc")
            dve.wait_ge(s_act, 2)
            dve.tensor_copy(new[:, MCH:LCH], mm[:, 0:GHEADS])
            dve.tensor_tensor(mo[:, :], wc[:, 0, :], car[:, 1, :], ALU.mult)
            link(dve.tensor_tensor(new[:, LCH:], wc[:, 1, :], old[:, LCH:], ALU.mult))
            link(dve.tensor_tensor(new[:, LCH:], new[:, LCH:], mo[:, :], ALU.add), "new")

        @block.sync
        def _(sp):
            sp.dma_start(hist[:, :], hist_in).then_inc(s_in, 16)
            sp.dma_start(ls[:, :], last_state).then_inc(s_in, 16)
            sp.dma_start(fs[:, :], first_start).then_inc(s_in, 16)
            sp.wait_ge(s_c, 7)
            sp.dma_start(state_rows[SORTED:SORTED + P, :], zero[:, 0:NROW]).then_inc(s_z, 16)
            sp.wait_ge(s_step, mark["ends"])
            sp.dma_start(end_rows, endi[:, :]).then_inc(s_out, 16)
            sp.wait_ge(s_out, 16)
            sp.wait_ge(s_new, 16)

        @block.gpsimd
        def _(pool):
            pool.memset(ones[:, :], 1.0).then_inc(s_c, 1)
            pool.memset(zero[:, :], 0.0).then_inc(s_c, 1)
            pool.wait_ge(s_c, 2)
            pool.affine_select(out=tri[:, :], in_=ones[:, :], compare_op=ALU.is_ge, fill=0.0, base=0,
                               pattern=[[1, P]], channel_multiplier=-1).then_inc(s_c, 1)
            pool.affine_select(out=ident[:, :], in_=zero[:, 0:P], compare_op=ALU.not_equal, fill=1.0, base=0,
                               pattern=[[-1, P]], channel_multiplier=1).then_inc(s_c, 1)
            pool.iota(rowi[:, :], pattern=[[P, HI]], base=0, channel_multiplier=1).then_inc(s_c, 1)
            pool.iota(ri[:, 0:1], pattern=[[0, 1]], base=0, channel_multiplier=ROWS).then_inc(s_c, 1)
            pool.iota(ri[:, 1:2], pattern=[[0, 1]], base=SORTED, channel_multiplier=1).then_inc(s_c, 1)
            pool.wait_ge(s_step, mark["row"])
            pool.wait_ge(s_z, 16)
            pool.indirect_dma_start(old[:, :], None, state_rows, bass.IndirectOffsetOnAxis(ap=ri[:, 0:1], axis=0)).then_inc(s_old, 16)
            pool.wait_ge(s_step, mark["new"])
            pool.indirect_dma_start(state_rows, bass.IndirectOffsetOnAxis(ap=ri[:, 0:1], axis=0), new[:, :], None).then_inc(s_new, 16)

        @block.tensor
        def _(pe):
            pe.wait_ge(s_c, 7)
            pe.wait_ge(s_in, 48)
            pe.matmul(bp[:, 0:HI], tri[:, :], hist[:, :], start=True, stop=True)
            pe.matmul(bt[:, 0:HI], ones[:, :], hist[:, :], start=True, stop=True).then_inc(s_pe, 1)
            pe.wait_ge(s_step, mark["x3"])
            for k in range(3):
                last = pe.transpose(bx[0:VCH, k * P:(k + 1) * P], x3[:, k, :], ident[:, :])
            last.then_inc(s_pe, 1)
            pe.wait_ge(s_step, mark["V"])
            pe.transpose(bc[:, 0:VCH], M[:, 0:P], ident[0:VCH, 0:VCH])
            pe.transpose(bc[:, VCH:2 * VCH], V[:, 0:P], ident[0:VCH, 0:VCH]).then_inc(s_pe, 1)

        @block.scalar
        def _(act):
            act.wait_ge(s_step, mark["w2"])
            act.activation(w2[:, :, :], w2[:, :, :], ACT.Exp).then_inc(s_act, 1)
            act.wait_ge(s_step, mark["wc"])
            act.activation(wc[:, :, :], wc[:, :, :], ACT.Exp).then_inc(s_act, 1)


def combine(nc, state_rows, end_rows, expert_out, x2_rows, b_gat, gamma, beta, out):
    with ExitStack() as ctx:
        def sb(name, shape, dt=F32):
            return ctx.enter_context(nc.sbuf_tensor("comb_" + name, shape, dt))

        def sem(name):
            return ctx.enter_context(nc.semaphore("comb_" + name))

        par = sb("par", [P, 3, GDIM])
        endt = sb("endt", [P, HI], I32)
        ix = [sb(f"ix{b}", [P, TILES], I32) for b in range(2)]
        srow = [sb(f"srow{b}", [P, TILES, NROW]) for b in range(2)]
        ye = [sb(f"ye{b}", [P, TILES, EXPERTS * P]) for b in range(2)]
        xr = [sb(f"xr{b}", [P, TILES, P]) for b in range(2)]
        res = [sb(f"res{b}", [P, TILES, P]) for b in range(2)]
        l = sb("l", [P, TILES, GHEADS])
        agg = sb("agg", [P, TILES, GHEADS, EH])
        sq = sb("sq", [P, TILES, GDIM])
        mu = sb("mu", [P, TILES])
        var = sb("var", [P, TILES])
        nh = sb("nh", [P, TILES])
        ny = sb("ny", [P, TILES])
        nt = sb("nt", [P, TILES])
        sc = sb("sc", [P, TILES, EXPERTS])
        beat = sb("beat", [P, TILES])
        rank = sb("rank", [P, TILES, EXPERTS])
        mx = sb("mx", [P, TILES])
        gate = [sb(f"gate{b}", [P, TILES, EXPERTS]) for b in range(2)]
        s_in = sem("s_in")
        s_ix = sem("s_ix")
        s_passed = sem("s_passed")
        s_rows = [sem("s_rows0"), sem("s_rows1")]
        s_ye = [sem("s_ye0"), sem("s_ye1")]
        s_used = sem("s_used")
        s_step = sem("s_step")
        s_lo = sem("s_lo")
        s_ex = sem("s_ex")
        s_res = sem("s_res")
        s_st = [sem("s_st0"), sem("s_st1")]

        def images(eng, body):
            for b in range(2):
                body(b, 0)
            with eng.Fori(1, IMAGES // 2 - 1) as i:
                for b in range(2):
                    body(b, i)
            for b in range(2):
                body(b, IMAGES // 2 - 1)

        def first_of(b, i, n=1):
            return isinstance(i, int) and 2 * i + b < n

        block = ctx.enter_context(nc.Block())

        @block.sync
        def _(sp):
            sp.dma_start(endt[:, :], end_rows).then_inc(s_in, 16)
            for k, v in enumerate((b_gat, gamma, beta)):
                sp.dma_start(par[:, k, :], v.rearrange("(o e) -> o e", o=1).to_broadcast([P, GDIM])).then_inc(s_in, 16)

            def body(b, i):
                m = 2 * i + b
                if not first_of(b, i, 2):
                    sp.wait_ge(s_res, m - 1)
                sp.dma_start(ye[b][:, :, :], expert_out[m].rearrange("h (t p) d -> p (h t) d", p=P)).then_inc(s_ye[b], 16)
                sp.dma_start(xr[b][:, :, :], x2_rows[m].rearrange("(j p) d -> p j d", p=P)).then_inc(s_ye[b], 16)

            images(sp, body)

        @block.scalar
        def _(act):
            def body(b, i):
                m = 2 * i + b
                act.wait_ge(s_lo, m + 1)
                act.activation(gate[b][:, :, :], gate[b][:, :, :], ACT.Exp).then_inc(s_ex, 1)
                act.wait_ge(s_res, m + 1)
                act.dma_start(out[m].rearrange("(j p) d -> p j d", p=P), res[b][:, :, :]).then_inc(s_st[b], 16)

            images(act, body)
            for b in range(2):
                act.wait_ge(s_st[b], 16 * IMAGES // 2)

        @block.gpsimd
        def _(pool):
            def body(b, i):
                m = 2 * i + b
                pool.wait_ge(s_ix, m + 1)
                pool.sem_inc(s_passed, 1)
                for t in range(TILES):
                    pool.indirect_dma_start(srow[b][:, t, :], None, state_rows,
                                            bass.IndirectOffsetOnAxis(ap=ix[b][:, t:t + 1], axis=0)).then_inc(s_rows[b], 16)

            images(pool, body)

        @block.vector
        def _(dve):
            dve.wait_ge(s_in, 64)
            k = [0]
            per = [None]

            def indices(b, i):
                m = 2 * i + b
                if not first_of(b, i, 2):
                    dve.wait_ge(s_rows[b], 16 * TILES * i)
                dve.tensor_copy(ix[b][:, :], endt[:, bass.ds(m * TILES, TILES)]).then_inc(s_ix, 1)

            indices(0, 0)

            def body(b, i):
                m = 2 * i + b
                k[0] = 0

                def link(ins):
                    ins.then_inc(s_step, 1)
                    k[0] += 1
                    dve.wait_ge(s_step, (m * per[0] if per[0] else 0) + k[0])

                if not (isinstance(i, int) and m == IMAGES - 1):
                    indices(1 - b, i + b)
                dve.wait_ge(s_rows[b], 16 * TILES * (i + 1))
                s = srow[b]
                bc4 = [P, TILES, GHEADS, EH]
                flat = agg[:, :, :, :].rearrange("p t h e -> p t (h e)")

                def by_token(t, n=GDIM):
                    return t.unsqueeze(2).to_broadcast([P, TILES, n])

                def by_feature(x):
                    return par[:, x, :].unsqueeze(1).to_broadcast([P, TILES, GDIM])

                link(dve.tensor_scalar(l[:, :, :], s[:, :, LCH:ACH], 1e-16, None, ALU.add))
                link(dve.reciprocal(l[:, :, :], l[:, :, :]))
                link(dve.tensor_tensor(agg[:, :, :, :], s[:, :, ACH:].rearrange("p t (h e) -> p t h e", e=EH),
                                       l[:, :, :].unsqueeze(3).to_broadcast(bc4), ALU.mult))
                link(dve.tensor_tensor(flat, flat, by_feature(0), ALU.add))
                link(dve.tensor_reduce(mu[:, :], flat, AX_X, ALU.add))
                link(dve.tensor_scalar(mu[:, :], mu[:, :], 1.0 / GDIM, None, ALU.mult))
                link(dve.tensor_tensor(flat, flat, by_token(mu[:, :]), ALU.subtract))
                link(dve.tensor_tensor(sq[:, :, :], flat, flat, ALU.mult))
                link(dve.tensor_reduce(var[:, :], sq[:, :, :], AX_X, ALU.add))
                link(dve.tensor_scalar(var[:, :], var[:, :], 1.0 / GDIM, EPS_TOKEN, ALU.mult, ALU.add))
                link(dve.tensor_scalar(nh[:, :].bitcast(I32), var[:, :].bitcast(I32), 1, None, ALU.logical_shift_right))
                link(dve.tensor_scalar(ny[:, :].bitcast(I32), nh[:, :].bitcast(I32), -1.0, float(0x5F3759DF), ALU.mult, ALU.add))
                for _ in range(4):
                    link(dve.tensor_tensor(nt[:, :], ny[:, :], ny[:, :], ALU.mult))
                    link(dve.scalar_tensor_tensor(out=nh[:, :], in0=nt[:, :], scalar=-0.5, in1=var[:, :], op0=ALU.mult, op1=ALU.mult))
                    link(dve.scalar_tensor_tensor(out=ny[:, :], in0=nh[:, :], scalar=1.5, in1=ny[:, :], op0=ALU.add, op1=ALU.mult))
                link(dve.tensor_tensor(flat, flat, by_token(ny[:, :]), ALU.mult))
                link(dve.tensor_tensor(flat, flat, by_feature(1), ALU.mult))
                link(dve.tensor_tensor(flat, flat, by_feature(2), ALU.add))
                link(dve.tensor_reduce(sc[:, :, :], agg[:, :, :, :].rearrange("p t h e -> p t e h"), AX_X, ALU.add))
                link(dve.tensor_scalar(sc[:, :, :], sc[:, :, :], 1.0 / GHEADS, None, ALU.mult))
                dve.memset(rank[:, :, :], 0.0)
                link(dve.tensor_reduce(mx[:, :], sc[:, :, :], AX_X, ALU.max))
                for u in range(EXPERTS):
                    for v in range(u + 1, EXPERTS):
                        link(dve.tensor_tensor(beat[:, :], sc[:, :, u], sc[:, :, v], ALU.is_ge))
                        dve.tensor_tensor(rank[:, :, v], rank[:, :, v], beat[:, :], ALU.add)
                        link(dve.scalar_tensor_tensor(out=rank[:, :, u], in0=rank[:, :, u], scalar=1.0, in1=beat[:, :],
                                                      op0=ALU.add, op1=ALU.subtract))
                g = gate[b]
                link(dve.tensor_scalar(rank[:, :, :], rank[:, :, :], 2.0, None, ALU.is_lt))
                dve.tensor_tensor(g[:, :, :], sc[:, :, :], by_token(mx[:, :], EXPERTS), ALU.subtract).then_inc(s_lo, 1)
                dve.wait_ge(s_ex, m + 1)
                link(dve.tensor_tensor(g[:, :, :], g[:, :, :], rank[:, :, :], ALU.mult))
                link(dve.tensor_reduce(mx[:, :], g[:, :, :], AX_X, ALU.add))
                link(dve.reciprocal(mx[:, :], mx[:, :]))
                link(dve.tensor_tensor(g[:, :, :], g[:, :, :], by_token(mx[:, :], EXPERTS), ALU.mult))
                dve.wait_ge(s_ye[b], 32 * i + 32)
                if not first_of(b, i, 2):
                    dve.wait_ge(s_st[b], 16 * i)
                for x in range(EXPERTS):
                    for t in range(TILES):
                        before = xr[b][:, t, :] if x == 0 else res[b][:, t, :]
                        last = dve.scalar_tensor_tensor(out=res[b][:, t, :], in0=ye[b][:, t, x * P:(x + 1) * P],
                                                        scalar=g[:, t, x:x + 1], in1=before, op0=ALU.mult, op1=ALU.add)
                    if x < EXPERTS - 1:
                        link(last)
                last.then_inc(s_res, 1)
                if per[0] is None:
                    per[0] = k[0]
                assert per[0] == k[0]

            images(dve, body)


def window_attention_graph_experts(nc, x, w_qkv, b_qkv, w_o, b_o, w_gat, att_src, att_dst, b_gat,
                                   gamma, beta, w1, b1, w2, b2, edge_index, out):
    def dram(name, shape, dt=F32):
        return nc.dram_tensor(name, shape, dt, kind="Internal").ap()

    sorted_keys = dram("sorted_keys", (1 + SORTED, 1))
    x2_rows = dram("x2_rows", (IMAGES, TOKENS, P))
    tokens_t = dram("tokens_t", (IMAGES, P, TOKENS))
    node_rows = dram("node_rows", (IMAGES, TOKENS, NROW))
    state_rows = dram("state_rows", (SORTED + P, NROW))
    expert_out = dram("expert_out", (IMAGES, TOKENS // UNIT, UNIT, EXPERTS * P))
    last_state = dram("last_state", (P, NROW))
    first_start = dram("first_start", (P, 1))
    counts = dram("counts", (P, HI))
    end_rows = dram("end_rows", (P, HI), I32)

    sort_edges(nc, edge_index, sorted_keys)
    attention(nc, x, w_qkv, b_qkv, w_o, b_o, w_gat, att_src, att_dst, x2_rows, tokens_t, node_rows)
    edges(nc, sorted_keys.bitcast(I32), node_rows.rearrange("i t d -> (i t) d"), edge_index, tokens_t,
          w1, b1, w2, b2, state_rows, expert_out, last_state, first_start, counts)
    ends(nc, state_rows, last_state, first_start, counts, end_rows)
    combine(nc, state_rows, end_rows, expert_out, x2_rows, b_gat, gamma, beta, out)


INPUTS = ["x", "L0_conv_w_qkv", "L0_conv_b_qkv", "L0_conv_w_o", "L0_conv_b_o", "L0_ffn_W_gat", "L0_ffn_att_src",
          "L0_ffn_att_dst", "L0_ffn_b_gat", "L0_ffn_ln_gamma", "L0_ffn_ln_beta", "L0_ffn_W1", "L0_ffn_b1",
          "L0_ffn_W2", "L0_ffn_b2", "L0_ffn_edge_index"]


def kernel(**inputs):
    import numpy as np
    import concourse.bacc as bacc
    from concourse.bass_utils import run_bass_kernel_spmd

    nc = bacc.Bacc("TRN2", target_bir_lowering=False, num_devices=1)
    arrays, args = {}, []
    for name in INPUTS:
        a = np.ascontiguousarray(inputs[name])
        arrays["in_" + name] = a
        args.append(nc.dram_tensor("in_" + name, a.shape, mybir.dt.from_np(a.dtype), kind="ExternalInput").ap())
    out = nc.dram_tensor("out", (IMAGES, TOKENS, P), F32, kind="ExternalOutput").ap()
    window_attention_graph_experts(nc, *args, out)
    result = run_bass_kernel_spmd(nc, [arrays], core_ids=[0])
    return result.results[0]["out"].reshape(inputs["x"].shape)
```

```python
from contextlib import ExitStack
import concourse.bass as bass
from concourse import mybir

F32 = mybir.dt.float32
I32 = mybir.dt.int32
BF16 = mybir.dt.bfloat16
ALU = mybir.AluOpType
ACT = mybir.ActivationFunctionType
AX_X = mybir.AxisListType.X

P = 128
BANK = 512
NODES = 32768
EDGES = 524288
NODE_BITS = 15
SORTED = EDGES + NODES
ROWS = SORTED // P
KEY_BASE = (1 << 23) >> NODE_BITS


def pair_views(tile, bit, direction=None):
    n = tile.shape[1].bit_length() - 1
    if direction is None:
        v = tile.rearrange("p (o b i) -> p o b i", b=2, i=1 << bit)
        return [(v[:, :, 0, :], v[:, :, 1, :])]
    hi, lo = max(bit, direction), min(bit, direction)
    v = tile.rearrange("p (o h m l i) -> p o h m l i", h=2, m=1 << (hi - lo - 1), l=2, i=1 << lo)
    out = []
    for d in range(2):
        if bit > direction:
            out.append((v[:, :, 0, :, d, :], v[:, :, 1, :, d, :]))
        else:
            out.append((v[:, :, d, :, 0, :], v[:, :, d, :, 1, :]))
    return out


def sort_edges(nc, edge_index, sorted_keys):
    COLS = EDGES // P
    CB = COLS.bit_length() - 1
    LB = 7
    BLOCKS = COLS // P
    LEVELS = EDGES.bit_length() - 1
    UCOLS = NODES // P

    with ExitStack() as ctx:
        def sb(name, shape, dt):
            return ctx.enter_context(nc.sbuf_tensor("sort_" + name, shape, dt))

        def sem(name):
            return ctx.enter_context(nc.semaphore("sort_" + name))

        keys = [sb(f"keys{i}", [P, COLS], F32) for i in range(2)]
        loops = sb("loops", [P, COLS], F32)
        upper = [sb(f"upper{i}", [P, UCOLS], F32) for i in range(2)]
        umax = sb("umax", [P, COLS], F32)
        ident = sb("ident", [P, P], F32)
        sign = sb("sign", [P, CB], F32)
        signi = sb("signi", [P, CB], I32)
        zero = sb("zero", [P, 1], F32)
        mark = sb("mark", [P, 1], F32)
        banks = [ctx.enter_context(nc.psum_tensor(f"sort_bank{i}", [P, BANK], F32)) for i in range(8)]

        s_dst = sem("s_dst")
        s_src = sem("s_src")
        s_const = sem("s_const")
        s_stage = sem("s_stage")
        s_turn = sem("s_turn")
        s_evac_a = sem("s_evac_a")
        s_evac_v = sem("s_evac_v")
        s_upout = sem("s_upout")
        s_upin = sem("s_upin")
        s_out = sem("s_out")
        s_out2 = sem("s_out2")
        s_out3 = sem("s_out3")

        plan = []
        stages = []

        step = [3]
        cur = [0]

        def compare(tiles, which, bit, direction):
            stages.append(("cmp", tiles, which, bit, direction))
            step[0] += 1
            return 1 - which

        def turn(tiles, which, blocks, col):
            plan.append((step[0], tiles[which], tiles[1 - which], blocks, col))
            stages.append(("turn", len(plan) - 1))
            step[0] += 1
            return 1 - which

        def scale(tiles, which, col):
            stages.append(("sign", tiles, which, col))
            step[0] += 1
            return 1 - which

        w = 1
        for level in range(1, CB + 1):
            if level == CB:
                w = scale(keys, w, 0)
            for j in range(level - 1, -1, -1):
                w = compare(keys, w, j, level if level < CB else None)
            if level == CB:
                w = scale(keys, w, 0)

        def column_bit(j):
            return j - CB if j >= CB else j - LB + LB
        for level in range(CB + 1, LEVELS + 1):
            w = turn(keys, w, BLOCKS, None)
            for j in range(level - 1, LB - 1, -1):
                w = compare(keys, w, column_bit(j), level - CB if level < LEVELS else None)
            w = turn(keys, w, BLOCKS, level - CB if level < LEVELS else None)
            for j in range(LB - 1, -1, -1):
                w = compare(keys, w, j, None)
            if level < LEVELS:
                w = scale(keys, w, level - CB)
        stages.append(("join", w))
        step[0] += 2
        join_step = step[0]
        w = 1 - w
        w = turn(keys, w, BLOCKS, None)
        for j in range(LEVELS - 1, LB - 1, -1):
            w = compare(keys, w, column_bit(j), None)
        w = turn(keys, w, BLOCKS, None)
        for j in range(LB - 1, -1, -1):
            w = compare(keys, w, j, None)
        final = w
        final_step = step[0]
        UL = UCOLS.bit_length() - 1
        stages.append(("upin",))
        u = turn(upper, 0, UCOLS // P, None)
        for j in range(NODE_BITS - 1, LB - 1, -1):
            u = compare(upper, u, j - UL if j >= UL else j, None)
        u = turn(upper, u, UCOLS // P, None)
        for j in range(LB - 1, -1, -1):
            u = compare(upper, u, j, None)
        ufinal = u
        last_step = step[0]

        def bank_count(blocks):
            return max(1, blocks // 4)
        before = []
        total = 0
        for (_, _, _, blocks, _) in plan:
            before.append(total)
            total += bank_count(blocks)

        def turned(n, b):
            return before[n] + b + 1

        def emptied_a(n):
            return sum((bank_count(pl[3]) + 1) // 2 for pl in plan[:n])

        def emptied_v(n):
            return sum(bank_count(pl[3]) // 2 for pl in plan[:n])

        block = ctx.enter_context(nc.Block())

        @block.sync
        def _(sp):
            sp.dma_start(keys[0][:, :].bitcast(I32), edge_index[1, :].rearrange("(p c) -> p c", p=P)).then_inc(s_dst, 16)
            sp.dma_start(keys[1][:, :].bitcast(I32), edge_index[0, :].rearrange("(p c) -> p c", p=P)).then_inc(s_src, 16)
            sp.wait_ge(s_const, 4)
            sp.dma_start(sorted_keys[0:1, :], zero[0:1, :]).then_inc(s_out3, 16)
            sp.wait_ge(s_stage, join_step)
            first = P - NODES // COLS
            sp.dma_start(sorted_keys[1 + EDGES:1 + SORTED, :].rearrange("(p c) o -> p (c o)", c=COLS),
                         umax[first:P, :]).then_inc(s_upout, 16)
            sp.wait_ge(s_upout, 16)
            sp.dma_start(upper[0][:, :], sorted_keys[1 + EDGES:1 + SORTED, :].rearrange("(p c) o -> p (c o)", c=UCOLS)
                         ).then_inc(s_upin, 16)
            sp.wait_ge(s_stage, final_step)
            sp.dma_start(sorted_keys[1:1 + EDGES, :].rearrange("(p c) o -> p (c o)", c=COLS),
                         keys[final][:, :]).then_inc(s_out, 16)
            sp.wait_ge(s_stage, last_step)
            sp.dma_start(sorted_keys[1 + EDGES:1 + SORTED, :].rearrange("(p c) o -> p (c o)", c=UCOLS),
                         upper[ufinal][:, :]).then_inc(s_out2, 16)
            sp.wait_ge(s_out, 16)
            sp.wait_ge(s_out2, 16)
            sp.wait_ge(s_out3, 16)

        @block.gpsimd
        def _(pool):
            pool.memset(ident[:, :], 0.0).then_inc(s_const, 1)
            pool.memset(zero[:, :], 0.0).then_inc(s_const, 1)
            pool.wait_ge(s_const, 2)
            pool.affine_select(out=ident[:, :], in_=ident[:, :], compare_op=ALU.not_equal, fill=1.0,
                               base=0, pattern=[[-1, P]], channel_multiplier=1).then_inc(s_const, 1)
            pool.iota(signi[:, :], pattern=[[0, CB]], base=0, channel_multiplier=1).then_inc(s_const, 1)
            lo = P - 32
            pool.wait_ge(s_const, 4)
            pool.iota(loops[lo:P, :].bitcast(I32), pattern=[[-1, COLS]], base=EDGES - 1 - lo * COLS,
                      channel_multiplier=-COLS).then_inc(s_const, 1)

        @block.scalar
        def _(act):
            used = 0
            for n, (need, src, dst, blocks, col) in enumerate(plan):
                for b in range(0, bank_count(blocks), 2):
                    width = min(BANK, blocks * P)
                    act.wait_ge(s_turn, turned(n, b))
                    out = dst[:, b * BANK:b * BANK + width]
                    if col is None:
                        act.activation(out, banks[b][:, 0:width], ACT.Copy).then_inc(s_evac_a, 1)
                    else:
                        act.activation(out, banks[b][:, 0:width], ACT.Copy, scale=sign[:, col:col + 1]).then_inc(s_evac_a, 1)

        @block.tensor
        def _(pe):
            pe.wait_ge(s_const, 5)
            for n, (need, src, dst, blocks, col) in enumerate(plan):
                if src is upper[0] and n == len(plan) - 2:
                    pe.wait_ge(s_upin, 16)
                pe.wait_ge(s_stage, need)
                pe.wait_ge(s_evac_a, emptied_a(n)) if n else None
                pe.wait_ge(s_evac_v, emptied_v(n)) if n else None
                for b in range(bank_count(blocks)):
                    for k in range(min(4, blocks)):
                        c = (4 * b + k) * P
                        last = pe.transpose(banks[b][:, k * P:(k + 1) * P], src[:, c:c + P], ident[:, :])
                    last.then_inc(s_turn, 1)

        @block.vector
        def _(dve):
            done = [0]

            def step_done(ins):
                ins.then_inc(s_stage, 1)
                done[0] += 1
                dve.wait_ge(s_stage, done[0])

            dve.wait_ge(s_const, 5)
            for c in range(CB):
                last = dve.tensor_scalar(signi[:, c:c + 1], signi[:, c:c + 1], c, 1, ALU.logical_shift_right, ALU.bitwise_and)
            dve.wait_ge(s_dst, 16)
            dve.wait_ge(s_src, 16)
            step_done(dve.tensor_tensor(keys[1][:, :].bitcast(I32), keys[0][:, :].bitcast(I32), keys[1][:, :].bitcast(I32),
                                        ALU.bitwise_xor))
            dve.tensor_scalar(sign[:, :], signi[:, :], -2.0, 1.0, ALU.mult, ALU.add)
            dve.tensor_scalar(loops[P - 32:P, :].bitcast(I32), loops[P - 32:P, :].bitcast(I32), float(NODES), float(KEY_BASE),
                              ALU.min, ALU.add)
            step_done(dve.tensor_scalar(keys[0][:, :].bitcast(I32), keys[0][:, :].bitcast(I32), float(KEY_BASE), None, ALU.add))
            dve.tensor_scalar(loops[P - 32:P, :].bitcast(I32), loops[P - 32:P, :].bitcast(I32), NODE_BITS, None,
                              ALU.logical_shift_left)
            step_done(dve.scalar_tensor_tensor(out=keys[1][:, :].bitcast(I32), in0=keys[0][:, :].bitcast(I32),
                                               scalar=NODE_BITS, in1=keys[1][:, :].bitcast(I32),
                                               op0=ALU.logical_shift_left, op1=ALU.bitwise_or))
            nturn = 0
            for st in stages:
                if st[0] == "cmp":
                    _, tiles, which, bit, direction = st
                    src, dst = tiles[which][:, :], tiles[1 - which][:, :]
                    ops = (ALU.min, ALU.max)
                    for d, ((a, b), (x, y)) in enumerate(zip(pair_views(src, bit, direction), pair_views(dst, bit, direction))):
                        dve.tensor_tensor(x, a, b, ops[d])
                        last = dve.tensor_tensor(y, a, b, ops[1 - d])
                    step_done(last)
                elif st[0] == "sign":
                    _, tiles, which, col = st
                    step_done(dve.tensor_scalar(tiles[1 - which][:, :], tiles[which][:, :], sign[:, col:col + 1], None, ALU.mult))
                elif st[0] == "turn":
                    n = st[1]
                    _, src, dst, blocks, col = plan[n]
                    for b in range(1, bank_count(blocks), 2):
                        dve.wait_ge(s_turn, turned(n, b))
                        out = dst[:, b * BANK:(b + 1) * BANK]
                        if col is None:
                            last = dve.tensor_copy(out, banks[b][:, :])
                        else:
                            last = dve.tensor_scalar(out, banks[b][:, :], sign[:, col:col + 1], None, ALU.mult)
                        last.then_inc(s_evac_v, 1)
                    dve.wait_ge(s_evac_a, emptied_a(n + 1))
                    if emptied_v(n + 1):
                        dve.wait_ge(s_evac_v, emptied_v(n + 1))
                    step_done(dve.memset(mark[:, :], 0.0))
                elif st[0] == "join":
                    src, dst = keys[st[1]], keys[1 - st[1]]
                    dve.tensor_copy(dst[0:P - 32, :], src[0:P - 32, :])
                    step_done(dve.tensor_tensor(dst[P - 32:P, :], src[P - 32:P, :], loops[P - 32:P, :], ALU.min))
                    step_done(dve.tensor_tensor(umax[P - 32:P, :], src[P - 32:P, :], loops[P - 32:P, :], ALU.max))
                elif st[0] == "upin":
                    dve.wait_ge(s_upin, 16)
            assert done[0] == last_step, (done[0], last_step)


IMAGES = 32
SIDE = 32
TOKENS = SIDE * SIDE
TILES = TOKENS // P
WIN = 8
WTOK = WIN * WIN
WGRID = SIDE // WIN
SHIFT = 4
PAD = SIDE + SHIFT
HEADS = 8
HDIM = P // HEADS
PAIRS = WGRID * WGRID // 2
GROUPS = HEADS // 2
VW = 2 * (HDIM + 1)
GHEADS = 4
GDIM = 16
NROW = GDIM + 2 * GHEADS
RING_S = 4
NEG = -1.0e9
SCALE = HDIM ** -0.5
EPS_LN = 1e-6
EPS_TOKEN = 1e-5


class Chain:

    def __init__(self, sem):
        self.sem, self.per, self.k = sem, None, 0

    def start(self, m):
        self.m, self.k = m, 0

    def value(self):
        return self.k if self.per is None else self.m * self.per + self.k

    def link(self, eng, ins):
        ins.then_inc(self.sem, 1)
        self.k += 1
        eng.wait_ge(self.sem, self.value())

    def end(self):
        if self.per is None:
            self.per = self.k
        assert self.per == self.k


def attention(nc, x, w_qkv, b_qkv, w_o, b_o, w_gat, att_src, att_dst, x2_out, tnT_out, node_rows):
    with ExitStack() as ctx:
        def sb(name, shape, dt=F32):
            return ctx.enter_context(nc.sbuf_tensor("attn_" + name, shape, dt))

        def ps(name):
            return ctx.enter_context(nc.psum_tensor("attn_" + name, [P, BANK], F32))

        def sem(name):
            return ctx.enter_context(nc.semaphore("attn_" + name))

        wqkv = sb("wqkv", [P, 3 * P])
        wo = sb("wo", [P, P])
        wgat = sb("wgat", [P, GDIM])
        bias = sb("bias", [P, 4])
        attv = sb("attv", [P, 2, GDIM])
        ident = sb("ident", [P, P])
        ones = sb("ones", [P, 1])
        hm = sb("hm", [P, HEADS])
        hmi = sb("hmi", [P, 2, HEADS], I32)
        mi = sb("mi", [P, 4, WTOK], I32)
        masks = sb("masks", [P, 3, WTOK])
        eps = sb("eps", [P, 2])
        xin = sb("xin", [P, TILES, P])
        xn = sb("xn", [P, TILES, P])
        xres = sb("xres", [P, TILES, P])
        x2 = sb("x2", [P, TILES, P])
        tn = sb("tn", [P, TILES, P])
        tnT = sb("tnT", [P, TOKENS])
        hrow = sb("hrow", [P, TILES, NROW])
        hprod = sb("hprod", [P, 2, TILES, GDIM])
        wmaj = sb("wmaj", [P, WGRID, WGRID, WTOK])
        ypad = sb("ypad", [P, PAD, PAD])
        ywin = sb("ywin", [P, WGRID, WGRID, WTOK])
        zmaj = sb("zmaj", [P, SIDE, SIDE])
        zrow = sb("zrow", [P, SIDE, SIDE])
        qT = [[sb(f"qT{s}{h}", [P, BANK]) for h in range(2)] for s in range(2)]
        kT = [[sb(f"kT{s}{h}", [P, BANK]) for h in range(2)] for s in range(2)]
        km = [[sb(f"km{s}{h}", [P, PAIRS, HEADS, WTOK]) for h in range(2)] for s in range(2)]
        vx = [sb(f"vx{s}", [P, 2 * PAIRS, GROUPS, VW]) for s in range(2)]
        S = [[sb(f"S{s}{i}", [P, HEADS, WTOK]) for i in range(RING_S)] for s in range(2)]
        mx = [sb(f"mx{s}", [P, PAIRS, HEADS]) for s in range(2)]
        pT = [[sb(f"pT{s}{i}", [P, GROUPS, P]) for i in range(2)] for s in range(2)]
        att = [sb(f"att{h}", [P, PAIRS // 2, 2, P]) for h in range(2)]
        rsum = [sb(f"rsum{i}", [P, 2, HEADS]) for i in range(2)]
        attT = [sb(f"attT{s}", [P, BANK]) for s in range(2)]
        st6 = [sb(f"st6{i}", [P, TILES, 6]) for i in range(2)]
        mv = [sb(f"mv{i}", [P, TILES, 2]) for i in range(2)]
        nw = [sb(f"nw{i}", [P, 4, TILES]) for i in range(2)]

        score_bank = [ps("score0"), ps("score1")]
        turn_bank = [ps("turn0"), ps("turn1")]
        out_bank = [ps("out0"), ps("out1")]
        misc = [ps("misc0"), ps("misc1")]

        s_w = sem("s_w")
        s_c = sem("s_c")
        s_cv = sem("s_cv")
        s_full = [sem("s_full0"), sem("s_full1")]
        s_free = [sem("s_free0"), sem("s_free1")]
        s_xin = sem("s_xin")
        s_xres = sem("s_xres")
        s_xn = sem("s_xn")
        s_km = [sem("s_kma"), sem("s_kmb")]
        s_sc = [sem("s_sca"), sem("s_scb")]
        s_mx = [sem("s_mxa"), sem("s_mxb")]
        s_sub = [sem("s_suba"), sem("s_subb")]
        s_exp = [sem("s_expa"), sem("s_expb")]
        s_pt = [sem("s_pta"), sem("s_ptb")]
        s_pte = [sem("s_ptea"), sem("s_pteb")]
        s_pv = sem("s_pv")
        s_nrm = sem("s_nrm")
        s_y = [sem("s_y"), sem("s_z")]
        s_roll = [sem("s_yroll"), sem("s_zroll")]
        YC, ZC = 2 + WGRID, 4
        s_x2 = sem("s_x2")
        s_tn = sem("s_tn")
        s_ct = sem("s_ct")
        s_h = sem("s_h")
        s_x2st = sem("s_x2st")
        s_tst = sem("s_tst")
        s_hst = sem("s_hst")
        s_passed = [sem("s_passed_v"), sem("s_passed_p")]
        ch_f = Chain(sem("ch_f"))
        ch_c = Chain(sem("ch_c"))
        ch_h = Chain(sem("ch_h"))
        ch_m = Chain(sem("ch_m"))
        s_recip = sem("s_recip")

        TASKS = [("Ap0", 1), ("Bp0", 3), ("Av0", 0), ("Bv0", 2),
                 ("Aq1", 0), ("Ak1", 0), ("Bq1", 2), ("Bk1", 2),
                 ("CT0", 4), ("CT1", 4),
                 ("CH0", 4), ("Ao1", 1), ("Bo1", 3),
                 ("Ap1", 1), ("Bp1", 3), ("Av1", 0), ("Bv1", 2),
                 ("FT0", -1), ("FT1", -1),
                 ("Aq0", -1), ("Ak0", -1), ("CZ0", 3), ("CZ1", 3),
                 ("Bq0", 1), ("Bk0", 1), ("Ao0", 0), ("Bo0", 2)]
        NAMES = [name for name, _ in TASKS]
        LAG = dict(TASKS)
        LAG.update(A=0, B=2)
        LAST_LAG = 4
        SLOT_TASKS = [4, 4, 2, 3, 4, 2, 4, 4]

        def slot_tasks(j):
            first = sum(SLOT_TASKS[:j])
            return NAMES[first:first + SLOT_TASKS[j]]

        def active(what, n):
            return not isinstance(n, int) or 0 <= n - LAG[what] < IMAGES

        def bank_of(task):
            return NAMES.index(task) % 2

        def count(n, task):
            at = NAMES.index(task)
            total = 0
            for i, (t, lag) in enumerate(TASKS):
                if bank_of(t) != bank_of(task):
                    continue
                m = n - lag
                if isinstance(n, int):
                    total = total + min(max(m, 0), IMAGES) + (i <= at and 0 <= m < IMAGES)
                else:
                    total = total + m + int(i <= at)
            return total

        def done(task, m):
            return count(m + LAG[task], task)

        def later(n, j, slots):
            return (n, j - slots) if j >= slots else (n - 1, j - slots + PAIRS)

        def streams(n):
            return [s for s in "AB" if active(s, n)]

        def first(m):
            return isinstance(m, int) and m == 0

        def steps(eng, body):
            for n in range(-1, LAST_LAG + 1):
                body(n)
            with eng.Fori(LAST_LAG + 1, IMAGES - 1) as n:
                body(n)
            for n in range(IMAGES - 1, IMAGES + LAST_LAG):
                body(n)

        STREAM = {"A": 0, "B": 1}
        block = ctx.enter_context(nc.Block())

        @block.sync
        def _(sp):
            sp.dma_start(wqkv[:, :], w_qkv).then_inc(s_w, 16)
            sp.dma_start(wo[:, :], w_o).then_inc(s_w, 16)
            sp.dma_start(wgat[:, :], w_gat).then_inc(s_w, 16)
            sp.dma_start(bias[:, 0:3], b_qkv.rearrange("(c p) -> p c", p=P),
                         allow_slow_non_contiguous=True).then_inc(s_w, 16)
            sp.dma_start(bias[:, 3:4], b_o.rearrange("(p o) -> p o", o=1), allow_slow_non_contiguous=True).then_inc(s_w, 16)
            sp.dma_start(attv[:, 0, :], att_src.rearrange("(o h) e -> o (h e)", o=1).to_broadcast([P, GDIM])).then_inc(s_w, 16)
            sp.dma_start(attv[:, 1, :], att_dst.rearrange("(o h) e -> o (h e)", o=1).to_broadcast([P, GDIM])).then_inc(s_w, 16)

            def body(n):
                if active("FT0", n):
                    m = n + 1
                    if not first(m):
                        sp.wait_ge(s_xn, m)
                    sp.dma_start(xin[:, :, :], x[m].rearrange("(j r) c d -> (r c) j d", j=TILES)).then_inc(s_xin, 16)
                if active("CZ0", n):
                    m = n - LAG["CZ0"]
                    if not first(m):
                        sp.wait_ge(s_x2, m)
                    sp.dma_start(xres[:, :, :], x[m].rearrange("(j r) c d -> (r c) j d", j=TILES)).then_inc(s_xres, 16)
                if active("CT0", n):
                    m = n - LAG["CT0"]
                    sp.wait_ge(s_ct, 2 * m + 2)
                    sp.dma_start(tnT_out[m], tnT[:, :]).then_inc(s_tst, 16)
                    sp.wait_ge(s_h, m + 1)
                    sp.dma_start(node_rows[m].rearrange("(j p) d -> p j d", p=P), hrow[:, :, :]).then_inc(s_hst, 16)
                if active("CZ0", n):
                    m = n - LAG["CZ0"]
                    sp.wait_ge(s_x2, m + 1)
                    sp.dma_start(x2_out[m].rearrange("(j p) d -> p j d", p=P), x2[:, :, :]).then_inc(s_x2st, 16)

            steps(sp, body)
            sp.wait_ge(s_x2st, 16 * IMAGES)
            sp.wait_ge(s_tst, 16 * IMAGES)
            sp.wait_ge(s_hst, 16 * IMAGES)

        @block.gpsimd
        def _(pool):
            pool.memset(ident[:, :], 0.0).then_inc(s_c, 1)
            pool.memset(eps[:, 0:1], EPS_LN)
            pool.memset(eps[:, 1:2], EPS_TOKEN)
            for s in range(2):
                v = vx[s][:, :, :, :].rearrange("p w g c -> p (w g c)")
                pool.memset(v, 0.0).then_inc(s_c, 1)
            pool.wait_ge(s_c, 3)
            pool.affine_select(out=ident[:, :], in_=ident[:, :], compare_op=ALU.not_equal, fill=1.0,
                               base=0, pattern=[[-1, P]], channel_multiplier=1).then_inc(s_c, 1)
            for s in range(2):
                pool.wait_ge(s_c, 4 + 2 * s)
                pool.memset(vx[s][0:WTOK, :, :, HDIM:HDIM + 1], 1.0).then_inc(s_c, 1)
                pool.wait_ge(s_c, 5 + 2 * s)
                pool.memset(vx[s][WTOK:P, :, :, VW - 1:VW], 1.0).then_inc(s_c, 1)
            pool.wait_ge(s_c, 8)
            pool.iota(hmi[:, 0, :], pattern=[[0, HEADS]], base=0, channel_multiplier=1).then_inc(s_c, 1)
            pool.wait_ge(s_c, 9)
            pool.iota(hmi[:, 1, :], pattern=[[1, HEADS]], base=0, channel_multiplier=0).then_inc(s_c, 1)
            pool.wait_ge(s_c, 10)
            pool.iota(mi[:, 0, :], pattern=[[0, WTOK]], base=0, channel_multiplier=1).then_inc(s_c, 1)
            pool.wait_ge(s_c, 11)
            pool.iota(mi[:, 1, :], pattern=[[1, WTOK]], base=0, channel_multiplier=0).then_inc(s_c, 1)

            def masked_keys(s, m, h):
                st, b = STREAM[s], bank_of(f"{s}k{h}")
                pool.wait_ge(s_free[b], done(f"{s}k{h}", m))
                k = kT[st][h][:, :].rearrange("p (w k) -> p w k", w=PAIRS)
                shape = [P, 2, HEADS, WTOK]
                for i in range(PAIRS // 2):
                    if not first(m):
                        pool.wait_ge(s_sc[st], (m - 1) * PAIRS + 4 * h + i + 1)
                    pool.tensor_tensor(km[st][h][:, 2 * i:2 * i + 2, :, :], k[:, 2 * i:2 * i + 2, :].unsqueeze(2).to_broadcast(shape),
                                       hm[:, :].unsqueeze(1).unsqueeze(3).to_broadcast(shape), ALU.mult).then_inc(s_km[st], 1)

            def wrap(m):
                pool.wait_ge(s_y[0], 2 * m + 2)
                if not first(m):
                    pool.wait_ge(s_full[bank_of("Bv1")], done("Bv1", m - 1))
                pool.sem_inc(s_passed[1], 1)
                pool.tensor_copy(ypad[:, 0:SIDE, SIDE:PAD], ypad[:, 0:SIDE, 0:SHIFT]).then_inc(s_roll[0], 1)
                pool.wait_ge(s_roll[0], YC * m + 1)
                pool.sem_inc(s_passed[1], 1)
                pool.tensor_copy(ypad[:, SIDE:PAD, :], ypad[:, 0:SHIFT, :]).then_inc(s_roll[0], 1)
                pool.wait_ge(s_roll[0], YC * m + 2)
                pool.sem_inc(s_passed[1], 1)
                for a in range(WGRID):
                    r = a * WIN + SHIFT
                    pool.tensor_copy(ywin[:, a, :, :].rearrange("p b (h c) -> p h b c", h=WIN),
                                     ypad[:, r:r + WIN, SHIFT:PAD].rearrange("p h (b c) -> p h b c", b=WGRID)
                                     ).then_inc(s_roll[0], 1)

            def unroll(m):
                pool.wait_ge(s_y[1], 2 * m + 2)
                if not first(m):
                    pool.wait_ge(s_full[bank_of("CZ1")], done("CZ1", m - 1))
                pool.sem_inc(s_passed[1], 1)
                e = SIDE - SHIFT
                for to, of in (((SHIFT, SIDE), (0, e)), ((0, SHIFT), (e, SIDE))):
                    for to2, of2 in (((SHIFT, SIDE), (0, e)), ((0, SHIFT), (e, SIDE))):
                        pool.tensor_copy(zrow[:, to[0]:to[1], to2[0]:to2[1]], zmaj[:, of[0]:of[1], of2[0]:of2[1]]
                                         ).then_inc(s_roll[1], 1)

            pool.wait_ge(s_cv, 2)

            def body(n):
                for s in "AB":
                    if active(f"{s}k1", n):
                        masked_keys(s, n - LAG[f"{s}k1"], 1)
                if active("Ap1", n):
                    wrap(n - LAG["Ap1"])
                if active("Bp1", n):
                    unroll(n - LAG["Bp1"])
                for s in "AB":
                    if active(f"{s}k0", n):
                        masked_keys(s, n - LAG[f"{s}k0"], 0)

            steps(pool, body)

        @block.scalar
        def _(act):
            act.wait_ge(s_w, 16 * 7)
            act.wait_ge(s_c, 8)

            def take(n, task):
                b = bank_of(task)
                act.wait_ge(s_full[b], count(n, task))
                return misc[b]

            def queries_or_keys(n, task):
                st, h, m = STREAM[task[0]], int(task[2]), n - LAG[task]
                t = take(n, task)
                if not first(m):
                    used = s_sc if task[1] == "q" else s_km
                    act.wait_ge(used[st], (m - 1) * PAIRS + 4 * h + 4)
                dst, col = ((qT, 0), (kT, 1))[task[1] == "k"]
                act.activation(dst[st][h][:, :], t[:, :], ACT.Identity, bias=bias[:, col:col + 1]).then_inc(s_free[bank_of(task)], 1)

            def values(n, task):
                st, h = STREAM[task[0]], int(task[2])
                t = take(n, task)
                if not first(n - LAG[task]):
                    act.wait_ge(s_pv, (n - 1) * PAIRS + 4 * h + 4)
                w = slice(PAIRS * h, PAIRS * h + PAIRS)
                src = t[:, :].rearrange("p (w g d) -> p w g d", w=PAIRS, g=GROUPS)
                act.activation(vx[st][0:WTOK, w, :, 0:HDIM], src[0:WTOK], ACT.Copy)
                act.activation(vx[st][WTOK:P, w, :, HDIM + 1:VW - 1], src[WTOK:P], ACT.Copy).then_inc(s_free[bank_of(task)], 1)

            def attended(n, task):
                act.activation(attT[STREAM[task[0]]][:, :], take(n, task)[:, :], ACT.Identity, bias=bias[:, 2:3]
                               ).then_inc(s_free[bank_of(task)], 1)

            def projected(n, task):
                st, h, m, b = STREAM[task[0]], int(task[2]), n - LAG[task], bank_of(task)
                src_bank, dst = take(n, task), (ypad, zmaj)[st]
                if not first(m):
                    act.wait_ge(s_roll[st], (YC, ZC)[st] * m)
                for i in range(2):
                    r = (2 * h + i) * WIN
                    src = src_bank[:, i * 256:(i + 1) * 256].rearrange("p (b h c) -> p h b c", b=WGRID, h=WIN)
                    out = dst[:, r:r + WIN, 0:SIDE].rearrange("p h (b c) -> p h b c", b=WGRID)
                    last = act.activation(out, src, ACT.Identity, bias=bias[:, 3:4])
                last.then_inc(s_free[b], 1)
                act.wait_ge(s_free[b], count(n, task))
                act.sem_inc(s_y[st], 1)

            def tokens(n, task):
                m, i, b = n - LAG[task], int(task[2]), bank_of(task)
                t = take(n, task)
                if i == 0 and not first(m):
                    act.wait_ge(s_tst, 16 * m)
                act.activation(tnT[:, i * BANK:(i + 1) * BANK], t[:, :], ACT.Copy).then_inc(s_free[b], 1)
                act.wait_ge(s_free[b], count(n, task))
                act.sem_inc(s_ct, 1)

            def image(n, task):
                i, b = int(task[2]), bank_of(task)
                t = take(n, task)
                for a in range(2):
                    src = t[:, a * 256:(a + 1) * 256].rearrange("p (h b c) -> p h b c", h=WIN, b=WGRID)
                    out = wmaj[:, 2 * i + a, :, :].rearrange("p b (h c) -> p h b c", h=WIN)
                    last = act.activation(out, src, ACT.Copy)
                last.then_inc(s_free[b], 1)

            KINDS = {"Aq": queries_or_keys, "Ak": queries_or_keys, "Bq": queries_or_keys, "Bk": queries_or_keys,
                     "Av": values, "Ao": attended, "Bo": attended, "Ap": projected, "Bp": projected,
                     "CT": tokens, "FT": image}

            def body(n):
                for j in range(PAIRS):
                    k, i = later(n, j, 1)
                    for s in streams(k):
                        st, m = STREAM[s], k - LAG[s]
                        act.wait_ge(s_sub[st], m * PAIRS + i + 1)
                        t = S[st][i % RING_S][:, :, :]
                        act.activation(t, t, ACT.Exp, scale=SCALE).then_inc(s_exp[st], 1)
                    k, i = later(n, j, 2)
                    for s in streams(k):
                        st, m = STREAM[s], k - LAG[s]
                        act.wait_ge(s_pt[st], m * PAIRS + i + 1)
                        if not (isinstance(k, int) and first(m) and i < 2):
                            act.wait_ge(s_pv, k * PAIRS + i - 1)
                        act.activation(pT[st][i % 2][:, :, :], turn_bank[st][:, :].rearrange("p (g q) -> p g q", g=GROUPS),
                                       ACT.Copy).then_inc(s_pte[st], 1)
                    for task in slot_tasks(j):
                        if task[:2] in KINDS and active(task, n):
                            KINDS[task[:2]](n, task)

            steps(act, body)

        @block.tensor
        def _(pe):
            pe.wait_ge(s_w, 16 * 7)
            pe.wait_ge(s_c, 8)

            def take(n, task):
                b = bank_of(task)
                before = count(n, task) - 1
                if not (isinstance(before, int) and before == 0):
                    pe.wait_ge(s_free[b], before)
                return misc[b]

            def source(task):
                m, t = task[0], task
                return wmaj if m == "A" else ywin

            def wait_source(n, task):
                m = n - LAG[task]
                if task[0] == "A":
                    for i in range(2):
                        pe.wait_ge(s_free[bank_of(f"FT{i}")], done(f"FT{i}", m))
                else:
                    pe.wait_ge(s_roll[0], YC * m + YC)

            def queries_or_keys(n, task):
                h = int(task[2])
                t = take(n, task)
                if h == 0:
                    wait_source(n, task)
                w = wqkv[:, 0:P] if task[1] == "q" else wqkv[:, P:2 * P]
                return pe.matmul(t[:, :], w, source(task)[:, 2 * h:2 * h + 2].rearrange("p a b k -> p (a b k)"), start=True, stop=True)

            def values(n, task):
                h = int(task[2])
                t = take(n, task)
                wv = wqkv[:, 2 * P:3 * P].rearrange("p (g e d) -> p e g d", g=GROUPS, e=2)
                for i in range(PAIRS):
                    a, b = divmod(PAIRS * h + i, WGRID)
                    for e in range(2):
                        last = pe.matmul(t[e * WTOK:(e + 1) * WTOK, i * WTOK:(i + 1) * WTOK], source(task)[:, a, b, :], wv[:, e],
                                         start=True, stop=True)
                return last

            def attended(n, task):
                st, h = STREAM[task[0]], int(task[2])
                t = take(n, task)
                k = n - LAG[task] + LAG[task[0]]
                pe.wait_ge(s_nrm, k * PAIRS + 4 * h + 4)
                for i in range(PAIRS // 2):
                    last = pe.transpose(t[:, i * P:(i + 1) * P], att[h][:, i, st, :], ident[:, :])
                return last

            def projected(n, task):
                t = take(n, task)
                turned = f"{task[0]}o{task[2]}"
                pe.wait_ge(s_free[bank_of(turned)], done(turned, n - LAG[task]))
                return pe.matmul(t[:, :], wo[:, :], attT[STREAM[task[0]]][:, :], start=True, stop=True)

            def result(n, task):
                i = int(task[2])
                t = take(n, task)
                pe.wait_ge(s_roll[1], ZC * (n - LAG[task]) + ZC)
                for k in range(4):
                    r = (4 * i + k) * (P // SIDE)
                    last = pe.transpose(t[:, k * P:(k + 1) * P], zrow[:, r:r + P // SIDE, :].rearrange("p h w -> p (h w)"), ident[:, :])
                return last

            def tiles(n, task):
                i = int(task[2])
                t, src, ready = take(n, task), (tn, xn)[task[0] == "F"], (s_tn, s_xn)[task[0] == "F"]
                pe.wait_ge(ready, n - LAG[task] + 1)
                for k in range(4):
                    last = pe.transpose(t[:, k * P:(k + 1) * P], src[:, 4 * i + k, :], ident[:, :])
                return last

            def graph_features(n, task):
                t = take(n, task)
                pe.wait_ge(s_ct, 2 * (n - LAG[task]) + 2)
                for k in range(TILES):
                    last = pe.matmul(t[:, k * GDIM:(k + 1) * GDIM], tnT[:, k * P:(k + 1) * P], wgat[:, :], start=True, stop=True)
                return last

            KINDS = {"Aq": queries_or_keys, "Ak": queries_or_keys, "Bq": queries_or_keys, "Bk": queries_or_keys,
                     "Av": values, "Bv": values, "Ao": attended, "Bo": attended, "Ap": projected, "Bp": projected,
                     "CT": tiles, "FT": tiles, "CZ": result, "CH": graph_features}

            def scores(n, s, j):
                st, m, h = STREAM[s], n - LAG[s], j // 4
                if j % 4 == 0:
                    pe.wait_ge(s_free[bank_of(f"{s}q{h}")], done(f"{s}q{h}", m))
                pe.wait_ge(s_km[st], m * PAIRS + j + 1)
                if j > 0 or not first(m):
                    pe.wait_ge(s_sub[st], m * PAIRS + j)
                for e in range(2):
                    w = (2 * j + e) % PAIRS
                    last = pe.matmul(score_bank[st][e * WTOK:(e + 1) * WTOK, :], qT[st][h][:, w * WTOK:(w + 1) * WTOK],
                                     km[st][h][:, w].rearrange("p h k -> p (h k)"), start=True, stop=True)
                last.then_inc(s_sc[st], 1)

            def turn(n, s, j):
                st, m = STREAM[s], n - LAG[s]
                pe.wait_ge(s_exp[st], m * PAIRS + j + 1)
                if j > 0 or not first(m):
                    pe.wait_ge(s_pte[st], m * PAIRS + j)
                src = S[st][j % RING_S][:, :, :].rearrange("p h k -> p (h k)")
                for g in range(GROUPS):
                    last = pe.transpose(turn_bank[st][:, g * P:(g + 1) * P], src[:, g * P:(g + 1) * P], ident[:, :])
                last.then_inc(s_pt[st], 1)

            def weigh(n, j):
                if j >= 2 or not first(n):
                    pe.wait_ge(s_nrm, n * PAIRS + j - 1)
                for s in streams(n):
                    st, m = STREAM[s], n - LAG[s]
                    if j % 4 == 0:
                        v = f"{s}v{j // 4}"
                        pe.wait_ge(s_free[bank_of(v)], done(v, m))
                    pe.wait_ge(s_pte[st], m * PAIRS + j + 1)
                    for g in range(GROUPS):
                        for e in range(2):
                            c = st * GROUPS * VW + g * VW
                            last = pe.matmul(out_bank[j % 2][e * WTOK:(e + 1) * WTOK, c:c + VW],
                                             pT[st][j % 2][:, g, e * WTOK:(e + 1) * WTOK], vx[st][:, 2 * j + e, g, :],
                                             start=True, stop=True)
                last.then_inc(s_pv, 1)

            def body(n):
                for j in range(PAIRS):
                    for s in streams(n):
                        scores(n, s, j)
                    k, i = later(n, j, 2)
                    for s in streams(k):
                        turn(k, s, i)
                    k, i = later(n, j, 3)
                    if streams(k):
                        weigh(k, i)
                    for task in slot_tasks(j):
                        if active(task, n):
                            KINDS[task[:2]](n, task).then_inc(s_full[bank_of(task)], 1)

            steps(pe, body)

        @block.vector
        def _(dve):
            dve.wait_ge(s_c, 12)
            cv = [0]

            def link(ins):
                ins.then_inc(s_cv, 1)
                cv[0] += 1
                dve.wait_ge(s_cv, cv[0])

            link(dve.tensor_scalar(hmi[:, 0, :], hmi[:, 0, :], 4, None, ALU.logical_shift_right))
            link(dve.tensor_tensor(hm[:, :], hmi[:, 0, :], hmi[:, 1, :], ALU.is_equal))
            link(dve.tensor_tensor(mi[:, 1, :], mi[:, 0, :], mi[:, 1, :], ALU.bitwise_xor))
            link(dve.tensor_scalar(mi[:, 2, :], mi[:, 1, :], 5, 1, ALU.logical_shift_right, ALU.bitwise_and))
            link(dve.tensor_scalar(mi[:, 3, :], mi[:, 1, :], 2, 1, ALU.logical_shift_right, ALU.bitwise_and))
            link(dve.tensor_scalar(mi[:, 0, :], mi[:, 0, :], 6, None, ALU.logical_shift_right))
            link(dve.tensor_tensor(mi[:, 3, :], mi[:, 3, :], mi[:, 0, :], ALU.mult))
            link(dve.tensor_tensor(mi[:, 0, :], mi[:, 2, :], mi[:, 3, :], ALU.max))
            big = NEG / SCALE
            link(dve.tensor_scalar(masks[:, 0, :], mi[:, 3, :], big, None, ALU.mult))
            link(dve.tensor_scalar(masks[:, 1, :], mi[:, 2, :], big, None, ALU.mult))
            link(dve.tensor_scalar(masks[:, 2, :], mi[:, 0, :], big, None, ALU.mult))

            def mask_of(j):
                row, right = j // 2 == WGRID - 1, j % 2 == 1
                return {(False, False): None, (False, True): 0, (True, False): 1, (True, True): 2}[(row, right)]

            def normalise(ch, k, src, dst, eps_col):
                for j in range(TILES):
                    last = dve.bn_stats(st6[k][:, j, :], src[:, j, :])
                ch.link(dve, last)
                dve.sem_inc(s_passed[0], 1)
                for j in range(TILES):
                    last = dve.bn_aggr(mv[k][:, j, :], st6[k][:, j, :])
                ch.link(dve, last)
                v, h, y, t = (nw[k][:, i, :] for i in range(4))
                ch.link(dve, dve.tensor_scalar(v, mv[k][:, :, 1], eps[:, eps_col:eps_col + 1], None, ALU.add))
                ch.link(dve, dve.tensor_scalar(h.bitcast(I32), v.bitcast(I32), 1, None, ALU.logical_shift_right))
                ch.link(dve, dve.tensor_scalar(y.bitcast(I32), h.bitcast(I32), -1.0, float(0x5F3759DF), ALU.mult, ALU.add))
                for _ in range(4):
                    ch.link(dve, dve.tensor_tensor(t, y, y, ALU.mult))
                    ch.link(dve, dve.scalar_tensor_tensor(out=h, in0=t, scalar=-0.5, in1=v, op0=ALU.mult, op1=ALU.mult))
                    ch.link(dve, dve.scalar_tensor_tensor(out=y, in0=h, scalar=1.5, in1=y, op0=ALU.add, op1=ALU.mult))
                for j in range(TILES):
                    last = dve.tensor_scalar(dst[:, j, :], src[:, j, :], mv[k][:, j, 0:1], y[:, j:j + 1],
                                             ALU.subtract, ALU.mult)
                return last

            def head(n):
                m = n + 1
                ch_f.start(m)
                dve.wait_ge(s_xin, 16 * m + 16)
                if not first(m):
                    for i in range(2):
                        dve.wait_ge(s_full[bank_of(f"FT{i}")], done(f"FT{i}", m - 1))
                normalise(ch_f, 0, xin, xn, 0).then_inc(s_xn, 1)
                ch_f.end()

            def residual(n):
                m = n - LAG["CZ0"]
                dve.wait_ge(s_xres, 16 * m + 16)
                if not first(m):
                    dve.wait_ge(s_x2st, 16 * m)
                for i in range(2):
                    b = bank_of(f"CZ{i}")
                    dve.wait_ge(s_full[b], count(n, f"CZ{i}"))
                    z = misc[b][:, :].rearrange("p (j d) -> p j d", d=P)
                    dve.tensor_tensor(x2[:, 4 * i:4 * i + 4, :], z, xres[:, 4 * i:4 * i + 4, :], ALU.add).then_inc(s_free[b], 1)
                for i in range(2):
                    b = bank_of(f"CZ{i}")
                    dve.wait_ge(s_free[b], count(n, f"CZ{i}"))
                dve.sem_inc(s_x2, 1)

            def tail(n):
                m = n - LAG["CZ0"]
                ch_c.start(m)
                if not first(m):
                    dve.wait_ge(s_ct, 2 * m)
                normalise(ch_c, 1, x2, tn, 1).then_inc(s_tn, 1)
                ch_c.end()

            def node_row(n):
                m, b = n - LAG["CH0"], bank_of("CH0")
                ch_h.start(m)
                dve.wait_ge(s_full[b], count(n, "CH0"))
                if not first(m):
                    dve.wait_ge(s_hst, 16 * m)
                dve.tensor_copy(hrow[:, :, 0:GDIM], misc[b][:, 0:TILES * GDIM].rearrange("p (j e) -> p j e", e=GDIM)
                                ).then_inc(s_free[b], 1)
                dve.wait_ge(s_free[b], count(n, "CH0"))
                for k in range(2):
                    last = dve.tensor_tensor(hprod[:, k], hrow[:, :, 0:GDIM],
                                             attv[:, k, :].unsqueeze(1).to_broadcast([P, TILES, GDIM]), ALU.mult)
                ch_h.link(dve, last)
                for k in range(2):
                    c = GDIM + k * GHEADS
                    last = dve.tensor_reduce(hrow[:, :, c:c + GHEADS],
                                             hprod[:, k].rearrange("p j (h e) -> p j h e", h=GHEADS), AX_X, ALU.add)
                last.then_inc(s_h, 1)
                ch_h.end()

            def b_values(n, h):
                b = bank_of(f"Bv{h}")
                dve.wait_ge(s_full[b], count(n, f"Bv{h}"))
                if not first(n - LAG["B"]):
                    dve.wait_ge(s_pv, (n - 1) * PAIRS + 4 * h + 4)
                w = slice(PAIRS * h, PAIRS * h + PAIRS)
                src = misc[b][:, :].rearrange("p (w g d) -> p w g d", w=PAIRS, g=GROUPS)
                dve.tensor_copy(vx[1][0:WTOK, w, :, 0:HDIM], src[0:WTOK])
                dve.tensor_copy(vx[1][WTOK:P, w, :, HDIM + 1:VW - 1], src[WTOK:P]).then_inc(s_free[b], 1)

            def normalised_output(n, j):
                on = streams(n)
                dve.wait_ge(s_pv, n * PAIRS + j + 1)
                lo, hi = STREAM[on[0]], STREAM[on[-1]] + 1
                o = out_bank[j % 2][:, 0:2 * GROUPS * VW].rearrange("p (s h d) -> p s h d", s=2, d=HDIM + 1)[:, lo:hi]
                r = rsum[j % 2][:, lo:hi, :]
                if j % 4 == 0:
                    for s in on:
                        if not first(n - LAG[s]):
                            turned = f"{s}o{j // 4}"
                            dve.wait_ge(s_full[bank_of(turned)], done(turned, n - LAG[s] - 1))
                dve.reciprocal(r, o[:, :, :, HDIM]).then_inc(s_recip, 1)
                dve.wait_ge(s_recip, n * PAIRS + j + 1)
                dve.tensor_tensor(att[j // 4][:, j % 4, lo:hi, :].rearrange("p s (h d) -> p s h d", h=HEADS),
                                  o[:, :, :, 0:HDIM], r.unsqueeze(3).to_broadcast([P, hi - lo, HEADS, HDIM]),
                                  ALU.mult).then_inc(s_nrm, 1)

            def less_maximum(n, j):
                full = [P, HEADS, WTOK]
                src = {}
                for s in streams(n):
                    st, m = STREAM[s], n - LAG[s]
                    t = S[st][j % RING_S][:, :, :]
                    src[s] = score_bank[st][:, :].rearrange("p (h k) -> p h k", h=HEADS)
                    dve.wait_ge(s_sc[st], m * PAIRS + j + 1)
                    if j >= RING_S or not first(m):
                        dve.wait_ge(s_pt[st], m * PAIRS + j + 1 - RING_S)
                    if s == "B":
                        if j == 0:
                            ch_m.start(m)
                        if mask_of(j) is not None:
                            ch_m.link(dve, dve.tensor_tensor(t, src[s], masks[:, mask_of(j), :].unsqueeze(1).to_broadcast(full), ALU.add))
                            src[s] = t
                    dve.tensor_reduce(mx[st][:, j, :], src[s], AX_X, ALU.max).then_inc(s_mx[st], 1)
                for s in streams(n):
                    st, m = STREAM[s], n - LAG[s]
                    dve.wait_ge(s_mx[st], m * PAIRS + j + 1)
                    dve.tensor_tensor(S[st][j % RING_S][:, :, :], src[s], mx[st][:, j, :].unsqueeze(2).to_broadcast(full),
                                      ALU.subtract).then_inc(s_sub[st], 1)
                    if s == "B" and j == PAIRS - 1:
                        ch_m.end()

            def body(n):
                for j in range(PAIRS):
                    k, i = later(n, j, 4)
                    if streams(k):
                        normalised_output(k, i)
                    less_maximum(n, j)
                    if j in (0, 4) and active(f"Bv{j // 4}", n):
                        b_values(n, j // 4)
                    if j == 3 and active("CH0", n):
                        node_row(n)
                    if j == 3 and active("FT0", n):
                        head(n)
                    if j == 6 and active("CZ0", n):
                        residual(n)
                    if j == 7 and active("CZ0", n):
                        tail(n)

            steps(dve, body)


CHUNKS = 64
TC = ROWS // CHUNKS
HC = EDGES // P // CHUNKS
EXPERTS = 4
HIDDEN = 256
HB = HIDDEN // P
UNIT = NODES // CHUNKS
UTILES = UNIT // P
LOW = -1.0e38
HI = NODES // P
MCH, LCH, ACH = 0, GHEADS, 2 * GHEADS
RING = 8


def edges(nc, sorted_keys, node_rows, edge_index, tnT, W1, b1, W2, b2, state_rows, expert_out, last_state, first_start, hist_out):
    with ExitStack() as ctx:
        def sb(name, shape, dt=F32):
            return ctx.enter_context(nc.sbuf_tensor("edge_" + name, shape, dt))

        def ps(name):
            return ctx.enter_context(nc.psum_tensor("edge_" + name, [P, BANK], F32))

        def sem(name):
            return ctx.enter_context(nc.semaphore("edge_" + name))

        key = [sb(f"key{b}", [P, 2, TC], I32) for b in range(2)]
        dst = sb("dst", [P, 2, TC], I32)
        low = sb("low", [P, TC], I32)
        node = sb("node", [P, TC], I32)
        src = [sb(f"src{b}", [P, TC], I32) for b in range(2)]
        start = [sb(f"start{b}", [P, TC]) for b in range(2)]
        keep = [sb(f"keep{b}", [P, TC]) for b in range(2)]
        neg = [sb(f"neg{b}", [P, TC]) for b in range(2)]
        pos = sb("pos", [P, TC])
        posi = sb("posi", [P, TC], I32)
        posv = sb("posv", [P, TC])
        base = sb("base", [P, 1])
        cmin = sb("cmin", [P, 1])
        fmin = sb("fmin", [P, 1])
        G = [sb(f"G{b}", [P, TC, NROW]) for b in range(2)]
        O = [sb(f"O{b}", [P, TC + 1, NROW]) for b in range(2)]
        adm = sb("adm", [P, GHEADS, TC])
        adp = [sb(f"adp{b}", [P, GHEADS, TC]) for b in range(2)]
        ad0 = sb("ad0", [P, NROW])
        first = sb("first", [P, 1], I32)
        e = sb("e", [P, GHEADS, TC])
        w = sb("w", [P, 2, GHEADS, TC])
        msg = sb("msg", [P, GHEADS, GDIM // GHEADS, TC])
        dx = [sb(f"dx{b}", [P, HC], I32) for b in range(2)]
        dlo = sb("dlo", [P, 2, HC], I32)
        dlf = sb("dlf", [P, 2, HC])
        io = sb("io", [P, HI], I32)
        iob = sb("iob", [P, HI], BF16)
        ohl = sb("ohl", [P, RING, P], BF16)
        ohh = sb("ohh", [P, RING, HI], BF16)
        hist = sb("hist", [P, HI])
        w1 = sb("w1", [P, EXPERTS, HIDDEN])
        w2 = sb("w2", [P, EXPERTS, HB, P])
        b1c = sb("b1c", [P, EXPERTS * HB])
        b2r = sb("b2r", [P, EXPERTS * P])
        xt = [sb(f"xt{b}", [P, UNIT]) for b in range(2)]
        hid = sb("hid", [P, EXPERTS * HB, UNIT])
        yo = [sb(f"yo{b}", [P, UTILES, EXPERTS * P]) for b in range(2)]
        hbank = [ps("hbank0"), ps("hbank1")]
        ybank = [ps("ybank0"), ps("ybank1")]
        cbank = [ps("cbank0"), ps("cbank1")]

        s_w = sem("s_w")
        s_c = sem("s_c")
        s_cv = sem("s_cv")
        s_key = [sem("s_key0"), sem("s_key1")]
        s_dec = sem("s_dec")
        s_g = [[sem(f"s_g{b}{i}") for i in range(2)] for b in range(2)]
        s_ad = sem("s_ad")
        s_lo = sem("s_lo")
        s_ex = sem("s_ex")
        s_math = sem("s_math")
        s_st = [sem("s_st0"), sem("s_st1")]
        s_dx = [sem("s_dx0"), sem("s_dx1")]
        s_dxr = sem("s_dxr")
        s_oh = sem("s_oh")
        s_ohp = sem("s_ohp")
        s_hs = sem("s_hs")
        s_xt = [sem("s_xt0"), sem("s_xt1")]
        s_l1 = sem("s_l1")
        s_ge = sem("s_ge")
        s_l2 = sem("s_l2")
        s_y = sem("s_y")
        s_yst = [sem("s_yst0"), sem("s_yst1")]
        s_end = sem("s_end")
        s_passed = sem("s_passed")

        keys_prev = sorted_keys[0:SORTED, :].rearrange("(p r) o -> p (r o)", p=P)
        keys_here = sorted_keys[1:1 + SORTED, :].rearrange("(p r) o -> p (r o)", p=P)
        raw_dst = edge_index[1, :].rearrange("(p c) -> p c", p=P)
        st_rows = state_rows[0:SORTED, :].rearrange("(p r) d -> p r d", p=P)
        halves = NODES // CHUNKS
        per_img = 1024 // UNIT

        def chunks(eng, body):
            body(0, 0)
            body(1, 0)
            with eng.Fori(1, CHUNKS // 2 - 1) as i:
                for b in range(2):
                    body(b, i)
            for b in range(2):
                body(b, CHUNKS // 2 - 1)

        def first_of(b, i, n=1):
            return isinstance(i, int) and 2 * i + b < n

        def last_of(b, i, n=1):
            return isinstance(i, int) and 2 * i + b >= CHUNKS - n

        block = ctx.enter_context(nc.Block())

        @block.sync
        def _(sp):
            sp.dma_start(w1[:, :, :], W1.rearrange("e p f -> p e f")).then_inc(s_w, 16)
            sp.dma_start(w2[:, :, :, :].rearrange("p e h d -> p (e h) d"), W2.rearrange("e (h p) d -> p (e h) d", p=P)).then_inc(s_w, 16)
            sp.dma_start(b1c[:, :], b1.rearrange("e (h p) -> p (e h)", p=P), allow_slow_non_contiguous=True).then_inc(s_w, 16)
            sp.dma_start(b2r[:, :], b2.rearrange("(o e) d -> o (e d)", o=1).to_broadcast([P, EXPERTS * P])).then_inc(s_w, 16)

            def load_keys(b, c):
                sp.dma_start(key[b][:, 0, :], keys_prev[:, bass.ds(c * TC, TC)]).then_inc(s_key[b], 16)
                sp.dma_start(key[b][:, 1, :], keys_here[:, bass.ds(c * TC, TC)]).then_inc(s_key[b], 16)

            def load_raw(b, c):
                sp.dma_start(dx[b][:, :], raw_dst[:, bass.ds(c * HC, HC)]).then_inc(s_dx[b], 16)

            def load_x(b, i):
                sp.dma_start(xt[b][:, :], tnT[i][:, b * UNIT:(b + 1) * UNIT]).then_inc(s_xt[b], 16)

            load_keys(0, 0)
            load_keys(1, 1)
            load_raw(0, 0)
            load_x(0, 0)

            def body(b, i):
                c = 2 * i + b
                if not last_of(b, i, 2):
                    sp.wait_ge(s_dec, c + 1)
                    load_keys(b, c + 2)
                if not last_of(b, i):
                    if not first_of(b, i):
                        sp.wait_ge(s_w, 64)
                        sp.wait_ge(s_dxr, c)
                        sp.wait_ge(s_l1, c * EXPERTS * HB)
                    load_raw(1 - b, c + 1)
                    load_x(1 - b, i + b)
                sp.wait_ge(s_math, c + 1)
                sp.dma_start(st_rows[:, bass.ds(c * TC, TC), :], O[b][:, 1:, :]).then_inc(s_st[b], 16)
                sp.wait_ge(s_y, (c + 1) * UTILES)
                sp.dma_start(expert_out[i][b].rearrange("(t p) d -> p t d", p=P), yo[b][:, :, :]).then_inc(s_yst[b], 16)

            chunks(sp, body)
            sp.dma_start(last_state, O[1][:, TC, :]).then_inc(s_end, 16)
            sp.dma_start(first_start, fmin[:, :]).then_inc(s_end, 16)
            sp.wait_ge(s_hs, CHUNKS)
            sp.dma_start(hist_out, hist[:, :]).then_inc(s_end, 16)
            sp.wait_ge(s_end, 48)
            for b in range(2):
                sp.wait_ge(s_st[b], 16 * CHUNKS // 2)
                sp.wait_ge(s_yst[b], 16 * CHUNKS // 2)

        @block.gpsimd
        def _(pool):
            pool.iota(posi[:, :], pattern=[[1, TC]], base=0, channel_multiplier=0).then_inc(s_c, 1)
            pool.iota(io[:, :], pattern=[[1, HI]], base=0, channel_multiplier=0).then_inc(s_c, 1)
            pool.wait_ge(s_dec, 1)
            pool.indirect_dma_start(ad0[:, :], None, node_rows, bass.IndirectOffsetOnAxis(ap=first[:, :], axis=0)).then_inc(s_ad, 16)

            def body(b, i):
                c = 2 * i + b
                pool.wait_ge(s_dec, c + 1)
                if not first_of(b, i, 2):
                    pool.wait_ge(s_math, c - 1)
                pool.sem_inc(s_passed, 1)
                for t in range(TC):
                    pool.indirect_dma_start(G[b][:, t, :], None, node_rows,
                                            bass.IndirectOffsetOnAxis(ap=src[b][:, t:t + 1], axis=0)
                                            ).then_inc(s_g[b][2 * t // TC], 16)

            chunks(pool, body)

        @block.scalar
        def _(act):
            act.wait_ge(s_w, 64)

            def body(b, i):
                c = 2 * i + b
                act.wait_ge(s_lo, c + 1)
                act.activation(w[:, :, :, :], w[:, :, :, :], ACT.Exp).then_inc(s_ex, 1)
                for k in range(EXPERTS * HB):
                    act.wait_ge(s_l1, c * EXPERTS * HB + k + 1)
                    if k == 0 and not first_of(b, i):
                        act.wait_ge(s_l2, c * UTILES)
                    act.activation(hid[:, k, :], hbank[k % 2][:, :], ACT.Gelu, bias=b1c[:, k:k + 1]).then_inc(s_ge, 1)

            chunks(act, body)

        @block.tensor
        def _(pe):
            pe.wait_ge(s_w, 64)

            def body(b, i):
                c = 2 * i + b
                if not first_of(b, i, 2):
                    pe.wait_ge(s_hs, c - 1)
                for t in range(HC):
                    pe.wait_ge(s_oh, c * HC + t + 1)
                    pe.matmul(cbank[b][:, 0:HI], ohl[:, t % RING, :], ohh[:, t % RING, :],
                              start=(t == 0), stop=(t == HC - 1)).then_inc(s_ohp, 1)
                pe.wait_ge(s_xt[b], 16 * i + 16)
                for k in range(EXPERTS * HB):
                    if k >= 2 or not first_of(b, i):
                        pe.wait_ge(s_ge, c * EXPERTS * HB + k - 1)
                    pe.matmul(hbank[k % 2][:, :], w1[:, k // HB, (k % HB) * P:(k % HB + 1) * P], xt[b][:, :],
                              start=True, stop=True).then_inc(s_l1, 1)
                pe.wait_ge(s_ge, (c + 1) * EXPERTS * HB)
                for t in range(UTILES):
                    if t >= 2 or not first_of(b, i):
                        pe.wait_ge(s_y, c * UTILES + t - 1)
                    for x in range(EXPERTS):
                        for h in range(HB):
                            last = pe.matmul(ybank[t % 2][:, x * P:(x + 1) * P], hid[:, x * HB + h, t * P:(t + 1) * P],
                                             w2[:, x, h, :], start=(h == 0), stop=(h == HB - 1))
                    last.then_inc(s_l2, 1)

            chunks(pe, body)

        @block.vector
        def _(dve):
            s_step = sem("s_step")
            per = {}

            class Steps:
                k = 0

            st = Steps()

            def link(ins, at):
                ins.then_inc(s_step, 1)
                st.k += 1
                dve.wait_ge(s_step, at + st.k)

            dve.wait_ge(s_c, 2)
            dve.wait_ge(s_w, 64)
            dve.tensor_copy(pos[:, :], posi[:, :])
            dve.tensor_copy(iob[:, :], io[:, :])
            dve.memset(hist[:, :], 0.0)
            dve.memset(fmin[:, :], 0.0)
            dve.memset(base[:, :], float(-ROWS))
            dve.memset(O[1][:, TC, MCH:LCH], LOW)
            dve.memset(O[1][:, TC, LCH:], 0.0).then_inc(s_cv, 1)
            dve.wait_ge(s_cv, 1)

            def decode(b, i, at):
                c = 2 * i + b
                dve.wait_ge(s_key[b], 32 * i + 32)
                if not first_of(b, i, 2):
                    for h in range(2):
                        dve.wait_ge(s_g[b][h], 16 * (TC // 2) * i)
                st.k = 0
                link(dve.tensor_scalar(dst[:, :, :], key[b][:, :, :], NODE_BITS, None, ALU.logical_shift_right), at)
                dve.tensor_tensor(start[b][:, :], dst[:, 0, :], dst[:, 1, :], ALU.not_equal)
                dve.tensor_scalar(low[:, :], key[b][:, 1, :], NODES - 1, None, ALU.bitwise_and)
                link(dve.tensor_scalar(node[:, :], dst[:, 1, :], float(KEY_BASE), None, ALU.subtract), at)
                dve.tensor_scalar(keep[b][:, :], start[b][:, :], -1.0, 1.0, ALU.mult, ALU.add)
                dve.tensor_scalar(neg[b][:, :], start[b][:, :], LOW, None, ALU.mult)
                dve.tensor_scalar(posv[:, :], pos[:, :], base[:, :], None, ALU.add)
                if first_of(b, i):
                    dve.tensor_copy(first[:, :], node[:, 0:1])
                link(dve.tensor_tensor(src[b][:, :], low[:, :], node[:, :], ALU.bitwise_xor), at)
                link(dve.tensor_tensor(posv[:, :], posv[:, :], start[b][:, :], ALU.mult), at)
                dve.tensor_scalar(base[:, :], base[:, :], float(TC), None, ALU.add)
                link(dve.tensor_reduce(cmin[:, :], posv[:, :], AX_X, ALU.min), at)
                link(dve.tensor_tensor(fmin[:, :], fmin[:, :], cmin[:, :], ALU.min), at)
                dve.sem_inc(s_dec, 1)

            def math(b, i, at):
                c = 2 * i + b
                o, g, before = O[b], G[b], O[1 - b]
                for h in range(2):
                    dve.wait_ge(s_g[b][h], 16 * (TC // 2) * (i + 1))
                if first_of(b, i):
                    dve.wait_ge(s_ad, 16)
                if not first_of(b, i, 2):
                    dve.wait_ge(s_st[b], 16 * i)
                G2 = GDIM + GHEADS

                def by_head(t):
                    return t.rearrange("p t h -> p h t")

                bc = [P, GHEADS, TC]
                dve.tensor_copy(o[:, 0, :], before[:, TC, :])
                link(dve.tensor_tensor(adm[:, :, :], by_head(g[:, :, G2:]), start[b][:, :].unsqueeze(1).to_broadcast(bc), ALU.mult), at)
                for h in range(GHEADS):
                    init = ad0[:, G2 + h:G2 + h + 1] if first_of(b, i) else adp[1 - b][:, h, TC - 1:TC]
                    last = dve.tensor_tensor_scan(adp[b][:, h, :], keep[b][:, :], adm[:, h, :], init, ALU.mult, ALU.add)
                link(last, at)
                link(dve.tensor_tensor(e[:, :, :], by_head(g[:, :, GDIM:G2]), adp[b][:, :, :], ALU.add), at)
                link(dve.scalar_tensor_tensor(out=e[:, :, :], in0=e[:, :, :], scalar=0.2, in1=e[:, :, :], op0=ALU.mult, op1=ALU.max), at)
                for h in range(GHEADS):
                    last = dve.tensor_tensor_scan(o[:, 1:, h], neg[b][:, :], e[:, h, :], o[:, 0, h:h + 1], ALU.add, ALU.max)
                link(last, at)
                dve.tensor_tensor(w[:, 1], e[:, :, :], by_head(o[:, 1:, MCH:LCH]), ALU.subtract)
                link(dve.tensor_tensor(w[:, 0], by_head(o[:, 0:TC, MCH:LCH]), by_head(o[:, 1:, MCH:LCH]), ALU.subtract), at)
                dve.scalar_tensor_tensor(out=w[:, 0], in0=w[:, 0], scalar=0.0, in1=neg[b][:, :].unsqueeze(1).to_broadcast(bc),
                                         op0=ALU.min, op1=ALU.add).then_inc(s_lo, 1)
                dve.wait_ge(s_ex, c + 1)
                for h in range(GHEADS):
                    dve.tensor_tensor_scan(o[:, 1:, LCH + h], w[:, 0, h, :], w[:, 1, h, :], o[:, 0, LCH + h:LCH + h + 1], ALU.mult, ALU.add)
                link(dve.tensor_tensor(msg[:, :, :, :], g[:, :, 0:GDIM].rearrange("p t (h e) -> p h e t", h=GHEADS),
                                       w[:, 1].unsqueeze(2).to_broadcast([P, GHEADS, GDIM // GHEADS, TC]), ALU.mult), at)
                for h in range(GHEADS):
                    for x in range(GDIM // GHEADS):
                        k = ACH + h * (GDIM // GHEADS) + x
                        last = dve.tensor_tensor_scan(o[:, 1:, k], w[:, 0, h, :], msg[:, h, x, :], o[:, 0, k:k + 1], ALU.mult, ALU.add)
                last.then_inc(s_math, 1)
                dve.wait_ge(s_math, c + 1)

            def counts(b, i, at):
                c = 2 * i + b
                dve.wait_ge(s_dx[b], 16 * i + 16)
                dve.tensor_scalar(dlo[:, 0, :], dx[b][:, :], P - 1, None, ALU.bitwise_and)
                link(dve.tensor_scalar(dlo[:, 1, :], dx[b][:, :], 7, None, ALU.logical_shift_right), at)
                link(dve.tensor_copy(dlf[:, :, :], dlo[:, :, :]), at)
                dve.sem_inc(s_dxr, 1)
                for t in range(HC):
                    if t >= RING or not first_of(b, i):
                        dve.wait_ge(s_ohp, c * HC + t - RING + 1)
                    dve.tensor_scalar(ohl[:, t % RING, :], iob[:, 0:P], dlf[:, 0, t:t + 1], None, ALU.is_equal)
                    dve.tensor_scalar(ohh[:, t % RING, :], iob[:, :], dlf[:, 1, t:t + 1], None, ALU.is_equal).then_inc(s_oh, 1)
                dve.wait_ge(s_ohp, (c + 1) * HC)
                dve.tensor_tensor(hist[:, :], cbank[b][:, 0:HI], hist[:, :], ALU.add).then_inc(s_hs, 1)

            def outputs(b, i):
                c = 2 * i + b
                if not first_of(b, i, 2):
                    dve.wait_ge(s_yst[b], 16 * i)
                for t in range(UTILES):
                    dve.wait_ge(s_l2, c * UTILES + t + 1)
                    dve.tensor_tensor(yo[b][:, t, :], ybank[t % 2][:, :], b2r[:, :], ALU.add).then_inc(s_y, 1)

            D, M = 6, 7
            C = 2
            decode(0, 0, 0)

            def body(b, i):
                c = 2 * i + b
                at = D + c * (D + M + C)
                if not last_of(b, i):
                    decode(1 - b, i + b, at)
                    assert st.k == D
                    at = at + D
                elif True:
                    at = at + 0
                st.k = 0
                math(b, i, at)
                assert st.k == M, st.k
                st.k = 0
                counts(b, i, at + M)
                assert st.k == C
                outputs(b, i)

            chunks(dve, body)


EH = GDIM // GHEADS
VCH = NROW - LCH


def ends(nc, state_rows, last_state, first_start, hist_in, end_rows):
    with ExitStack() as ctx:
        def sb(name, shape, dt=F32):
            return ctx.enter_context(nc.sbuf_tensor("ends_" + name, shape, dt))

        def sem(name):
            return ctx.enter_context(nc.semaphore("ends_" + name))

        hist = sb("hist", [P, HI])
        tri = sb("tri", [P, P])
        ones = sb("ones", [P, P])
        ident = sb("ident", [P, P])
        rowi = sb("rowi", [P, HI], I32)
        rowf = sb("rowf", [P, HI])
        pref = sb("pref", [P, HI])
        tot = sb("tot", [P, HI])
        zero = sb("zero", [P, HI])
        endi = sb("endi", [P, HI], I32)
        ls = sb("ls", [P, NROW])
        fs = sb("fs", [P, 1])
        nost = sb("nost", [P, 1])
        x3 = sb("x3", [P, 3, VCH])
        xt = sb("xt", [VCH, 3, P])
        M = sb("M", [VCH, P + 1])
        V = sb("V", [VCH, P + 1])
        w2 = sb("w2", [VCH, 2, P])
        car = sb("car", [P, 2, VCH])
        old = sb("old", [P, NROW])
        new = sb("new", [P, NROW])
        mm = sb("mm", [P, VCH])
        mo = sb("mo", [P, VCH])
        wc = sb("wc", [P, 2, VCH])
        has = sb("has", [P, 1])
        ri = sb("ri", [P, 2], I32)
        rf = sb("rf", [P, 4])
        bp = ctx.enter_context(nc.psum_tensor("bp", [P, BANK], F32))
        bt = ctx.enter_context(nc.psum_tensor("bt", [P, BANK], F32))
        bx = ctx.enter_context(nc.psum_tensor("bx", [P, BANK], F32))
        bc = ctx.enter_context(nc.psum_tensor("bc", [P, BANK], F32))

        s_in = sem("s_in")
        s_c = sem("s_c")
        s_step = sem("s_step")
        s_pe = sem("s_pe")
        s_act = sem("s_act")
        s_z = sem("s_z")
        s_old = sem("s_old")
        s_new = sem("s_new")
        s_out = sem("s_out")
        mark = {}
        block = ctx.enter_context(nc.Block())

        @block.vector
        def _(dve):
            n = [0]

            def link(ins, name=None):
                ins.then_inc(s_step, 1)
                n[0] += 1
                dve.wait_ge(s_step, n[0])
                mark[name] = n[0]

            dve.wait_ge(s_c, 7)
            dve.wait_ge(s_in, 48)
            dve.tensor_scalar(nost[:, :], fs[:, :], 0.0, LOW, ALU.is_lt, ALU.mult)
            dve.tensor_copy(x3[:, 0, 0:GHEADS], ls[:, MCH:LCH])
            dve.tensor_copy(x3[:, 0, GHEADS:].rearrange("p (h e) -> p h e", e=EH), ls[:, MCH:LCH].unsqueeze(2).to_broadcast([P, GHEADS, EH]))
            link(dve.tensor_copy(x3[:, 1, :], ls[:, LCH:]))
            link(dve.tensor_copy(x3[:, 2, :], nost[:, :].to_broadcast([P, VCH])), "x3")
            dve.tensor_scalar(rf[:, 0:1], fs[:, :], float(ROWS - 1), None, ALU.add)
            link(dve.tensor_scalar(has[:, :], fs[:, :], float(-ROWS), None, ALU.is_gt))
            dve.tensor_copy(rf[:, 1:2], ri[:, 0:1])
            link(dve.tensor_copy(rf[:, 2:3], ri[:, 1:2]))
            link(dve.tensor_tensor(rf[:, 0:1], rf[:, 0:1], rf[:, 1:2], ALU.add))
            link(dve.tensor_tensor(rf[:, 0:1], rf[:, 0:1], rf[:, 2:3], ALU.subtract))
            link(dve.scalar_tensor_tensor(out=rf[:, 3:4], in0=rf[:, 0:1], scalar=has[:, 0:1], in1=rf[:, 2:3], op0=ALU.mult, op1=ALU.add))
            link(dve.tensor_copy(ri[:, 0:1], rf[:, 3:4]), "row")
            dve.wait_ge(s_pe, 1)
            link(dve.tensor_copy(tot[:, :], bt[:, 0:HI]))
            link(dve.tensor_tensor_scan(pref[:, :], tot[:, :], zero[:, :], 0.0, ALU.add, ALU.add))
            link(dve.tensor_tensor(pref[:, :], pref[:, :], tot[:, :], ALU.subtract))
            link(dve.tensor_tensor(pref[:, :], bp[:, 0:HI], pref[:, :], ALU.add))
            link(dve.tensor_copy(rowf[:, :], rowi[:, :]))
            link(dve.tensor_tensor(pref[:, :], pref[:, :], rowf[:, :], ALU.add))
            link(dve.tensor_copy(endi[:, :], pref[:, :]), "ends")
            dve.wait_ge(s_pe, 2)
            link(dve.tensor_copy(xt[:, :, :], bx[0:VCH, 0:3 * P].rearrange("p (a b) -> p a b", a=3)))
            dve.memset(M[:, 0:1], LOW)
            link(dve.memset(V[:, 0:1], 0.0))
            link(dve.tensor_tensor_scan(M[:, 1:], xt[:, 2, :], xt[:, 0, :], M[:, 0:1], ALU.add, ALU.max))
            dve.tensor_tensor(w2[:, 1, :], xt[:, 0, :], M[:, 1:], ALU.subtract)
            link(dve.tensor_tensor(w2[:, 0, :], M[:, 0:P], M[:, 1:], ALU.subtract))
            link(dve.scalar_tensor_tensor(out=w2[:, 0, :], in0=w2[:, 0, :], scalar=0.0, in1=xt[:, 2, :], op0=ALU.min, op1=ALU.add), "w2")
            dve.wait_ge(s_act, 1)
            link(dve.tensor_tensor(xt[:, 1, :], xt[:, 1, :], w2[:, 1, :], ALU.mult))
            link(dve.tensor_tensor_scan(V[:, 1:], w2[:, 0, :], xt[:, 1, :], V[:, 0:1], ALU.mult, ALU.add), "V")
            dve.wait_ge(s_pe, 3)
            link(dve.tensor_copy(car[:, :, :], bc[:, 0:2 * VCH].rearrange("p (a b) -> p a b", a=2)))
            dve.wait_ge(s_old, 16)
            dve.tensor_copy(mo[:, 0:GHEADS], old[:, MCH:LCH])
            link(dve.tensor_copy(mo[:, GHEADS:].rearrange("p (h e) -> p h e", e=EH), old[:, MCH:LCH].unsqueeze(2).to_broadcast([P, GHEADS, EH])))
            link(dve.tensor_tensor(mm[:, :], mo[:, :], car[:, 0, :], ALU.max))
            dve.tensor_tensor(wc[:, 0, :], car[:, 0, :], mm[:, :], ALU.subtract)
            link(dve.tensor_tensor(wc[:, 1, :], mo[:, :], mm[:, :], ALU.subtract), "wc")
            dve.wait_ge(s_act, 2)
            dve.tensor_copy(new[:, MCH:LCH], mm[:, 0:GHEADS])
            dve.tensor_tensor(mo[:, :], wc[:, 0, :], car[:, 1, :], ALU.mult)
            link(dve.tensor_tensor(new[:, LCH:], wc[:, 1, :], old[:, LCH:], ALU.mult))
            link(dve.tensor_tensor(new[:, LCH:], new[:, LCH:], mo[:, :], ALU.add), "new")

        @block.sync
        def _(sp):
            sp.dma_start(hist[:, :], hist_in).then_inc(s_in, 16)
            sp.dma_start(ls[:, :], last_state).then_inc(s_in, 16)
            sp.dma_start(fs[:, :], first_start).then_inc(s_in, 16)
            sp.wait_ge(s_c, 7)
            sp.dma_start(state_rows[SORTED:SORTED + P, :], zero[:, 0:NROW]).then_inc(s_z, 16)
            sp.wait_ge(s_step, mark["ends"])
            sp.dma_start(end_rows, endi[:, :]).then_inc(s_out, 16)
            sp.wait_ge(s_out, 16)
            sp.wait_ge(s_new, 16)

        @block.gpsimd
        def _(pool):
            pool.memset(ones[:, :], 1.0).then_inc(s_c, 1)
            pool.memset(zero[:, :], 0.0).then_inc(s_c, 1)
            pool.wait_ge(s_c, 2)
            pool.affine_select(out=tri[:, :], in_=ones[:, :], compare_op=ALU.is_ge, fill=0.0, base=0,
                               pattern=[[1, P]], channel_multiplier=-1).then_inc(s_c, 1)
            pool.affine_select(out=ident[:, :], in_=zero[:, 0:P], compare_op=ALU.not_equal, fill=1.0, base=0,
                               pattern=[[-1, P]], channel_multiplier=1).then_inc(s_c, 1)
            pool.iota(rowi[:, :], pattern=[[P, HI]], base=0, channel_multiplier=1).then_inc(s_c, 1)
            pool.iota(ri[:, 0:1], pattern=[[0, 1]], base=0, channel_multiplier=ROWS).then_inc(s_c, 1)
            pool.iota(ri[:, 1:2], pattern=[[0, 1]], base=SORTED, channel_multiplier=1).then_inc(s_c, 1)
            pool.wait_ge(s_step, mark["row"])
            pool.wait_ge(s_z, 16)
            pool.indirect_dma_start(old[:, :], None, state_rows, bass.IndirectOffsetOnAxis(ap=ri[:, 0:1], axis=0)).then_inc(s_old, 16)
            pool.wait_ge(s_step, mark["new"])
            pool.indirect_dma_start(state_rows, bass.IndirectOffsetOnAxis(ap=ri[:, 0:1], axis=0), new[:, :], None).then_inc(s_new, 16)

        @block.tensor
        def _(pe):
            pe.wait_ge(s_c, 7)
            pe.wait_ge(s_in, 48)
            pe.matmul(bp[:, 0:HI], tri[:, :], hist[:, :], start=True, stop=True)
            pe.matmul(bt[:, 0:HI], ones[:, :], hist[:, :], start=True, stop=True).then_inc(s_pe, 1)
            pe.wait_ge(s_step, mark["x3"])
            for k in range(3):
                last = pe.transpose(bx[0:VCH, k * P:(k + 1) * P], x3[:, k, :], ident[:, :])
            last.then_inc(s_pe, 1)
            pe.wait_ge(s_step, mark["V"])
            pe.transpose(bc[:, 0:VCH], M[:, 0:P], ident[0:VCH, 0:VCH])
            pe.transpose(bc[:, VCH:2 * VCH], V[:, 0:P], ident[0:VCH, 0:VCH]).then_inc(s_pe, 1)

        @block.scalar
        def _(act):
            act.wait_ge(s_step, mark["w2"])
            act.activation(w2[:, :, :], w2[:, :, :], ACT.Exp).then_inc(s_act, 1)
            act.wait_ge(s_step, mark["wc"])
            act.activation(wc[:, :, :], wc[:, :, :], ACT.Exp).then_inc(s_act, 1)


def combine(nc, state_rows, end_rows, expert_out, x2_rows, b_gat, gamma, beta, out):
    with ExitStack() as ctx:
        def sb(name, shape, dt=F32):
            return ctx.enter_context(nc.sbuf_tensor("comb_" + name, shape, dt))

        def sem(name):
            return ctx.enter_context(nc.semaphore("comb_" + name))

        par = sb("par", [P, 3, GDIM])
        endt = sb("endt", [P, HI], I32)
        ix = [sb(f"ix{b}", [P, TILES], I32) for b in range(2)]
        srow = [sb(f"srow{b}", [P, TILES, NROW]) for b in range(2)]
        ye = [sb(f"ye{b}", [P, TILES, EXPERTS * P]) for b in range(2)]
        xr = [sb(f"xr{b}", [P, TILES, P]) for b in range(2)]
        res = [sb(f"res{b}", [P, TILES, P]) for b in range(2)]
        l = sb("l", [P, TILES, GHEADS])
        agg = sb("agg", [P, TILES, GHEADS, EH])
        sq = sb("sq", [P, TILES, GDIM])
        mu = sb("mu", [P, TILES])
        var = sb("var", [P, TILES])
        nh = sb("nh", [P, TILES])
        ny = sb("ny", [P, TILES])
        nt = sb("nt", [P, TILES])
        sc = sb("sc", [P, TILES, EXPERTS])
        beat = sb("beat", [P, TILES])
        rank = sb("rank", [P, TILES, EXPERTS])
        mx = sb("mx", [P, TILES])
        gate = [sb(f"gate{b}", [P, TILES, EXPERTS]) for b in range(2)]
        s_in = sem("s_in")
        s_ix = sem("s_ix")
        s_passed = sem("s_passed")
        s_rows = [sem("s_rows0"), sem("s_rows1")]
        s_ye = [sem("s_ye0"), sem("s_ye1")]
        s_used = sem("s_used")
        s_step = sem("s_step")
        s_lo = sem("s_lo")
        s_ex = sem("s_ex")
        s_res = sem("s_res")
        s_st = [sem("s_st0"), sem("s_st1")]

        def images(eng, body):
            for b in range(2):
                body(b, 0)
            with eng.Fori(1, IMAGES // 2 - 1) as i:
                for b in range(2):
                    body(b, i)
            for b in range(2):
                body(b, IMAGES // 2 - 1)

        def first_of(b, i, n=1):
            return isinstance(i, int) and 2 * i + b < n

        block = ctx.enter_context(nc.Block())

        @block.sync
        def _(sp):
            sp.dma_start(endt[:, :], end_rows).then_inc(s_in, 16)
            for k, v in enumerate((b_gat, gamma, beta)):
                sp.dma_start(par[:, k, :], v.rearrange("(o e) -> o e", o=1).to_broadcast([P, GDIM])).then_inc(s_in, 16)

            def body(b, i):
                m = 2 * i + b
                if not first_of(b, i, 2):
                    sp.wait_ge(s_res, m - 1)
                sp.dma_start(ye[b][:, :, :], expert_out[m].rearrange("h (t p) d -> p (h t) d", p=P)).then_inc(s_ye[b], 16)
                sp.dma_start(xr[b][:, :, :], x2_rows[m].rearrange("(j p) d -> p j d", p=P)).then_inc(s_ye[b], 16)

            images(sp, body)

        @block.scalar
        def _(act):
            def body(b, i):
                m = 2 * i + b
                act.wait_ge(s_lo, m + 1)
                act.activation(gate[b][:, :, :], gate[b][:, :, :], ACT.Exp).then_inc(s_ex, 1)
                act.wait_ge(s_res, m + 1)
                act.dma_start(out[m].rearrange("(j p) d -> p j d", p=P), res[b][:, :, :]).then_inc(s_st[b], 16)

            images(act, body)
            for b in range(2):
                act.wait_ge(s_st[b], 16 * IMAGES // 2)

        @block.gpsimd
        def _(pool):
            def body(b, i):
                m = 2 * i + b
                pool.wait_ge(s_ix, m + 1)
                pool.sem_inc(s_passed, 1)
                for t in range(TILES):
                    pool.indirect_dma_start(srow[b][:, t, :], None, state_rows,
                                            bass.IndirectOffsetOnAxis(ap=ix[b][:, t:t + 1], axis=0)).then_inc(s_rows[b], 16)

            images(pool, body)

        @block.vector
        def _(dve):
            dve.wait_ge(s_in, 64)
            k = [0]
            per = [None]

            def indices(b, i):
                m = 2 * i + b
                if not first_of(b, i, 2):
                    dve.wait_ge(s_rows[b], 16 * TILES * i)
                dve.tensor_copy(ix[b][:, :], endt[:, bass.ds(m * TILES, TILES)]).then_inc(s_ix, 1)

            indices(0, 0)

            def body(b, i):
                m = 2 * i + b
                k[0] = 0

                def link(ins):
                    ins.then_inc(s_step, 1)
                    k[0] += 1
                    dve.wait_ge(s_step, (m * per[0] if per[0] else 0) + k[0])

                if not (isinstance(i, int) and m == IMAGES - 1):
                    indices(1 - b, i + b)
                dve.wait_ge(s_rows[b], 16 * TILES * (i + 1))
                s = srow[b]
                bc4 = [P, TILES, GHEADS, EH]
                flat = agg[:, :, :, :].rearrange("p t h e -> p t (h e)")

                def by_token(t, n=GDIM):
                    return t.unsqueeze(2).to_broadcast([P, TILES, n])

                def by_feature(x):
                    return par[:, x, :].unsqueeze(1).to_broadcast([P, TILES, GDIM])

                link(dve.tensor_scalar(l[:, :, :], s[:, :, LCH:ACH], 1e-16, None, ALU.add))
                link(dve.reciprocal(l[:, :, :], l[:, :, :]))
                link(dve.tensor_tensor(agg[:, :, :, :], s[:, :, ACH:].rearrange("p t (h e) -> p t h e", e=EH),
                                       l[:, :, :].unsqueeze(3).to_broadcast(bc4), ALU.mult))
                link(dve.tensor_tensor(flat, flat, by_feature(0), ALU.add))
                link(dve.tensor_reduce(mu[:, :], flat, AX_X, ALU.add))
                link(dve.tensor_scalar(mu[:, :], mu[:, :], 1.0 / GDIM, None, ALU.mult))
                link(dve.tensor_tensor(flat, flat, by_token(mu[:, :]), ALU.subtract))
                link(dve.tensor_tensor(sq[:, :, :], flat, flat, ALU.mult))
                link(dve.tensor_reduce(var[:, :], sq[:, :, :], AX_X, ALU.add))
                link(dve.tensor_scalar(var[:, :], var[:, :], 1.0 / GDIM, EPS_TOKEN, ALU.mult, ALU.add))
                link(dve.tensor_scalar(nh[:, :].bitcast(I32), var[:, :].bitcast(I32), 1, None, ALU.logical_shift_right))
                link(dve.tensor_scalar(ny[:, :].bitcast(I32), nh[:, :].bitcast(I32), -1.0, float(0x5F3759DF), ALU.mult, ALU.add))
                for _ in range(4):
                    link(dve.tensor_tensor(nt[:, :], ny[:, :], ny[:, :], ALU.mult))
                    link(dve.scalar_tensor_tensor(out=nh[:, :], in0=nt[:, :], scalar=-0.5, in1=var[:, :], op0=ALU.mult, op1=ALU.mult))
                    link(dve.scalar_tensor_tensor(out=ny[:, :], in0=nh[:, :], scalar=1.5, in1=ny[:, :], op0=ALU.add, op1=ALU.mult))
                link(dve.tensor_tensor(flat, flat, by_token(ny[:, :]), ALU.mult))
                link(dve.tensor_tensor(flat, flat, by_feature(1), ALU.mult))
                link(dve.tensor_tensor(flat, flat, by_feature(2), ALU.add))
                link(dve.tensor_reduce(sc[:, :, :], agg[:, :, :, :].rearrange("p t h e -> p t e h"), AX_X, ALU.add))
                link(dve.tensor_scalar(sc[:, :, :], sc[:, :, :], 1.0 / GHEADS, None, ALU.mult))
                dve.memset(rank[:, :, :], 0.0)
                link(dve.tensor_reduce(mx[:, :], sc[:, :, :], AX_X, ALU.max))
                for u in range(EXPERTS):
                    for v in range(u + 1, EXPERTS):
                        link(dve.tensor_tensor(beat[:, :], sc[:, :, u], sc[:, :, v], ALU.is_ge))
                        dve.tensor_tensor(rank[:, :, v], rank[:, :, v], beat[:, :], ALU.add)
                        link(dve.scalar_tensor_tensor(out=rank[:, :, u], in0=rank[:, :, u], scalar=1.0, in1=beat[:, :],
                                                      op0=ALU.add, op1=ALU.subtract))
                g = gate[b]
                link(dve.tensor_scalar(rank[:, :, :], rank[:, :, :], 2.0, None, ALU.is_lt))
                dve.tensor_tensor(g[:, :, :], sc[:, :, :], by_token(mx[:, :], EXPERTS), ALU.subtract).then_inc(s_lo, 1)
                dve.wait_ge(s_ex, m + 1)
                link(dve.tensor_tensor(g[:, :, :], g[:, :, :], rank[:, :, :], ALU.mult))
                link(dve.tensor_reduce(mx[:, :], g[:, :, :], AX_X, ALU.add))
                link(dve.reciprocal(mx[:, :], mx[:, :]))
                link(dve.tensor_tensor(g[:, :, :], g[:, :, :], by_token(mx[:, :], EXPERTS), ALU.mult))
                dve.wait_ge(s_ye[b], 32 * i + 32)
                if not first_of(b, i, 2):
                    dve.wait_ge(s_st[b], 16 * i)
                for x in range(EXPERTS):
                    for t in range(TILES):
                        before = xr[b][:, t, :] if x == 0 else res[b][:, t, :]
                        last = dve.scalar_tensor_tensor(out=res[b][:, t, :], in0=ye[b][:, t, x * P:(x + 1) * P],
                                                        scalar=g[:, t, x:x + 1], in1=before, op0=ALU.mult, op1=ALU.add)
                    if x < EXPERTS - 1:
                        link(last)
                last.then_inc(s_res, 1)
                if per[0] is None:
                    per[0] = k[0]
                assert per[0] == k[0]

            images(dve, body)


def window_attention_graph_experts(nc, x, w_qkv, b_qkv, w_o, b_o, w_gat, att_src, att_dst, b_gat,
                                   gamma, beta, w1, b1, w2, b2, edge_index, out):
    def dram(name, shape, dt=F32):
        return nc.dram_tensor(name, shape, dt, kind="Internal").ap()

    sorted_keys = dram("sorted_keys", (1 + SORTED, 1))
    x2_rows = dram("x2_rows", (IMAGES, TOKENS, P))
    tokens_t = dram("tokens_t", (IMAGES, P, TOKENS))
    node_rows = dram("node_rows", (IMAGES, TOKENS, NROW))
    state_rows = dram("state_rows", (SORTED + P, NROW))
    expert_out = dram("expert_out", (IMAGES, TOKENS // UNIT, UNIT, EXPERTS * P))
    last_state = dram("last_state", (P, NROW))
    first_start = dram("first_start", (P, 1))
    counts = dram("counts", (P, HI))
    end_rows = dram("end_rows", (P, HI), I32)

    sort_edges(nc, edge_index, sorted_keys)
    attention(nc, x, w_qkv, b_qkv, w_o, b_o, w_gat, att_src, att_dst, x2_rows, tokens_t, node_rows)
    edges(nc, sorted_keys.bitcast(I32), node_rows.rearrange("i t d -> (i t) d"), edge_index, tokens_t,
          w1, b1, w2, b2, state_rows, expert_out, last_state, first_start, counts)
    ends(nc, state_rows, last_state, first_start, counts, end_rows)
    combine(nc, state_rows, end_rows, expert_out, x2_rows, b_gat, gamma, beta, out)


INPUTS = ["x", "L0_conv_w_qkv", "L0_conv_b_qkv", "L0_conv_w_o", "L0_conv_b_o", "L0_ffn_W_gat", "L0_ffn_att_src",
          "L0_ffn_att_dst", "L0_ffn_b_gat", "L0_ffn_ln_gamma", "L0_ffn_ln_beta", "L0_ffn_W1", "L0_ffn_b1",
          "L0_ffn_W2", "L0_ffn_b2", "L0_ffn_edge_index"]


def kernel(**inputs):
    import numpy as np
    import concourse.bacc as bacc
    from concourse.bass_utils import run_bass_kernel_spmd

    nc = bacc.Bacc("TRN2", target_bir_lowering=False, num_devices=1)
    arrays, args = {}, []
    for name in INPUTS:
        a = np.ascontiguousarray(inputs[name])
        arrays["in_" + name] = a
        args.append(nc.dram_tensor("in_" + name, a.shape, mybir.dt.from_np(a.dtype), kind="ExternalInput").ap())
    out = nc.dram_tensor("out", (IMAGES, TOKENS, P), F32, kind="ExternalOutput").ap()
    window_attention_graph_experts(nc, *args, out)
    result = run_bass_kernel_spmd(nc, [arrays], core_ids=[0])
    return result.results[0]["out"].reshape(inputs["x"].shape)
```

```python
from contextlib import ExitStack
import concourse.bass as bass
from concourse import mybir

F32 = mybir.dt.float32
I32 = mybir.dt.int32
BF16 = mybir.dt.bfloat16
ALU = mybir.AluOpType
ACT = mybir.ActivationFunctionType
AX_X = mybir.AxisListType.X

P = 128
BANK = 512
NODES = 32768
EDGES = 524288
NODE_BITS = 15
SORTED = EDGES + NODES
ROWS = SORTED // P
KEY_BASE = (1 << 23) >> NODE_BITS


def pair_views(tile, bit, direction):
    if direction is None:
        v = tile.rearrange("p (o b i) -> p o b i", b=2, i=1 << bit)
        return [(v[:, :, 0, :], v[:, :, 1, :])]
    hi, lo = max(bit, direction), min(bit, direction)
    v = tile.rearrange("p (o h m l i) -> p o h m l i", h=2, m=1 << (hi - lo - 1), l=2, i=1 << lo)
    if bit > direction:
        return [(v[:, :, 0, :, d, :], v[:, :, 1, :, d, :]) for d in range(2)]
    return [(v[:, :, d, :, 0, :], v[:, :, d, :, 1, :]) for d in range(2)]


COLS = EDGES // P
COL_BITS = COLS.bit_length() - 1
PART_BITS = P.bit_length() - 1
LEVELS = COL_BITS + PART_BITS
LOOP_ROWS = NODES // COLS
LOOPS_AT = P - 32
UCOLS = NODES // P
UPPER_BITS = UCOLS.bit_length() - 1



def row_network():
    network = []
    for level in range(1, COL_BITS + 1):
        if level == COL_BITS:
            network.append(("negate", 0))
        for j in range(level - 1, -1, -1):
            network.append(("compare", j, level if level < COL_BITS else None, False))
    return network


def turned_merge(top, kept, first_negated, direction, sign):
    network = [("turn", None)]
    for j in range(top - 1, PART_BITS - 1, -1):
        network.append(("compare", j - kept if j >= kept else j, direction, first_negated and j == top - 1))
    network.append(("turn", sign))
    network += [("compare", j, None, False) for j in range(PART_BITS - 1, -1, -1)]
    return network


def partition_network():
    network = []
    for level in range(COL_BITS + 1, LEVELS + 1):
        side = level - COL_BITS if level < LEVELS else None
        network += turned_merge(level, COL_BITS, True, side, side)
    network.append(("join",))
    network += turned_merge(LEVELS, COL_BITS, False, None, None)
    network.append(("upper",))
    return network + turned_merge(UPPER_BITS + PART_BITS, UPPER_BITS, False, None, None)


def row_sort(dve, keys, sign, s_dst, s_src, s_piece):
    PIECE = COLS // 4
    done = 0
    at = 1

    def pieces(width):
        return [(c, c + width) for c in range(0, COLS, width)]

    dst, src = keys[0][:, :].bitcast(I32), keys[1][:, :].bitcast(I32)
    dve.wait_ge(s_dst, 16)
    dve.wait_ge(s_src, 16)
    for lo, hi in pieces(PIECE):
        dve.tensor_tensor(src[:, lo:hi], dst[:, lo:hi], src[:, lo:hi], ALU.bitwise_xor).then_inc(s_piece, 1)
        done += 1
        yield
    dve.wait_ge(s_piece, done)
    for lo, hi in pieces(2 * PIECE):
        dve.tensor_scalar(dst[:, lo:hi], dst[:, lo:hi], float(KEY_BASE), None, ALU.add).then_inc(s_piece, 1)
        done += 1
        yield
    dve.wait_ge(s_piece, done)
    for lo, hi in pieces(PIECE):
        dve.scalar_tensor_tensor(out=src[:, lo:hi], in0=dst[:, lo:hi], scalar=NODE_BITS, in1=src[:, lo:hi],
                                 op0=ALU.logical_shift_left, op1=ALU.bitwise_or).then_inc(s_piece, 1)
        done += 1
        yield
    for step in row_network():
        a, b = keys[at], keys[1 - at]
        dve.wait_ge(s_piece, done)
        if step[0] == "negate":
            for lo, hi in pieces(2 * PIECE):
                dve.tensor_scalar(b[:, lo:hi], a[:, lo:hi], sign[:, step[1]:step[1] + 1], None, ALU.mult).then_inc(s_piece, 1)
                done += 1
                yield
        else:
            _, bit, direction, _ = step
            views = list(zip(pair_views(a[:, :], bit, direction), pair_views(b[:, :], bit, direction)))
            if direction is None and bit < COL_BITS - 1:
                views = [view for lo, hi in pieces(2 * PIECE)
                         for view in zip(pair_views(a[:, lo:hi], bit, None), pair_views(b[:, lo:hi], bit, None))]
            for down, ((first, second), (x, y)) in enumerate(views):
                ops = (ALU.max, ALU.min) if down and direction is not None else (ALU.min, ALU.max)
                for out, op in ((x, ops[0]), (y, ops[1])):
                    dve.tensor_tensor(out, first, second, op).then_inc(s_piece, 1)
                    done += 1
                    yield
        at = 1 - at


ROW_SORTED = (1 + len(row_network())) % 2


def sort_partitions(nc, keys, sign, sorted_keys):
    network = partition_network()

    with ExitStack() as ctx:
        def sb(name, shape, dt):
            return ctx.enter_context(nc.sbuf_tensor("sort_" + name, shape, dt))

        def sem(name):
            return ctx.enter_context(nc.semaphore("sort_" + name))

        loops = sb("loops", [P, COLS], F32)
        umax = sb("umax", [P, COLS], F32)
        upper = [sb(f"upper{i}", [P, UCOLS], F32) for i in range(2)]
        ident = sb("ident", [P, P], F32)
        zero = sb("zero", [1, 1], F32)
        banks = [ctx.enter_context(nc.psum_tensor(f"sort_bank{i}", [P, BANK], F32)) for i in range(8)]

        s_const = sem("s_const")
        s_loops = sem("s_loops")
        s_stage = sem("s_stage")
        s_turn = sem("s_turn")
        s_out_a = sem("s_out_a")
        s_out_v = sem("s_out_v")
        s_upout = sem("s_upout")
        s_upin = sem("s_upin")
        s_store = sem("s_store")

        class Walk:

            def __init__(self):
                self.stage = 0
                self.tiles, self.at = keys, ROW_SORTED
                self.turned = self.out_a = self.out_v = 0
                self.final_stage = self.join_stage = None

            def src(self):
                return self.tiles[self.at]

            def dst(self):
                return self.tiles[1 - self.at]

            def halves(self, i):
                n = self.src().shape[1]
                near = network[max(i - 1, 0)][0] == "turn" or network[min(i + 1, len(network) - 1)][0] == "turn"
                return [(0, n // 2), (n // 2, n)] if near and self.tiles is keys else [(0, n)]

            def banks(self):
                n = self.src().shape[1]
                width = min(BANK, n)
                return [(b, b * width, width, b in (1, 3)) for b in range(n // width)]

        def walk():
            w = Walk()
            for i, step in enumerate(network):
                if step[0] == "upper":
                    w.main, w.main_stage = w.src(), w.stage
                    w.tiles, w.at = upper, 0
                yield i, step, w
                if step[0] in ("compare", "negate"):
                    w.stage += len(w.halves(i))
                    w.at = 1 - w.at
                elif step[0] == "join":
                    w.stage += 2
                    w.join_stage = w.stage
                    w.at = 1 - w.at
                elif step[0] == "turn":
                    for _, _, _, by_vector in w.banks():
                        w.turned += 1
                        w.out_v += by_vector
                        w.out_a += not by_vector
                    w.at = 1 - w.at

        for _, _, end in walk():
            pass

        block = ctx.enter_context(nc.Block())

        @block.sync
        def _(sp):
            sp.wait_ge(s_const, 3)
            sp.dma_start(sorted_keys[0:1, :], zero[:, :]).then_inc(s_store, 16)
            sp.wait_ge(s_stage, end.join_stage)
            sp.dma_start(sorted_keys[1 + EDGES:1 + SORTED, :].rearrange("(p c) o -> p (c o)", c=COLS),
                         umax[P - LOOP_ROWS:P, :]).then_inc(s_upout, 16)
            sp.wait_ge(s_upout, 16)
            sp.dma_start(upper[0][:, :], sorted_keys[1 + EDGES:1 + SORTED, :].rearrange("(p c) o -> p (c o)", c=UCOLS)
                         ).then_inc(s_upin, 16)
            sp.wait_ge(s_stage, end.main_stage)
            sp.dma_start(sorted_keys[1:1 + EDGES, :].rearrange("(p c) o -> p (c o)", c=COLS), end.main[:, :]).then_inc(s_store, 16)
            sp.wait_ge(s_stage, end.stage)
            sp.dma_start(sorted_keys[1 + EDGES:1 + SORTED, :].rearrange("(p c) o -> p (c o)", c=UCOLS),
                         end.src()[:, :]).then_inc(s_store, 16)
            sp.wait_ge(s_store, 48)

        @block.gpsimd
        def _(pool):
            pool.memset(ident[:, :], 0.0).then_inc(s_const, 1)
            pool.memset(zero[:, :], 0.0).then_inc(s_const, 1)
            pool.wait_ge(s_const, 2)
            pool.affine_select(out=ident[:, :], in_=ident[:, :], compare_op=ALU.not_equal, fill=1.0,
                               base=0, pattern=[[-1, P]], channel_multiplier=1).then_inc(s_const, 1)
            pool.wait_ge(s_const, 3)
            pool.iota(loops[LOOPS_AT:P, :].bitcast(I32), pattern=[[-1, COLS]], base=EDGES - 1 - LOOPS_AT * COLS,
                      channel_multiplier=-COLS).then_inc(s_const, 1)

        @block.tensor
        def _(pe):
            pe.wait_ge(s_const, 4)
            for i, step, w in walk():
                if step[0] == "upper":
                    pe.wait_ge(s_upin, 16)
                if step[0] != "turn":
                    continue
                if w.turned:
                    pe.wait_ge(s_out_a, w.out_a)
                    pe.wait_ge(s_out_v, w.out_v)
                pieces = len(w.banks())
                halved = i > 0 and network[i - 1][0] in ("compare", "negate") and w.tiles is keys
                for b, first, width, _ in w.banks():
                    if b == 0 and w.stage:
                        pe.wait_ge(s_stage, w.stage - halved)
                    if b == pieces // 2 and halved:
                        pe.wait_ge(s_stage, w.stage)
                    for c in range(0, width, P):
                        last = pe.transpose(banks[b][:, c:c + P], w.src()[:, first + c:first + c + P], ident[:, :])
                    last.then_inc(s_turn, 1)

        @block.scalar
        def _(act):
            for i, step, w in walk():
                if step[0] != "turn":
                    continue
                for b, first, width, by_vector in w.banks():
                    if by_vector:
                        continue
                    act.wait_ge(s_turn, w.turned + b + 1)
                    out = w.dst()[:, first:first + width]
                    if step[1] is None:
                        act.activation(out, banks[b][:, 0:width], ACT.Copy).then_inc(s_out_a, 1)
                    else:
                        act.activation(out, banks[b][:, 0:width], ACT.Copy, scale=sign[:, step[1]:step[1] + 1]).then_inc(s_out_a, 1)

        @block.vector
        def _(dve):
            done = [0]

            def step_done(ins):
                ins.then_inc(s_stage, 1)
                done[0] += 1
                dve.wait_ge(s_stage, done[0])

            dve.wait_ge(s_const, 4)
            rows = loops[LOOPS_AT:P, :].bitcast(I32)
            dve.tensor_scalar(rows, rows, float(NODES), float(KEY_BASE), ALU.min, ALU.add).then_inc(s_loops, 1)
            dve.wait_ge(s_loops, 1)
            dve.tensor_scalar(rows, rows, NODE_BITS, None, ALU.logical_shift_left).then_inc(s_loops, 1)
            dve.wait_ge(s_loops, 2)
            for i, step, w in walk():
                src, dst = w.src(), w.dst()
                if step[0] in ("compare", "negate"):
                    for h, (lo, hi) in enumerate(w.halves(i)):
                        if i > 0 and network[i - 1][0] == "turn":
                            all_banks = hi == src.shape[1]
                            dve.wait_ge(s_out_a, w.out_a - (0 if all_banks else 4))
                            dve.wait_ge(s_out_v, w.out_v)
                        if step[0] == "negate":
                            step_done(dve.tensor_scalar(dst[:, lo:hi], src[:, lo:hi], sign[:, step[1]:step[1] + 1], None, ALU.mult))
                            continue
                        _, bit, direction, negated = step
                        views = zip(pair_views(src[:, lo:hi], bit, direction), pair_views(dst[:, lo:hi], bit, direction))
                        for down, ((a, b), (x, y)) in enumerate(views):
                            ops = (ALU.max, ALU.min) if down else (ALU.min, ALU.max)
                            for out, op in ((x, ops[0]), (y, ops[1])):
                                if negated:
                                    last = dve.scalar_tensor_tensor(out=out, in0=b, scalar=-1.0, in1=a, op0=ALU.mult, op1=op)
                                else:
                                    last = dve.tensor_tensor(out, a, b, op)
                        step_done(last)
                elif step[0] == "turn":
                    for b, first, width, by_vector in w.banks():
                        if by_vector:
                            dve.wait_ge(s_turn, w.turned + b + 1)
                            out = dst[:, first:first + width]
                            if step[1] is None:
                                dve.tensor_copy(out, banks[b][:, 0:width]).then_inc(s_out_v, 1)
                            else:
                                dve.tensor_scalar(out, banks[b][:, 0:width], sign[:, step[1]:step[1] + 1], None, ALU.mult
                                                  ).then_inc(s_out_v, 1)
                elif step[0] == "join":
                    lo = LOOPS_AT
                    dve.tensor_copy(dst[0:lo, :], src[0:lo, :])
                    step_done(dve.tensor_tensor(dst[lo:P, :], src[lo:P, :], loops[lo:P, :], ALU.min))
                    step_done(dve.tensor_tensor(umax[lo:P, :], src[lo:P, :], loops[lo:P, :], ALU.max))
                elif step[0] == "upper":
                    dve.wait_ge(s_upin, 16)


IMAGES = 32
SIDE = 32
TOKENS = SIDE * SIDE
TILES = TOKENS // P
WIN = 8
WTOK = WIN * WIN
WGRID = SIDE // WIN
SHIFT = 4
PAD = SIDE + SHIFT
HEADS = 8
HDIM = P // HEADS
PAIRS = WGRID * WGRID // 2
GROUPS = HEADS // 2
VW = 2 * (HDIM + 1)
GHEADS = 4
GDIM = 16
NROW = GDIM + 2 * GHEADS
RING_S = 4
RING_K = 4
NEG = -1.0e9
SCALE = HDIM ** -0.5
EPS_LN = 1e-6
EPS_TOKEN = 1e-5


class Chain:

    def __init__(self, sem):
        self.sem, self.per, self.k = sem, None, 0

    def start(self, m):
        self.m, self.k = m, 0

    def value(self):
        return self.k if self.per is None else self.m * self.per + self.k

    def link(self, eng, ins):
        ins.then_inc(self.sem, 1)
        self.k += 1
        eng.wait_ge(self.sem, self.value())

    def end(self):
        if self.per is None:
            self.per = self.k
        assert self.per == self.k


def attention(nc, x, w_qkv, b_qkv, w_o, b_o, w_gat, att_src, att_dst, edge_index, keys, sign,
              x2_out, tnT_out, node_rows):
    with ExitStack() as ctx:
        def sb(name, shape, dt=F32):
            return ctx.enter_context(nc.sbuf_tensor("attn_" + name, shape, dt))

        def ps(name):
            return ctx.enter_context(nc.psum_tensor("attn_" + name, [P, BANK], F32))

        def sem(name):
            return ctx.enter_context(nc.semaphore("attn_" + name))

        wqkv = sb("wqkv", [P, 3 * P])
        wo = sb("wo", [P, P])
        wgat = sb("wgat", [P, GDIM])
        bias = sb("bias", [P, 4])
        attv = sb("attv", [P, 2, GDIM])
        ident = sb("ident", [P, P])
        ones = sb("ones", [P, 1])
        hm = sb("hm", [P, HEADS])
        hmi = sb("hmi", [P, 2, HEADS], I32)
        mi = sb("mi", [P, 4, WTOK], I32)
        signi = sb("signi", [P, PART_BITS], I32)
        masks = sb("masks", [P, 3, WTOK])
        eps = sb("eps", [P, 2])
        xin = sb("xin", [P, TILES, P])
        xn = sb("xn", [P, TILES, P])
        xres = sb("xres", [P, TILES, P])
        x2 = sb("x2", [P, TILES, P])
        tn = sb("tn", [P, TILES, P])
        tnT = sb("tnT", [P, TOKENS])
        hrow = sb("hrow", [P, TILES, NROW])
        hprod = sb("hprod", [P, 2, TILES, GDIM])
        wmaj = sb("wmaj", [P, WGRID, WGRID, WTOK])
        ypad = sb("ypad", [P, PAD, PAD])
        ywin = sb("ywin", [P, WGRID, WGRID, WTOK])
        zmaj = sb("zmaj", [P, SIDE, SIDE])
        zrow = sb("zrow", [P, SIDE, SIDE])
        qT = [[sb(f"qT{s}{h}", [P, BANK]) for h in range(2)] for s in range(2)]
        kT = [[sb(f"kT{s}{h}", [P, BANK]) for h in range(2)] for s in range(2)]
        km = [sb(f"km{s}", [P, RING_K, 2, HEADS, WTOK]) for s in range(2)]
        vx = [sb(f"vx{s}", [P, 2 * PAIRS, GROUPS, VW]) for s in range(2)]
        S = [[sb(f"S{s}{i}", [P, HEADS, WTOK]) for i in range(RING_S)] for s in range(2)]
        mx = [sb(f"mx{s}", [P, PAIRS, HEADS]) for s in range(2)]
        pT = [[sb(f"pT{s}{i}", [P, GROUPS, P]) for i in range(2)] for s in range(2)]
        att = [sb(f"att{h}", [P, PAIRS // 2, 2, P]) for h in range(2)]
        rsum = [sb(f"rsum{i}", [P, 2, HEADS]) for i in range(2)]
        attT = [sb(f"attT{s}", [P, BANK]) for s in range(2)]
        st6 = [sb(f"st6{i}", [P, TILES, 6]) for i in range(2)]
        mv = [sb(f"mv{i}", [P, TILES, 2]) for i in range(2)]
        nw = [sb(f"nw{i}", [P, 4, TILES]) for i in range(2)]

        score_bank = [ps("score0"), ps("score1")]
        turn_bank = [ps("turn0"), ps("turn1")]
        out_bank = [ps("out0"), ps("out1")]
        misc = [ps("misc0"), ps("misc1")]

        s_w = sem("s_w")
        s_c = sem("s_c")
        s_cv = sem("s_cv")
        s_full = [sem("s_full0"), sem("s_full1")]
        s_free = [sem("s_free0"), sem("s_free1")]
        s_xin = sem("s_xin")
        s_xres = sem("s_xres")
        s_xn = sem("s_xn")
        s_km = [sem("s_kma"), sem("s_kmb")]
        s_sc = [sem("s_sca"), sem("s_scb")]
        s_mx = [sem("s_mxa"), sem("s_mxb")]
        s_sub = [sem("s_suba"), sem("s_subb")]
        s_exp = [sem("s_expa"), sem("s_expb")]
        s_pt = [sem("s_pta"), sem("s_ptb")]
        s_pte = [sem("s_ptea"), sem("s_pteb")]
        s_pv = sem("s_pv")
        s_nrm = sem("s_nrm")
        s_y = [sem("s_y"), sem("s_z")]
        s_roll = [sem("s_yroll"), sem("s_zroll")]
        YC, ZC = 2 + WGRID, 4
        s_dst = sem("s_dst")
        s_src = sem("s_src")
        s_piece = sem("s_piece")
        s_x2 = sem("s_x2")
        s_tn = sem("s_tn")
        s_ct = sem("s_ct")
        s_h = sem("s_h")
        s_x2st = sem("s_x2st")
        s_tst = sem("s_tst")
        s_hst = sem("s_hst")
        s_passed = sem("s_passed")
        ch_f = Chain(sem("ch_f"))
        ch_c = Chain(sem("ch_c"))
        ch_h = Chain(sem("ch_h"))
        ch_m = Chain(sem("ch_m"))
        s_recip = sem("s_recip")

        TASKS = [("Ap0", 1), ("Bp0", 3), ("Av0", 0), ("Bv0", 2),
                 ("Aq1", 0), ("Ak1", 0), ("Bq1", 2), ("Bk1", 2),
                 ("CT0", 4), ("CT1", 4),
                 ("Av1", 0), ("Bv1", 2), ("Ao1", 1), ("Bo1", 3),
                 ("Ap1", 1), ("Bp1", 3), ("CH0", 4),
                 ("FT0", -1), ("FT1", -1),
                 ("Aq0", -1), ("Ak0", -1), ("CZ0", 3), ("CZ1", 3),
                 ("Bq0", 1), ("Bk0", 1), ("Ao0", 0), ("Bo0", 2)]
        NAMES = [name for name, _ in TASKS]
        LAG = dict(TASKS)
        LAG.update(A=0, B=2)
        LAST_LAG = 4
        SLOT_TASKS = [4, 4, 2, 4, 3, 2, 4, 4]

        def slot_tasks(j):
            first = sum(SLOT_TASKS[:j])
            return NAMES[first:first + SLOT_TASKS[j]]

        def active(what, n):
            return not isinstance(n, int) or 0 <= n - LAG[what] < IMAGES

        def bank_of(task):
            return NAMES.index(task) % 2

        def count(n, task):
            at = NAMES.index(task)
            total = 0
            for i, (t, lag) in enumerate(TASKS):
                if bank_of(t) != bank_of(task):
                    continue
                m = n - lag
                if isinstance(n, int):
                    total = total + min(max(m, 0), IMAGES) + (i <= at and 0 <= m < IMAGES)
                else:
                    total = total + m + int(i <= at)
            return total

        def done(task, m):
            return count(m + LAG[task], task)

        def later(n, j, slots):
            return (n, j - slots) if j >= slots else (n - 1, j - slots + PAIRS)

        def streams(n):
            return [s for s in "AB" if active(s, n)]

        def first(m):
            return isinstance(m, int) and m == 0

        def steps(eng, body):
            for n in range(-1, LAST_LAG + 1):
                body(n)
            with eng.Fori(LAST_LAG + 1, IMAGES - 1) as n:
                body(n)
            for n in range(IMAGES - 1, IMAGES + LAST_LAG):
                body(n)

        STREAM = {"A": 0, "B": 1}
        block = ctx.enter_context(nc.Block())

        @block.sync
        def _(sp):
            sp.dma_start(wqkv[:, :], w_qkv).then_inc(s_w, 16)
            sp.dma_start(wo[:, :], w_o).then_inc(s_w, 16)
            sp.dma_start(wgat[:, :], w_gat).then_inc(s_w, 16)
            sp.dma_start(bias[:, 0:3], b_qkv.rearrange("(c p) -> p c", p=P),
                         allow_slow_non_contiguous=True).then_inc(s_w, 16)
            sp.dma_start(bias[:, 3:4], b_o.rearrange("(p o) -> p o", o=1), allow_slow_non_contiguous=True).then_inc(s_w, 16)
            sp.dma_start(attv[:, 0, :], att_src.rearrange("(o h) e -> o (h e)", o=1).to_broadcast([P, GDIM])).then_inc(s_w, 16)
            sp.dma_start(attv[:, 1, :], att_dst.rearrange("(o h) e -> o (h e)", o=1).to_broadcast([P, GDIM])).then_inc(s_w, 16)

            def body(n):
                if active("FT0", n):
                    m = n + 1
                    if not first(m):
                        sp.wait_ge(s_xn, m)
                    sp.dma_start(xin[:, :, :], x[m].rearrange("(j r) c d -> (r c) j d", j=TILES)).then_inc(s_xin, 16)
                if active("CZ0", n):
                    m = n - LAG["CZ0"]
                    if not first(m):
                        sp.wait_ge(s_x2, m)
                    sp.dma_start(xres[:, :, :], x[m].rearrange("(j r) c d -> (r c) j d", j=TILES)).then_inc(s_xres, 16)
                if active("CT0", n):
                    m = n - LAG["CT0"]
                    sp.wait_ge(s_ct, 2 * m + 2)
                    sp.dma_start(tnT_out[m], tnT[:, :]).then_inc(s_tst, 16)
                    sp.wait_ge(s_h, m + 1)
                    sp.dma_start(node_rows[m].rearrange("(j p) d -> p j d", p=P), hrow[:, :, :]).then_inc(s_hst, 16)
                if active("CZ0", n):
                    m = n - LAG["CZ0"]
                    sp.wait_ge(s_x2, m + 1)
                    sp.dma_start(x2_out[m].rearrange("(j p) d -> p j d", p=P), x2[:, :, :]).then_inc(s_x2st, 16)

            sp.dma_start(keys[0][:, :].bitcast(I32), edge_index[1, :].rearrange("(p c) -> p c", p=P)).then_inc(s_dst, 16)
            sp.dma_start(keys[1][:, :].bitcast(I32), edge_index[0, :].rearrange("(p c) -> p c", p=P)).then_inc(s_src, 16)

            steps(sp, body)
            sp.wait_ge(s_x2st, 16 * IMAGES)
            sp.wait_ge(s_tst, 16 * IMAGES)
            sp.wait_ge(s_hst, 16 * IMAGES)

        @block.gpsimd
        def _(pool):
            pool.memset(ident[:, :], 0.0).then_inc(s_c, 1)
            pool.memset(eps[:, 0:1], EPS_LN)
            pool.memset(eps[:, 1:2], EPS_TOKEN)
            for s in range(2):
                v = vx[s][:, :, :, :].rearrange("p w g c -> p (w g c)")
                pool.memset(v, 0.0).then_inc(s_c, 1)
            pool.wait_ge(s_c, 3)
            pool.affine_select(out=ident[:, :], in_=ident[:, :], compare_op=ALU.not_equal, fill=1.0,
                               base=0, pattern=[[-1, P]], channel_multiplier=1).then_inc(s_c, 1)
            for s in range(2):
                pool.wait_ge(s_c, 4 + 2 * s)
                pool.memset(vx[s][0:WTOK, :, :, HDIM:HDIM + 1], 1.0).then_inc(s_c, 1)
                pool.wait_ge(s_c, 5 + 2 * s)
                pool.memset(vx[s][WTOK:P, :, :, VW - 1:VW], 1.0).then_inc(s_c, 1)
            pool.wait_ge(s_c, 8)
            pool.iota(hmi[:, 0, :], pattern=[[0, HEADS]], base=0, channel_multiplier=1).then_inc(s_c, 1)
            pool.wait_ge(s_c, 9)
            pool.iota(hmi[:, 1, :], pattern=[[1, HEADS]], base=0, channel_multiplier=0).then_inc(s_c, 1)
            pool.wait_ge(s_c, 10)
            pool.iota(mi[:, 0, :], pattern=[[0, WTOK]], base=0, channel_multiplier=1).then_inc(s_c, 1)
            pool.wait_ge(s_c, 11)
            pool.iota(mi[:, 1, :], pattern=[[1, WTOK]], base=0, channel_multiplier=0).then_inc(s_c, 1)
            pool.wait_ge(s_c, 12)
            pool.iota(signi[:, :], pattern=[[0, PART_BITS]], base=0, channel_multiplier=1).then_inc(s_c, 1)

            def masked_keys(s, n, lag, j):
                st, h, m = STREAM[s], j // 4, n - lag
                b = bank_of(f"{s}k{h}")
                if j % 4 == 0:
                    pool.wait_ge(s_free[b], done(f"{s}k{h}", m))
                if j >= RING_K or not first(m):
                    pool.wait_ge(s_sc[st], m * PAIRS + j - RING_K + 1)
                w = (2 * j) % PAIRS
                k = kT[st][h][:, w * WTOK:(w + 2) * WTOK].rearrange("p (w k) -> p w k", w=2)
                shape = [P, 2, HEADS, WTOK]
                pool.tensor_tensor(km[st][:, j % RING_K], k.unsqueeze(2).to_broadcast(shape),
                                   hm[:, :].unsqueeze(1).unsqueeze(3).to_broadcast(shape), ALU.mult).then_inc(s_km[st], 1)

            def wrap(m):
                pool.wait_ge(s_y[0], 2 * m + 2)
                if not first(m):
                    pool.wait_ge(s_full[bank_of("Bv1")], done("Bv1", m - 1))
                pool.sem_inc(s_passed, 1)
                pool.tensor_copy(ypad[:, 0:SIDE, SIDE:PAD], ypad[:, 0:SIDE, 0:SHIFT]).then_inc(s_roll[0], 1)
                pool.wait_ge(s_roll[0], YC * m + 1)
                pool.sem_inc(s_passed, 1)
                pool.tensor_copy(ypad[:, SIDE:PAD, :], ypad[:, 0:SHIFT, :]).then_inc(s_roll[0], 1)
                pool.wait_ge(s_roll[0], YC * m + 2)
                pool.sem_inc(s_passed, 1)
                for a in range(WGRID):
                    r = a * WIN + SHIFT
                    pool.tensor_copy(ywin[:, a, :, :].rearrange("p b (h c) -> p h b c", h=WIN),
                                     ypad[:, r:r + WIN, SHIFT:PAD].rearrange("p h (b c) -> p h b c", b=WGRID)
                                     ).then_inc(s_roll[0], 1)

            def unroll(m):
                pool.wait_ge(s_y[1], 2 * m + 2)
                if not first(m):
                    pool.wait_ge(s_full[bank_of("CZ1")], done("CZ1", m - 1))
                pool.sem_inc(s_passed, 1)
                e = SIDE - SHIFT
                for to, of in (((SHIFT, SIDE), (0, e)), ((0, SHIFT), (e, SIDE))):
                    for to2, of2 in (((SHIFT, SIDE), (0, e)), ((0, SHIFT), (e, SIDE))):
                        pool.tensor_copy(zrow[:, to[0]:to[1], to2[0]:to2[1]], zmaj[:, of[0]:of[1], of2[0]:of2[1]]
                                         ).then_inc(s_roll[1], 1)

            pool.wait_ge(s_cv, 2)

            MASKING = [[3], [4], [5], [6], [7], [], [8, 9], [10]]

            def body(n):
                for j in range(PAIRS):
                    for pair in MASKING[j]:
                        for s in "AB":
                            lag = LAG[s] - pair // PAIRS
                            if not isinstance(n, int) or 0 <= n - lag < IMAGES:
                                masked_keys(s, n, lag, pair % PAIRS)
                    if j == 4 and active("Ap1", n):
                        wrap(n - LAG["Ap1"])
                    if j == 5 and active("Bp1", n):
                        unroll(n - LAG["Bp1"])

            steps(pool, body)

        @block.scalar
        def _(act):
            act.wait_ge(s_w, 16 * 7)
            act.wait_ge(s_c, 8)

            def take(n, task):
                b = bank_of(task)
                act.wait_ge(s_full[b], count(n, task))
                return misc[b]

            def queries_or_keys(n, task):
                st, h, m = STREAM[task[0]], int(task[2]), n - LAG[task]
                t = take(n, task)
                if not first(m):
                    used = s_sc if task[1] == "q" else s_km
                    act.wait_ge(used[st], (m - 1) * PAIRS + 4 * h + 4)
                dst, col = ((qT, 0), (kT, 1))[task[1] == "k"]
                act.activation(dst[st][h][:, :], t[:, :], ACT.Identity, bias=bias[:, col:col + 1]).then_inc(s_free[bank_of(task)], 1)

            def values(n, task):
                st, h = STREAM[task[0]], int(task[2])
                t = take(n, task)
                if not first(n - LAG[task]):
                    act.wait_ge(s_pv, (n - 1) * PAIRS + 4 * h + 4)
                w = slice(PAIRS * h, PAIRS * h + PAIRS)
                src = t[:, :].rearrange("p (w g d) -> p w g d", w=PAIRS, g=GROUPS)
                act.activation(vx[st][0:WTOK, w, :, 0:HDIM], src[0:WTOK], ACT.Copy)
                act.activation(vx[st][WTOK:P, w, :, HDIM + 1:VW - 1], src[WTOK:P], ACT.Copy).then_inc(s_free[bank_of(task)], 1)

            def attended(n, task):
                act.activation(attT[STREAM[task[0]]][:, :], take(n, task)[:, :], ACT.Identity, bias=bias[:, 2:3]
                               ).then_inc(s_free[bank_of(task)], 1)

            def projected(n, task):
                st, h, m, b = STREAM[task[0]], int(task[2]), n - LAG[task], bank_of(task)
                src_bank, dst = take(n, task), (ypad, zmaj)[st]
                if not first(m):
                    act.wait_ge(s_roll[st], (YC, ZC)[st] * m)
                for i in range(2):
                    r = (2 * h + i) * WIN
                    src = src_bank[:, i * 256:(i + 1) * 256].rearrange("p (b h c) -> p h b c", b=WGRID, h=WIN)
                    out = dst[:, r:r + WIN, 0:SIDE].rearrange("p h (b c) -> p h b c", b=WGRID)
                    last = act.activation(out, src, ACT.Identity, bias=bias[:, 3:4])
                last.then_inc(s_free[b], 1)
                act.wait_ge(s_free[b], count(n, task))
                act.sem_inc(s_y[st], 1)

            def tokens(n, task):
                m, i, b = n - LAG[task], int(task[2]), bank_of(task)
                t = take(n, task)
                if i == 0 and not first(m):
                    act.wait_ge(s_tst, 16 * m)
                act.activation(tnT[:, i * BANK:(i + 1) * BANK], t[:, :], ACT.Copy).then_inc(s_free[b], 1)
                act.wait_ge(s_free[b], count(n, task))
                act.sem_inc(s_ct, 1)

            def image(n, task):
                i, b = int(task[2]), bank_of(task)
                t = take(n, task)
                for a in range(2):
                    src = t[:, a * 256:(a + 1) * 256].rearrange("p (h b c) -> p h b c", h=WIN, b=WGRID)
                    out = wmaj[:, 2 * i + a, :, :].rearrange("p b (h c) -> p h b c", h=WIN)
                    last = act.activation(out, src, ACT.Copy)
                last.then_inc(s_free[b], 1)

            KINDS = {"Aq": queries_or_keys, "Ak": queries_or_keys, "Bq": queries_or_keys, "Bk": queries_or_keys,
                     "Av": values, "Ao": attended, "Bo": attended, "Ap": projected, "Bp": projected,
                     "CT": tokens, "FT": image}

            def body(n):
                for j in range(PAIRS):
                    k, i = later(n, j, 1)
                    for s in streams(k):
                        st, m = STREAM[s], k - LAG[s]
                        act.wait_ge(s_sub[st], m * PAIRS + i + 1)
                        t = S[st][i % RING_S][:, :, :]
                        act.activation(t, t, ACT.Exp, scale=SCALE).then_inc(s_exp[st], 1)
                    k, i = later(n, j, 2)
                    for s in streams(k):
                        st, m = STREAM[s], k - LAG[s]
                        act.wait_ge(s_pt[st], m * PAIRS + i + 1)
                        if not (isinstance(k, int) and first(m) and i < 2):
                            act.wait_ge(s_pv, k * PAIRS + i - 1)
                        act.activation(pT[st][i % 2][:, :, :], turn_bank[st][:, :].rearrange("p (g q) -> p g q", g=GROUPS),
                                       ACT.Copy).then_inc(s_pte[st], 1)
                    for task in slot_tasks(j):
                        if task[:2] in KINDS and active(task, n):
                            KINDS[task[:2]](n, task)

            steps(act, body)

        @block.tensor
        def _(pe):
            pe.wait_ge(s_w, 16 * 7)
            pe.wait_ge(s_c, 8)

            def take(n, task):
                b = bank_of(task)
                before = count(n, task) - 1
                if not (isinstance(before, int) and before == 0):
                    pe.wait_ge(s_free[b], before)
                return misc[b]

            SOURCE = {"A": wmaj, "B": ywin}

            def wait_source(n, task):
                m = n - LAG[task]
                if task[0] == "A":
                    for i in range(2):
                        pe.wait_ge(s_free[bank_of(f"FT{i}")], done(f"FT{i}", m))
                else:
                    pe.wait_ge(s_roll[0], YC * m + YC)

            def queries_or_keys(n, task):
                h = int(task[2])
                t = take(n, task)
                if h == 0:
                    wait_source(n, task)
                w = wqkv[:, 0:P] if task[1] == "q" else wqkv[:, P:2 * P]
                return pe.matmul(t[:, :], w, SOURCE[task[0]][:, 2 * h:2 * h + 2].rearrange("p a b k -> p (a b k)"), start=True, stop=True)

            def values(n, task):
                h = int(task[2])
                t = take(n, task)
                wv = wqkv[:, 2 * P:3 * P].rearrange("p (g e d) -> p e g d", g=GROUPS, e=2)
                for i in range(PAIRS):
                    a, b = divmod(PAIRS * h + i, WGRID)
                    for e in range(2):
                        last = pe.matmul(t[e * WTOK:(e + 1) * WTOK, i * WTOK:(i + 1) * WTOK], SOURCE[task[0]][:, a, b, :], wv[:, e],
                                         start=True, stop=True)
                return last

            def attended(n, task):
                st, h = STREAM[task[0]], int(task[2])
                t = take(n, task)
                k = n - LAG[task] + LAG[task[0]]
                pe.wait_ge(s_nrm, k * PAIRS + 4 * h + 4)
                for i in range(PAIRS // 2):
                    last = pe.transpose(t[:, i * P:(i + 1) * P], att[h][:, i, st, :], ident[:, :])
                return last

            def projected(n, task):
                t = take(n, task)
                turned = f"{task[0]}o{task[2]}"
                pe.wait_ge(s_free[bank_of(turned)], done(turned, n - LAG[task]))
                return pe.matmul(t[:, :], wo[:, :], attT[STREAM[task[0]]][:, :], start=True, stop=True)

            def result(n, task):
                i = int(task[2])
                t = take(n, task)
                pe.wait_ge(s_roll[1], ZC * (n - LAG[task]) + ZC)
                for k in range(4):
                    r = (4 * i + k) * (P // SIDE)
                    last = pe.transpose(t[:, k * P:(k + 1) * P], zrow[:, r:r + P // SIDE, :].rearrange("p h w -> p (h w)"), ident[:, :])
                return last

            def tiles(n, task):
                i = int(task[2])
                t, src, ready = take(n, task), (tn, xn)[task[0] == "F"], (s_tn, s_xn)[task[0] == "F"]
                pe.wait_ge(ready, n - LAG[task] + 1)
                for k in range(4):
                    last = pe.transpose(t[:, k * P:(k + 1) * P], src[:, 4 * i + k, :], ident[:, :])
                return last

            def graph_features(n, task):
                t = take(n, task)
                pe.wait_ge(s_ct, 2 * (n - LAG[task]) + 2)
                for k in range(TILES):
                    last = pe.matmul(t[:, k * GDIM:(k + 1) * GDIM], tnT[:, k * P:(k + 1) * P], wgat[:, :], start=True, stop=True)
                return last

            KINDS = {"Aq": queries_or_keys, "Ak": queries_or_keys, "Bq": queries_or_keys, "Bk": queries_or_keys,
                     "Av": values, "Bv": values, "Ao": attended, "Bo": attended, "Ap": projected, "Bp": projected,
                     "CT": tiles, "FT": tiles, "CZ": result, "CH": graph_features}

            def scores(n, s, j):
                st, m, h = STREAM[s], n - LAG[s], j // 4
                if j % 4 == 0:
                    pe.wait_ge(s_free[bank_of(f"{s}q{h}")], done(f"{s}q{h}", m))
                pe.wait_ge(s_km[st], m * PAIRS + j + 1)
                if j > 0 or not first(m):
                    pe.wait_ge(s_sub[st], m * PAIRS + j)
                for e in range(2):
                    w = (2 * j + e) % PAIRS
                    last = pe.matmul(score_bank[st][e * WTOK:(e + 1) * WTOK, :], qT[st][h][:, w * WTOK:(w + 1) * WTOK],
                                     km[st][:, j % RING_K, e].rearrange("p h k -> p (h k)"), start=True, stop=True)
                last.then_inc(s_sc[st], 1)

            def turn(n, s, j):
                st, m = STREAM[s], n - LAG[s]
                pe.wait_ge(s_exp[st], m * PAIRS + j + 1)
                if j > 0 or not first(m):
                    pe.wait_ge(s_pte[st], m * PAIRS + j)
                src = S[st][j % RING_S][:, :, :].rearrange("p h k -> p (h k)")
                for g in range(GROUPS):
                    last = pe.transpose(turn_bank[st][:, g * P:(g + 1) * P], src[:, g * P:(g + 1) * P], ident[:, :])
                last.then_inc(s_pt[st], 1)

            def weigh(n, j):
                if j >= 2 or not first(n):
                    pe.wait_ge(s_nrm, n * PAIRS + j - 1)
                for s in streams(n):
                    st, m = STREAM[s], n - LAG[s]
                    if j % 4 == 0:
                        v = f"{s}v{j // 4}"
                        pe.wait_ge(s_free[bank_of(v)], done(v, m))
                    pe.wait_ge(s_pte[st], m * PAIRS + j + 1)
                    for g in range(GROUPS):
                        for e in range(2):
                            c = st * GROUPS * VW + g * VW
                            last = pe.matmul(out_bank[j % 2][e * WTOK:(e + 1) * WTOK, c:c + VW],
                                             pT[st][j % 2][:, g, e * WTOK:(e + 1) * WTOK], vx[st][:, 2 * j + e, g, :],
                                             start=True, stop=True)
                last.then_inc(s_pv, 1)

            def body(n):
                for j in range(PAIRS):
                    for s in streams(n):
                        scores(n, s, j)
                    k, i = later(n, j, 2)
                    for s in streams(k):
                        turn(k, s, i)
                    k, i = later(n, j, 3)
                    if streams(k):
                        weigh(k, i)
                    for task in slot_tasks(j):
                        if active(task, n):
                            KINDS[task[:2]](n, task).then_inc(s_full[bank_of(task)], 1)

            steps(pe, body)

        @block.vector
        def _(dve):
            dve.wait_ge(s_c, 13)
            cv = [0]

            def link(ins):
                ins.then_inc(s_cv, 1)
                cv[0] += 1
                dve.wait_ge(s_cv, cv[0])

            link(dve.tensor_scalar(hmi[:, 0, :], hmi[:, 0, :], 4, None, ALU.logical_shift_right))
            link(dve.tensor_tensor(hm[:, :], hmi[:, 0, :], hmi[:, 1, :], ALU.is_equal))
            link(dve.tensor_tensor(mi[:, 1, :], mi[:, 0, :], mi[:, 1, :], ALU.bitwise_xor))
            link(dve.tensor_scalar(mi[:, 2, :], mi[:, 1, :], 5, 1, ALU.logical_shift_right, ALU.bitwise_and))
            link(dve.tensor_scalar(mi[:, 3, :], mi[:, 1, :], 2, 1, ALU.logical_shift_right, ALU.bitwise_and))
            link(dve.tensor_scalar(mi[:, 0, :], mi[:, 0, :], 6, None, ALU.logical_shift_right))
            link(dve.tensor_tensor(mi[:, 3, :], mi[:, 3, :], mi[:, 0, :], ALU.mult))
            link(dve.tensor_tensor(mi[:, 0, :], mi[:, 2, :], mi[:, 3, :], ALU.max))
            big = NEG / SCALE
            link(dve.tensor_scalar(masks[:, 0, :], mi[:, 3, :], big, None, ALU.mult))
            link(dve.tensor_scalar(masks[:, 1, :], mi[:, 2, :], big, None, ALU.mult))
            link(dve.tensor_scalar(masks[:, 2, :], mi[:, 0, :], big, None, ALU.mult))
            for b in range(PART_BITS):
                last = dve.tensor_scalar(signi[:, b:b + 1], signi[:, b:b + 1], b, 1, ALU.logical_shift_right, ALU.bitwise_and)
            link(last)
            link(dve.tensor_scalar(sign[:, :], signi[:, :], -2.0, 1.0, ALU.mult, ALU.add))
            sorting = row_sort(dve, keys, sign, s_dst, s_src, s_piece)
            SORTING = [1, 2, 1, 0, 2, 2, 0, 0]

            def mask_of(j):
                row, right = j // 2 == WGRID - 1, j % 2 == 1
                return {(False, False): None, (False, True): 0, (True, False): 1, (True, True): 2}[(row, right)]

            def moments(ch, k, src, eps_col):
                for j in range(TILES):
                    last = dve.bn_stats(st6[k][:, j, :], src[:, j, :])
                ch.link(dve, last)
                for j in range(TILES):
                    last = dve.bn_aggr(mv[k][:, j, :], st6[k][:, j, :])
                ch.link(dve, last)
                v, h, y, t = (nw[k][:, i, :] for i in range(4))
                ch.link(dve, dve.tensor_scalar(v, mv[k][:, :, 1], eps[:, eps_col:eps_col + 1], None, ALU.add))
                ch.link(dve, dve.tensor_scalar(h.bitcast(I32), v.bitcast(I32), 1, None, ALU.logical_shift_right))
                ch.link(dve, dve.tensor_scalar(y.bitcast(I32), h.bitcast(I32), -1.0, float(0x5F3759DF), ALU.mult, ALU.add))
                for _ in range(4):
                    ch.link(dve, dve.tensor_tensor(t, y, y, ALU.mult))
                    ch.link(dve, dve.scalar_tensor_tensor(out=h, in0=t, scalar=-0.5, in1=v, op0=ALU.mult, op1=ALU.mult))
                    ch.link(dve, dve.scalar_tensor_tensor(out=y, in0=h, scalar=1.5, in1=y, op0=ALU.add, op1=ALU.mult))

            def normalise(k, src, dst):
                y = nw[k][:, 2, :]
                for j in range(TILES):
                    last = dve.tensor_scalar(dst[:, j, :], src[:, j, :], mv[k][:, j, 0:1], y[:, j:j + 1],
                                             ALU.subtract, ALU.mult)
                return last

            def head(n):
                m = n + 1
                ch_f.start(m)
                dve.wait_ge(s_xin, 16 * m + 16)
                moments(ch_f, 0, xin, 0)
                ch_f.end()

            def head_normalised(n):
                if not first(n + 1):
                    for i in range(2):
                        dve.wait_ge(s_full[bank_of(f"FT{i}")], done(f"FT{i}", n))
                normalise(0, xin, xn).then_inc(s_xn, 1)

            def residual(n):
                m = n - LAG["CZ0"]
                dve.wait_ge(s_xres, 16 * m + 16)
                if not first(m):
                    dve.wait_ge(s_x2st, 16 * m)
                for i in range(2):
                    b = bank_of(f"CZ{i}")
                    dve.wait_ge(s_full[b], count(n, f"CZ{i}"))
                    z = misc[b][:, :].rearrange("p (j d) -> p j d", d=P)
                    dve.tensor_tensor(x2[:, 4 * i:4 * i + 4, :], z, xres[:, 4 * i:4 * i + 4, :], ALU.add).then_inc(s_free[b], 1)
                for i in range(2):
                    b = bank_of(f"CZ{i}")
                    dve.wait_ge(s_free[b], count(n, f"CZ{i}"))
                dve.sem_inc(s_x2, 1)

            def tail(n):
                ch_c.start(n - LAG["CZ0"])
                moments(ch_c, 1, x2, 1)
                ch_c.end()

            def tail_normalised(n):
                m = n - LAG["CT0"]
                if not first(m):
                    dve.wait_ge(s_ct, 2 * m)
                normalise(1, x2, tn).then_inc(s_tn, 1)

            def node_row(n):
                m, b = n - LAG["CH0"], bank_of("CH0")
                ch_h.start(m)
                dve.wait_ge(s_full[b], count(n, "CH0"))
                if not first(m):
                    dve.wait_ge(s_hst, 16 * m)
                dve.tensor_copy(hrow[:, :, 0:GDIM], misc[b][:, 0:TILES * GDIM].rearrange("p (j e) -> p j e", e=GDIM)
                                ).then_inc(s_free[b], 1)
                dve.wait_ge(s_free[b], count(n, "CH0"))
                for k in range(2):
                    last = dve.tensor_tensor(hprod[:, k], hrow[:, :, 0:GDIM],
                                             attv[:, k, :].unsqueeze(1).to_broadcast([P, TILES, GDIM]), ALU.mult)
                ch_h.link(dve, last)
                for k in range(2):
                    c = GDIM + k * GHEADS
                    last = dve.tensor_reduce(hrow[:, :, c:c + GHEADS],
                                             hprod[:, k].rearrange("p j (h e) -> p j h e", h=GHEADS), AX_X, ALU.add)
                last.then_inc(s_h, 1)
                ch_h.end()

            def b_values(n, h):
                b = bank_of(f"Bv{h}")
                dve.wait_ge(s_full[b], count(n, f"Bv{h}"))
                if not first(n - LAG["B"]):
                    dve.wait_ge(s_pv, (n - 1) * PAIRS + 4 * h + 4)
                w = slice(PAIRS * h, PAIRS * h + PAIRS)
                src = misc[b][:, :].rearrange("p (w g d) -> p w g d", w=PAIRS, g=GROUPS)
                dve.tensor_copy(vx[1][0:WTOK, w, :, 0:HDIM], src[0:WTOK])
                dve.tensor_copy(vx[1][WTOK:P, w, :, HDIM + 1:VW - 1], src[WTOK:P]).then_inc(s_free[b], 1)

            def normalised_output(n, j):
                on = streams(n)
                dve.wait_ge(s_pv, n * PAIRS + j + 1)
                lo, hi = STREAM[on[0]], STREAM[on[-1]] + 1
                o = out_bank[j % 2][:, 0:2 * GROUPS * VW].rearrange("p (s h d) -> p s h d", s=2, d=HDIM + 1)[:, lo:hi]
                r = rsum[j % 2][:, lo:hi, :]
                if j % 4 == 0:
                    for s in on:
                        if not first(n - LAG[s]):
                            turned = f"{s}o{j // 4}"
                            dve.wait_ge(s_full[bank_of(turned)], done(turned, n - LAG[s] - 1))
                dve.reciprocal(r, o[:, :, :, HDIM]).then_inc(s_recip, 1)
                dve.wait_ge(s_recip, n * PAIRS + j + 1)
                dve.tensor_tensor(att[j // 4][:, j % 4, lo:hi, :].rearrange("p s (h d) -> p s h d", h=HEADS),
                                  o[:, :, :, 0:HDIM], r.unsqueeze(3).to_broadcast([P, hi - lo, HEADS, HDIM]),
                                  ALU.mult).then_inc(s_nrm, 1)

            def less_maximum(n, j):
                full = [P, HEADS, WTOK]
                src = {}
                for s in streams(n):
                    st, m = STREAM[s], n - LAG[s]
                    t = S[st][j % RING_S][:, :, :]
                    src[s] = score_bank[st][:, :].rearrange("p (h k) -> p h k", h=HEADS)
                    dve.wait_ge(s_sc[st], m * PAIRS + j + 1)
                    if j >= RING_S or not first(m):
                        dve.wait_ge(s_pt[st], m * PAIRS + j + 1 - RING_S)
                    if s == "B":
                        if j == 0:
                            ch_m.start(m)
                        if mask_of(j) is not None:
                            ch_m.link(dve, dve.tensor_tensor(t, src[s], masks[:, mask_of(j), :].unsqueeze(1).to_broadcast(full), ALU.add))
                            src[s] = t
                    dve.tensor_reduce(mx[st][:, j, :], src[s], AX_X, ALU.max).then_inc(s_mx[st], 1)
                for s in streams(n):
                    st, m = STREAM[s], n - LAG[s]
                    dve.wait_ge(s_mx[st], m * PAIRS + j + 1)
                    dve.tensor_tensor(S[st][j % RING_S][:, :, :], src[s], mx[st][:, j, :].unsqueeze(2).to_broadcast(full),
                                      ALU.subtract).then_inc(s_sub[st], 1)
                    if s == "B" and j == PAIRS - 1:
                        ch_m.end()

            def body(n):
                for j in range(PAIRS):
                    k, i = later(n, j, 4)
                    if streams(k):
                        normalised_output(k, i)
                    less_maximum(n, j)
                    for _ in range(SORTING[j]):
                        next(sorting, None)
                    if j == 0 and active("CT0", n):
                        tail_normalised(n)
                    if j in (0, 3) and active(f"Bv{min(j, 1)}", n):
                        b_values(n, min(j, 1))
                    if j == 2 and active("FT0", n):
                        head(n)
                    if j == 3 and active("FT0", n):
                        head_normalised(n)
                    if j == 4 and active("CH0", n):
                        node_row(n)
                    if j == 6 and active("CZ0", n):
                        residual(n)
                    if j == 7 and active("CZ0", n):
                        tail(n)

            for n in range(-1, IMAGES + LAST_LAG):
                body(n)
            for _ in sorting:
                pass


CHUNKS = 64
TC = ROWS // CHUNKS
HC = EDGES // P // CHUNKS
EXPERTS = 4
HIDDEN = 256
HB = HIDDEN // P
UNIT = NODES // CHUNKS
UTILES = UNIT // P
LOW = -1.0e38
HI = NODES // P
MCH, LCH, ACH = 0, GHEADS, 2 * GHEADS
RING = 8


def edges(nc, sorted_keys, node_rows, edge_index, tnT, W1, b1, W2, b2, state_rows, expert_out, last_state, first_start, hist_out):
    with ExitStack() as ctx:
        def sb(name, shape, dt=F32):
            return ctx.enter_context(nc.sbuf_tensor("edge_" + name, shape, dt))

        def ps(name):
            return ctx.enter_context(nc.psum_tensor("edge_" + name, [P, BANK], F32))

        def sem(name):
            return ctx.enter_context(nc.semaphore("edge_" + name))

        key = [sb(f"key{b}", [P, 2, TC], I32) for b in range(2)]
        dst = sb("dst", [P, 2, TC], I32)
        low = sb("low", [P, TC], I32)
        node = sb("node", [P, TC], I32)
        src = [sb(f"src{b}", [P, TC], I32) for b in range(2)]
        start = [sb(f"start{b}", [P, TC]) for b in range(2)]
        keep = [sb(f"keep{b}", [P, TC]) for b in range(2)]
        neg = [sb(f"neg{b}", [P, TC]) for b in range(2)]
        pos = sb("pos", [P, TC])
        posi = sb("posi", [P, TC], I32)
        posv = sb("posv", [P, TC])
        base = sb("base", [P, 1])
        cmin = sb("cmin", [P, 1])
        fmin = sb("fmin", [P, 1])
        G = [sb(f"G{b}", [P, TC, NROW]) for b in range(2)]
        O = [sb(f"O{b}", [P, TC + 1, NROW]) for b in range(2)]
        adm = sb("adm", [P, GHEADS, TC])
        adp = [sb(f"adp{b}", [P, GHEADS, TC]) for b in range(2)]
        ad0 = sb("ad0", [P, NROW])
        first = sb("first", [P, 1], I32)
        e = sb("e", [P, GHEADS, TC])
        w = sb("w", [P, 2, GHEADS, TC])
        msg = sb("msg", [P, GHEADS, GDIM // GHEADS, TC])
        dx = [sb(f"dx{b}", [P, HC], I32) for b in range(2)]
        dlo = sb("dlo", [P, 2, HC], I32)
        dlf = sb("dlf", [P, 2, HC])
        io = sb("io", [P, HI], I32)
        iob = sb("iob", [P, HI], BF16)
        ohl = sb("ohl", [P, RING, P], BF16)
        ohh = sb("ohh", [P, RING, HI], BF16)
        hist = sb("hist", [P, HI])
        w1 = sb("w1", [P, EXPERTS, HIDDEN])
        w2 = sb("w2", [P, EXPERTS, HB, P])
        b1c = sb("b1c", [P, EXPERTS * HB])
        b2r = sb("b2r", [P, EXPERTS * P])
        xt = [sb(f"xt{b}", [P, UNIT]) for b in range(2)]
        hid = sb("hid", [P, EXPERTS * HB, UNIT])
        yo = [sb(f"yo{b}", [P, UTILES, EXPERTS * P]) for b in range(2)]
        hbank = [ps("hbank0"), ps("hbank1")]
        ybank = [ps("ybank0"), ps("ybank1")]
        cbank = [ps("cbank0"), ps("cbank1")]

        s_w = sem("s_w")
        s_c = sem("s_c")
        s_cv = sem("s_cv")
        s_key = [sem("s_key0"), sem("s_key1")]
        s_dec = sem("s_dec")
        s_g = [[sem(f"s_g{b}{i}") for i in range(2)] for b in range(2)]
        s_ad = sem("s_ad")
        s_lo = sem("s_lo")
        s_ex = sem("s_ex")
        s_math = sem("s_math")
        s_st = [sem("s_st0"), sem("s_st1")]
        s_dx = [sem("s_dx0"), sem("s_dx1")]
        s_dxr = sem("s_dxr")
        s_oh = sem("s_oh")
        s_ohp = sem("s_ohp")
        s_hs = sem("s_hs")
        s_xt = [sem("s_xt0"), sem("s_xt1")]
        s_l1 = sem("s_l1")
        s_ge = sem("s_ge")
        s_l2 = sem("s_l2")
        s_y = sem("s_y")
        s_yst = [sem("s_yst0"), sem("s_yst1")]
        s_end = sem("s_end")
        s_passed = sem("s_passed")

        keys_prev = sorted_keys[0:SORTED, :].rearrange("(p r) o -> p (r o)", p=P)
        keys_here = sorted_keys[1:1 + SORTED, :].rearrange("(p r) o -> p (r o)", p=P)
        raw_dst = edge_index[1, :].rearrange("(p c) -> p c", p=P)
        st_rows = state_rows[0:SORTED, :].rearrange("(p r) d -> p r d", p=P)

        def chunks(eng, body):
            body(0, 0)
            body(1, 0)
            with eng.Fori(1, CHUNKS // 2 - 1) as i:
                for b in range(2):
                    body(b, i)
            for b in range(2):
                body(b, CHUNKS // 2 - 1)

        def first_of(b, i, n=1):
            return isinstance(i, int) and 2 * i + b < n

        def last_of(b, i, n=1):
            return isinstance(i, int) and 2 * i + b >= CHUNKS - n

        block = ctx.enter_context(nc.Block())

        @block.sync
        def _(sp):
            sp.dma_start(w1[:, :, :], W1.rearrange("e p f -> p e f")).then_inc(s_w, 16)
            sp.dma_start(w2[:, :, :, :].rearrange("p e h d -> p (e h) d"), W2.rearrange("e (h p) d -> p (e h) d", p=P)).then_inc(s_w, 16)
            sp.dma_start(b1c[:, :], b1.rearrange("e (h p) -> p (e h)", p=P), allow_slow_non_contiguous=True).then_inc(s_w, 16)
            sp.dma_start(b2r[:, :], b2.rearrange("(o e) d -> o (e d)", o=1).to_broadcast([P, EXPERTS * P])).then_inc(s_w, 16)

            def load_keys(b, c):
                sp.dma_start(key[b][:, 0, :], keys_prev[:, bass.ds(c * TC, TC)]).then_inc(s_key[b], 16)
                sp.dma_start(key[b][:, 1, :], keys_here[:, bass.ds(c * TC, TC)]).then_inc(s_key[b], 16)

            def load_raw(b, c):
                sp.dma_start(dx[b][:, :], raw_dst[:, bass.ds(c * HC, HC)]).then_inc(s_dx[b], 16)

            def load_x(b, i):
                sp.dma_start(xt[b][:, :], tnT[i][:, b * UNIT:(b + 1) * UNIT]).then_inc(s_xt[b], 16)

            load_keys(0, 0)
            load_keys(1, 1)
            load_raw(0, 0)
            load_x(0, 0)

            def body(b, i):
                c = 2 * i + b
                if not last_of(b, i, 2):
                    sp.wait_ge(s_dec, c + 1)
                    load_keys(b, c + 2)
                if not last_of(b, i):
                    if not first_of(b, i):
                        sp.wait_ge(s_w, 64)
                        sp.wait_ge(s_dxr, c)
                        sp.wait_ge(s_l1, c * EXPERTS * HB)
                    load_raw(1 - b, c + 1)
                    load_x(1 - b, i + b)
                sp.wait_ge(s_math, c + 1)
                sp.dma_start(st_rows[:, bass.ds(c * TC, TC), :], O[b][:, 1:, :]).then_inc(s_st[b], 16)
                sp.wait_ge(s_y, (c + 1) * UTILES)
                sp.dma_start(expert_out[i][b].rearrange("(t p) d -> p t d", p=P), yo[b][:, :, :]).then_inc(s_yst[b], 16)

            chunks(sp, body)
            sp.dma_start(last_state, O[1][:, TC, :]).then_inc(s_end, 16)
            sp.dma_start(first_start, fmin[:, :]).then_inc(s_end, 16)
            sp.wait_ge(s_hs, CHUNKS)
            sp.dma_start(hist_out, hist[:, :]).then_inc(s_end, 16)
            sp.wait_ge(s_end, 48)
            for b in range(2):
                sp.wait_ge(s_st[b], 16 * CHUNKS // 2)
                sp.wait_ge(s_yst[b], 16 * CHUNKS // 2)

        @block.gpsimd
        def _(pool):
            pool.iota(posi[:, :], pattern=[[1, TC]], base=0, channel_multiplier=0).then_inc(s_c, 1)
            pool.iota(io[:, :], pattern=[[1, HI]], base=0, channel_multiplier=0).then_inc(s_c, 1)
            pool.wait_ge(s_dec, 1)
            pool.indirect_dma_start(ad0[:, :], None, node_rows, bass.IndirectOffsetOnAxis(ap=first[:, :], axis=0)).then_inc(s_ad, 16)

            def body(b, i):
                c = 2 * i + b
                pool.wait_ge(s_dec, c + 1)
                if not first_of(b, i, 2):
                    pool.wait_ge(s_math, c - 1)
                pool.sem_inc(s_passed, 1)
                for t in range(TC):
                    pool.indirect_dma_start(G[b][:, t, :], None, node_rows,
                                            bass.IndirectOffsetOnAxis(ap=src[b][:, t:t + 1], axis=0)
                                            ).then_inc(s_g[b][2 * t // TC], 16)

            chunks(pool, body)

        @block.scalar
        def _(act):
            act.wait_ge(s_w, 64)

            def body(b, i):
                c = 2 * i + b
                for k in range(EXPERTS * HB):
                    act.wait_ge(s_l1, c * EXPERTS * HB + k + 1)
                    if k == 0 and not first_of(b, i):
                        act.wait_ge(s_l2, c * UTILES)
                    act.activation(hid[:, k, :], hbank[k % 2][:, :], ACT.Gelu, bias=b1c[:, k:k + 1]).then_inc(s_ge, 1)
                act.wait_ge(s_lo, c + 1)
                act.activation(w[:, :, :, :], w[:, :, :, :], ACT.Exp).then_inc(s_ex, 1)

            chunks(act, body)

        @block.tensor
        def _(pe):
            pe.wait_ge(s_w, 64)

            def body(b, i):
                c = 2 * i + b
                if not first_of(b, i, 2):
                    pe.wait_ge(s_hs, c - 1)
                for t in range(HC):
                    pe.wait_ge(s_oh, c * HC + t + 1)
                    pe.matmul(cbank[b][:, 0:HI], ohl[:, t % RING, :], ohh[:, t % RING, :],
                              start=(t == 0), stop=(t == HC - 1)).then_inc(s_ohp, 1)
                pe.wait_ge(s_xt[b], 16 * i + 16)
                for k in range(EXPERTS * HB):
                    if k >= 2 or not first_of(b, i):
                        pe.wait_ge(s_ge, c * EXPERTS * HB + k - 1)
                    pe.matmul(hbank[k % 2][:, :], w1[:, k // HB, (k % HB) * P:(k % HB + 1) * P], xt[b][:, :],
                              start=True, stop=True).then_inc(s_l1, 1)
                pe.wait_ge(s_ge, (c + 1) * EXPERTS * HB)
                for t in range(UTILES):
                    if t >= 2 or not first_of(b, i):
                        pe.wait_ge(s_y, c * UTILES + t - 1)
                    for x in range(EXPERTS):
                        for h in range(HB):
                            last = pe.matmul(ybank[t % 2][:, x * P:(x + 1) * P], hid[:, x * HB + h, t * P:(t + 1) * P],
                                             w2[:, x, h, :], start=(h == 0), stop=(h == HB - 1))
                    last.then_inc(s_l2, 1)

            chunks(pe, body)

        @block.vector
        def _(dve):
            s_step = sem("s_step")

            class Steps:
                k = 0

            st = Steps()

            def link(ins, at):
                ins.then_inc(s_step, 1)
                st.k += 1
                dve.wait_ge(s_step, at + st.k)

            dve.wait_ge(s_c, 2)
            dve.wait_ge(s_w, 64)
            dve.tensor_copy(pos[:, :], posi[:, :])
            dve.tensor_copy(iob[:, :], io[:, :])
            dve.memset(hist[:, :], 0.0)
            dve.memset(fmin[:, :], 0.0)
            dve.memset(base[:, :], float(-ROWS))
            dve.memset(O[1][:, TC, MCH:LCH], LOW)
            dve.memset(O[1][:, TC, LCH:], 0.0).then_inc(s_cv, 1)
            dve.wait_ge(s_cv, 1)

            def decode(b, i, at):
                c = 2 * i + b
                dve.wait_ge(s_key[b], 32 * i + 32)
                if not first_of(b, i, 2):
                    for h in range(2):
                        dve.wait_ge(s_g[b][h], 16 * (TC // 2) * i)
                st.k = 0
                link(dve.tensor_scalar(dst[:, :, :], key[b][:, :, :], NODE_BITS, None, ALU.logical_shift_right), at)
                dve.tensor_tensor(start[b][:, :], dst[:, 0, :], dst[:, 1, :], ALU.not_equal)
                dve.tensor_scalar(low[:, :], key[b][:, 1, :], NODES - 1, None, ALU.bitwise_and)
                link(dve.tensor_scalar(node[:, :], dst[:, 1, :], float(KEY_BASE), None, ALU.subtract), at)
                dve.tensor_scalar(keep[b][:, :], start[b][:, :], -1.0, 1.0, ALU.mult, ALU.add)
                dve.tensor_scalar(neg[b][:, :], start[b][:, :], LOW, None, ALU.mult)
                dve.tensor_scalar(posv[:, :], pos[:, :], base[:, :], None, ALU.add)
                if first_of(b, i):
                    dve.tensor_copy(first[:, :], node[:, 0:1])
                link(dve.tensor_tensor(src[b][:, :], low[:, :], node[:, :], ALU.bitwise_xor), at)
                link(dve.tensor_tensor(posv[:, :], posv[:, :], start[b][:, :], ALU.mult), at)
                dve.tensor_scalar(base[:, :], base[:, :], float(TC), None, ALU.add)
                link(dve.tensor_reduce(cmin[:, :], posv[:, :], AX_X, ALU.min), at)
                link(dve.tensor_tensor(fmin[:, :], fmin[:, :], cmin[:, :], ALU.min), at)
                dve.sem_inc(s_dec, 1)

            def math(b, i, at):
                c = 2 * i + b
                o, g, before = O[b], G[b], O[1 - b]
                for h in range(2):
                    dve.wait_ge(s_g[b][h], 16 * (TC // 2) * (i + 1))
                if first_of(b, i):
                    dve.wait_ge(s_ad, 16)
                if not first_of(b, i, 2):
                    dve.wait_ge(s_st[b], 16 * i)
                G2 = GDIM + GHEADS

                def by_head(t):
                    return t.rearrange("p t h -> p h t")

                bc = [P, GHEADS, TC]
                dve.tensor_copy(o[:, 0, :], before[:, TC, :])
                link(dve.tensor_tensor(adm[:, :, :], by_head(g[:, :, G2:]), start[b][:, :].unsqueeze(1).to_broadcast(bc), ALU.mult), at)
                for h in range(GHEADS):
                    init = ad0[:, G2 + h:G2 + h + 1] if first_of(b, i) else adp[1 - b][:, h, TC - 1:TC]
                    last = dve.tensor_tensor_scan(adp[b][:, h, :], keep[b][:, :], adm[:, h, :], init, ALU.mult, ALU.add)
                link(last, at)
                link(dve.tensor_tensor(e[:, :, :], by_head(g[:, :, GDIM:G2]), adp[b][:, :, :], ALU.add), at)
                link(dve.scalar_tensor_tensor(out=e[:, :, :], in0=e[:, :, :], scalar=0.2, in1=e[:, :, :], op0=ALU.mult, op1=ALU.max), at)
                for h in range(GHEADS):
                    last = dve.tensor_tensor_scan(o[:, 1:, h], neg[b][:, :], e[:, h, :], o[:, 0, h:h + 1], ALU.add, ALU.max)
                link(last, at)
                dve.tensor_tensor(w[:, 1], e[:, :, :], by_head(o[:, 1:, MCH:LCH]), ALU.subtract)
                link(dve.tensor_tensor(w[:, 0], by_head(o[:, 0:TC, MCH:LCH]), by_head(o[:, 1:, MCH:LCH]), ALU.subtract), at)
                dve.scalar_tensor_tensor(out=w[:, 0], in0=w[:, 0], scalar=0.0, in1=neg[b][:, :].unsqueeze(1).to_broadcast(bc),
                                         op0=ALU.min, op1=ALU.add).then_inc(s_lo, 1)
                dve.wait_ge(s_ex, c + 1)
                for h in range(GHEADS):
                    dve.tensor_tensor_scan(o[:, 1:, LCH + h], w[:, 0, h, :], w[:, 1, h, :], o[:, 0, LCH + h:LCH + h + 1], ALU.mult, ALU.add)
                link(dve.tensor_tensor(msg[:, :, :, :], g[:, :, 0:GDIM].rearrange("p t (h e) -> p h e t", h=GHEADS),
                                       w[:, 1].unsqueeze(2).to_broadcast([P, GHEADS, GDIM // GHEADS, TC]), ALU.mult), at)
                for h in range(GHEADS):
                    for x in range(GDIM // GHEADS):
                        k = ACH + h * (GDIM // GHEADS) + x
                        last = dve.tensor_tensor_scan(o[:, 1:, k], w[:, 0, h, :], msg[:, h, x, :], o[:, 0, k:k + 1], ALU.mult, ALU.add)
                last.then_inc(s_math, 1)
                dve.wait_ge(s_math, c + 1)

            def counts(b, i, at):
                c = 2 * i + b
                dve.wait_ge(s_dx[b], 16 * i + 16)
                dve.tensor_scalar(dlo[:, 0, :], dx[b][:, :], P - 1, None, ALU.bitwise_and)
                link(dve.tensor_scalar(dlo[:, 1, :], dx[b][:, :], 7, None, ALU.logical_shift_right), at)
                link(dve.tensor_copy(dlf[:, :, :], dlo[:, :, :]), at)
                dve.sem_inc(s_dxr, 1)
                for t in range(HC):
                    if t >= RING or not first_of(b, i):
                        dve.wait_ge(s_ohp, c * HC + t - RING + 1)
                    dve.tensor_scalar(ohl[:, t % RING, :], iob[:, 0:P], dlf[:, 0, t:t + 1], None, ALU.is_equal)
                    dve.tensor_scalar(ohh[:, t % RING, :], iob[:, :], dlf[:, 1, t:t + 1], None, ALU.is_equal).then_inc(s_oh, 1)
                dve.wait_ge(s_ohp, (c + 1) * HC)
                dve.tensor_tensor(hist[:, :], cbank[b][:, 0:HI], hist[:, :], ALU.add).then_inc(s_hs, 1)

            def outputs(b, i):
                c = 2 * i + b
                if not first_of(b, i, 2):
                    dve.wait_ge(s_yst[b], 16 * i)
                for t in range(UTILES):
                    dve.wait_ge(s_l2, c * UTILES + t + 1)
                    dve.tensor_tensor(yo[b][:, t, :], ybank[t % 2][:, :], b2r[:, :], ALU.add).then_inc(s_y, 1)

            D, M = 6, 7
            C = 2
            decode(0, 0, 0)

            def body(b, i):
                c = 2 * i + b
                at = D + c * (D + M + C)
                if not last_of(b, i):
                    decode(1 - b, i + b, at)
                    assert st.k == D
                    at = at + D
                st.k = 0
                counts(b, i, at)
                assert st.k == C
                outputs(b, i)
                st.k = 0
                math(b, i, at + C)
                assert st.k == M

            chunks(dve, body)


EH = GDIM // GHEADS
VCH = NROW - LCH


def ends(nc, state_rows, last_state, first_start, hist_in, end_rows):
    with ExitStack() as ctx:
        def sb(name, shape, dt=F32):
            return ctx.enter_context(nc.sbuf_tensor("ends_" + name, shape, dt))

        def sem(name):
            return ctx.enter_context(nc.semaphore("ends_" + name))

        hist = sb("hist", [P, HI])
        tri = sb("tri", [P, P])
        ones = sb("ones", [P, P])
        ident = sb("ident", [P, P])
        rowi = sb("rowi", [P, HI], I32)
        rowf = sb("rowf", [P, HI])
        pref = sb("pref", [P, HI])
        tot = sb("tot", [P, HI])
        zero = sb("zero", [P, HI])
        endi = sb("endi", [P, HI], I32)
        ls = sb("ls", [P, NROW])
        fs = sb("fs", [P, 1])
        nost = sb("nost", [P, 1])
        x3 = sb("x3", [P, 3, VCH])
        xt = sb("xt", [VCH, 3, P])
        M = sb("M", [VCH, P + 1])
        V = sb("V", [VCH, P + 1])
        w2 = sb("w2", [VCH, 2, P])
        car = sb("car", [P, 2, VCH])
        old = sb("old", [P, NROW])
        new = sb("new", [P, NROW])
        mm = sb("mm", [P, VCH])
        mo = sb("mo", [P, VCH])
        wc = sb("wc", [P, 2, VCH])
        has = sb("has", [P, 1])
        ri = sb("ri", [P, 2], I32)
        rf = sb("rf", [P, 4])
        bp = ctx.enter_context(nc.psum_tensor("ends_bp", [P, BANK], F32))
        bt = ctx.enter_context(nc.psum_tensor("ends_bt", [P, BANK], F32))
        bx = ctx.enter_context(nc.psum_tensor("ends_bx", [P, BANK], F32))
        bc = ctx.enter_context(nc.psum_tensor("ends_bc", [P, BANK], F32))

        s_in = sem("s_in")
        s_c = sem("s_c")
        s_step = sem("s_step")
        s_pe = sem("s_pe")
        s_act = sem("s_act")
        s_z = sem("s_z")
        s_old = sem("s_old")
        s_new = sem("s_new")
        s_out = sem("s_out")
        mark = {}
        block = ctx.enter_context(nc.Block())

        @block.vector
        def _(dve):
            n = [0]

            def link(ins, name=None):
                ins.then_inc(s_step, 1)
                n[0] += 1
                dve.wait_ge(s_step, n[0])
                if name is not None:
                    mark[name] = n[0]

            dve.wait_ge(s_c, 7)
            dve.wait_ge(s_in, 48)
            dve.tensor_scalar(nost[:, :], fs[:, :], 0.0, LOW, ALU.is_lt, ALU.mult)
            dve.tensor_copy(x3[:, 0, 0:GHEADS], ls[:, MCH:LCH])
            dve.tensor_copy(x3[:, 0, GHEADS:].rearrange("p (h e) -> p h e", e=EH), ls[:, MCH:LCH].unsqueeze(2).to_broadcast([P, GHEADS, EH]))
            link(dve.tensor_copy(x3[:, 1, :], ls[:, LCH:]))
            link(dve.tensor_copy(x3[:, 2, :], nost[:, :].to_broadcast([P, VCH])), "x3")
            dve.tensor_scalar(rf[:, 0:1], fs[:, :], float(ROWS - 1), None, ALU.add)
            link(dve.tensor_scalar(has[:, :], fs[:, :], float(-ROWS), None, ALU.is_gt))
            dve.tensor_copy(rf[:, 1:2], ri[:, 0:1])
            link(dve.tensor_copy(rf[:, 2:3], ri[:, 1:2]))
            link(dve.tensor_tensor(rf[:, 0:1], rf[:, 0:1], rf[:, 1:2], ALU.add))
            link(dve.tensor_tensor(rf[:, 0:1], rf[:, 0:1], rf[:, 2:3], ALU.subtract))
            link(dve.scalar_tensor_tensor(out=rf[:, 3:4], in0=rf[:, 0:1], scalar=has[:, 0:1], in1=rf[:, 2:3], op0=ALU.mult, op1=ALU.add))
            link(dve.tensor_copy(ri[:, 0:1], rf[:, 3:4]), "row")
            dve.wait_ge(s_pe, 1)
            link(dve.tensor_copy(tot[:, :], bt[:, 0:HI]))
            link(dve.tensor_tensor_scan(pref[:, :], tot[:, :], zero[:, :], 0.0, ALU.add, ALU.add))
            link(dve.tensor_tensor(pref[:, :], pref[:, :], tot[:, :], ALU.subtract))
            link(dve.tensor_tensor(pref[:, :], bp[:, 0:HI], pref[:, :], ALU.add))
            link(dve.tensor_copy(rowf[:, :], rowi[:, :]))
            link(dve.tensor_tensor(pref[:, :], pref[:, :], rowf[:, :], ALU.add))
            link(dve.tensor_copy(endi[:, :], pref[:, :]), "ends")
            dve.wait_ge(s_pe, 2)
            link(dve.tensor_copy(xt[:, :, :], bx[0:VCH, 0:3 * P].rearrange("p (a b) -> p a b", a=3)))
            dve.memset(M[:, 0:1], LOW)
            link(dve.memset(V[:, 0:1], 0.0))
            link(dve.tensor_tensor_scan(M[:, 1:], xt[:, 2, :], xt[:, 0, :], M[:, 0:1], ALU.add, ALU.max))
            dve.tensor_tensor(w2[:, 1, :], xt[:, 0, :], M[:, 1:], ALU.subtract)
            link(dve.tensor_tensor(w2[:, 0, :], M[:, 0:P], M[:, 1:], ALU.subtract))
            link(dve.scalar_tensor_tensor(out=w2[:, 0, :], in0=w2[:, 0, :], scalar=0.0, in1=xt[:, 2, :], op0=ALU.min, op1=ALU.add), "w2")
            dve.wait_ge(s_act, 1)
            link(dve.tensor_tensor(xt[:, 1, :], xt[:, 1, :], w2[:, 1, :], ALU.mult))
            link(dve.tensor_tensor_scan(V[:, 1:], w2[:, 0, :], xt[:, 1, :], V[:, 0:1], ALU.mult, ALU.add), "V")
            dve.wait_ge(s_pe, 3)
            link(dve.tensor_copy(car[:, :, :], bc[:, 0:2 * VCH].rearrange("p (a b) -> p a b", a=2)))
            dve.wait_ge(s_old, 16)
            dve.tensor_copy(mo[:, 0:GHEADS], old[:, MCH:LCH])
            link(dve.tensor_copy(mo[:, GHEADS:].rearrange("p (h e) -> p h e", e=EH), old[:, MCH:LCH].unsqueeze(2).to_broadcast([P, GHEADS, EH])))
            link(dve.tensor_tensor(mm[:, :], mo[:, :], car[:, 0, :], ALU.max))
            dve.tensor_tensor(wc[:, 0, :], car[:, 0, :], mm[:, :], ALU.subtract)
            link(dve.tensor_tensor(wc[:, 1, :], mo[:, :], mm[:, :], ALU.subtract), "wc")
            dve.wait_ge(s_act, 2)
            dve.tensor_copy(new[:, MCH:LCH], mm[:, 0:GHEADS])
            dve.tensor_tensor(mo[:, :], wc[:, 0, :], car[:, 1, :], ALU.mult)
            link(dve.tensor_tensor(new[:, LCH:], wc[:, 1, :], old[:, LCH:], ALU.mult))
            link(dve.tensor_tensor(new[:, LCH:], new[:, LCH:], mo[:, :], ALU.add), "new")

        @block.sync
        def _(sp):
            sp.dma_start(hist[:, :], hist_in).then_inc(s_in, 16)
            sp.dma_start(ls[:, :], last_state).then_inc(s_in, 16)
            sp.dma_start(fs[:, :], first_start).then_inc(s_in, 16)
            sp.wait_ge(s_c, 7)
            sp.dma_start(state_rows[SORTED:SORTED + P, :], zero[:, 0:NROW]).then_inc(s_z, 16)
            sp.wait_ge(s_step, mark["ends"])
            sp.dma_start(end_rows, endi[:, :]).then_inc(s_out, 16)
            sp.wait_ge(s_out, 16)
            sp.wait_ge(s_new, 16)

        @block.gpsimd
        def _(pool):
            pool.memset(ones[:, :], 1.0).then_inc(s_c, 1)
            pool.memset(zero[:, :], 0.0).then_inc(s_c, 1)
            pool.wait_ge(s_c, 2)
            pool.affine_select(out=tri[:, :], in_=ones[:, :], compare_op=ALU.is_ge, fill=0.0, base=0,
                               pattern=[[1, P]], channel_multiplier=-1).then_inc(s_c, 1)
            pool.affine_select(out=ident[:, :], in_=zero[:, 0:P], compare_op=ALU.not_equal, fill=1.0, base=0,
                               pattern=[[-1, P]], channel_multiplier=1).then_inc(s_c, 1)
            pool.iota(rowi[:, :], pattern=[[P, HI]], base=0, channel_multiplier=1).then_inc(s_c, 1)
            pool.iota(ri[:, 0:1], pattern=[[0, 1]], base=0, channel_multiplier=ROWS).then_inc(s_c, 1)
            pool.iota(ri[:, 1:2], pattern=[[0, 1]], base=SORTED, channel_multiplier=1).then_inc(s_c, 1)
            pool.wait_ge(s_step, mark["row"])
            pool.wait_ge(s_z, 16)
            pool.indirect_dma_start(old[:, :], None, state_rows, bass.IndirectOffsetOnAxis(ap=ri[:, 0:1], axis=0)).then_inc(s_old, 16)
            pool.wait_ge(s_step, mark["new"])
            pool.indirect_dma_start(state_rows, bass.IndirectOffsetOnAxis(ap=ri[:, 0:1], axis=0), new[:, :], None).then_inc(s_new, 16)

        @block.tensor
        def _(pe):
            pe.wait_ge(s_c, 7)
            pe.wait_ge(s_in, 48)
            pe.matmul(bp[:, 0:HI], tri[:, :], hist[:, :], start=True, stop=True)
            pe.matmul(bt[:, 0:HI], ones[:, :], hist[:, :], start=True, stop=True).then_inc(s_pe, 1)
            pe.wait_ge(s_step, mark["x3"])
            for k in range(3):
                last = pe.transpose(bx[0:VCH, k * P:(k + 1) * P], x3[:, k, :], ident[:, :])
            last.then_inc(s_pe, 1)
            pe.wait_ge(s_step, mark["V"])
            pe.transpose(bc[:, 0:VCH], M[:, 0:P], ident[0:VCH, 0:VCH])
            pe.transpose(bc[:, VCH:2 * VCH], V[:, 0:P], ident[0:VCH, 0:VCH]).then_inc(s_pe, 1)

        @block.scalar
        def _(act):
            act.wait_ge(s_step, mark["w2"])
            act.activation(w2[:, :, :], w2[:, :, :], ACT.Exp).then_inc(s_act, 1)
            act.wait_ge(s_step, mark["wc"])
            act.activation(wc[:, :, :], wc[:, :, :], ACT.Exp).then_inc(s_act, 1)


def combine(nc, state_rows, end_rows, expert_out, x2_rows, b_gat, gamma, beta, out):
    BATCH = 8
    BT = BATCH * TILES
    BUFS = 4
    BATCHES = IMAGES // BATCH
    ROUNDS = BATCH // BUFS
    BY_VECTOR = 2

    with ExitStack() as ctx:
        def sb(name, shape, dt=F32):
            return ctx.enter_context(nc.sbuf_tensor("comb_" + name, shape, dt))

        def sem(name):
            return ctx.enter_context(nc.semaphore("comb_" + name))

        par = sb("par", [P, 3, GDIM])
        endt = sb("endt", [P, HI + BT], I32)
        ix = sb("ix", [P, BT], I32)
        srow = sb("srow", [P, BT, NROW])
        ye = [sb(f"ye{b}", [P, TILES, EXPERTS * P]) for b in range(BUFS)]
        xr = [sb(f"xr{b}", [P, TILES, P]) for b in range(BUFS)]
        res = [sb(f"res{b}", [P, TILES, P]) for b in range(BUFS)]
        l = sb("l", [P, BT, GHEADS])
        agg = sb("agg", [P, BT, GHEADS, EH])
        sq = sb("sq", [P, BT, GDIM])
        mu = sb("mu", [P, BT])
        var = sb("var", [P, BT])
        nh = sb("nh", [P, BT])
        ny = sb("ny", [P, BT])
        nt = sb("nt", [P, BT])
        sc = sb("sc", [P, BT, EXPERTS])
        beat = sb("beat", [P, BT])
        rank = sb("rank", [P, BT, EXPERTS])
        mx = sb("mx", [P, BT])
        gate = sb("gate", [P, BT, EXPERTS])
        s_in = sem("s_in")
        s_spare = sem("s_spare")
        s_ix = sem("s_ix")
        s_passed = sem("s_passed")
        s_rows = sem("s_rows")
        s_read = sem("s_read")
        s_ye = [sem(f"s_ye{b}") for b in range(BUFS)]
        s_xr = [sem(f"s_xr{b}") for b in range(BUFS)]
        s_step = sem("s_step")
        s_lo = sem("s_lo")
        s_ex = sem("s_ex")
        s_gate = sem("s_gate")
        s_scaled = sem("s_scaled")
        s_res = sem("s_res")
        s_st = [sem(f"s_st{b}") for b in range(BUFS)]

        def batches(eng, body):
            body(0)
            with eng.Fori(1, BATCHES) as k:
                body(k)

        def first_use(k, r):
            return isinstance(k, int) and k == 0 and r == 0

        block = ctx.enter_context(nc.Block())

        @block.sync
        def _(sp):
            sp.dma_start(endt[:, 0:HI], end_rows).then_inc(s_in, 16)
            for k, v in enumerate((b_gat, gamma, beta)):
                sp.dma_start(par[:, k, :], v.rearrange("(o e) -> o e", o=1).to_broadcast([P, GDIM])).then_inc(s_in, 16)

            def body(k):
                for r in range(ROUNDS):
                    for b in range(BUFS):
                        m = k * BATCH + r * BUFS + b
                        if not first_use(k, r):
                            sp.wait_ge(s_res, m - BUFS + 1)
                        sp.dma_start(ye[b][:, :, :], expert_out[m].rearrange("h (t p) d -> p (h t) d", p=P)).then_inc(s_ye[b], 16)

            batches(sp, body)

        @block.scalar
        def _(act):
            def load(b, m):
                act.dma_start(xr[b][:, :, :], x2_rows[m].rearrange("(j p) d -> p j d", p=P)).then_inc(s_xr[b], 16)

            for b in range(BUFS):
                load(b, b)

            def weigh(k, r, b):
                act.wait_ge(s_ye[b], 16 * (k * ROUNDS + r) + 16)
                for x in range(BY_VECTOR, EXPERTS):
                    for t in range(TILES):
                        part = ye[b][:, t, x * P:(x + 1) * P]
                        g = (r * BUFS + b) * TILES + t
                        last = act.activation(part, part, ACT.Copy, scale=gate[:, g, x:x + 1])
                last.then_inc(s_scaled, 1)

            def store(k, r, b, loads):
                m = k * BATCH + r * BUFS + b
                act.wait_ge(s_res, m + 1)
                act.dma_start(out[m].rearrange("(j p) d -> p j d", p=P), res[b][:, :, :]).then_inc(s_st[b], 16)
                if loads:
                    load(b, m + BUFS)

            def body(k, last):
                act.wait_ge(s_lo, k + 1)
                act.activation(gate[:, :, :], gate[:, :, :], ACT.Exp).then_inc(s_ex, 1)
                act.wait_ge(s_gate, k + 1)
                for i in range(BATCH):
                    weigh(k, i // BUFS, i % BUFS)
                    if i:
                        store(k, (i - 1) // BUFS, (i - 1) % BUFS, not last or i <= BATCH - BUFS)
                store(k, ROUNDS - 1, BUFS - 1, not last)

            with act.Fori(0, BATCHES - 1) as k:
                body(k, False)
            body(BATCHES - 1, True)
            for b in range(BUFS):
                act.wait_ge(s_st[b], 16 * IMAGES // BUFS)

        @block.gpsimd
        def _(pool):
            def body(k):
                pool.wait_ge(s_ix, k + 1)
                if not (isinstance(k, int) and k == 0):
                    pool.wait_ge(s_read, k)
                pool.sem_inc(s_passed, 1)
                for t in range(BT):
                    pool.indirect_dma_start(srow[:, t, :], None, state_rows,
                                            bass.IndirectOffsetOnAxis(ap=ix[:, t:t + 1], axis=0)).then_inc(s_rows, 16)

            batches(pool, body)

        @block.vector
        def _(dve):
            LINKS = 47
            SUMS = BATCH * (EXPERTS - 1)
            dve.wait_ge(s_in, 64)
            dve.memset(endt[:, HI:], 0.0).then_inc(s_spare, 1)
            dve.tensor_copy(ix[:, :], endt[:, 0:BT]).then_inc(s_ix, 1)
            dve.wait_ge(s_spare, 1)
            n = [0]

            def body(k):
                n[0] = 0

                def link(ins):
                    ins.then_inc(s_step, 1)
                    n[0] += 1
                    dve.wait_ge(s_step, k * (LINKS + SUMS) + n[0])

                def by_token(t, n=GDIM):
                    return t.unsqueeze(2).to_broadcast([P, BT, n])

                def by_feature(x):
                    return par[:, x, :].unsqueeze(1).to_broadcast([P, BT, GDIM])

                dve.wait_ge(s_rows, 16 * BT * (k + 1))
                flat = agg[:, :, :, :].rearrange("p t h e -> p t (h e)")
                link(dve.tensor_scalar(l[:, :, :], srow[:, :, LCH:ACH], 1e-16, None, ALU.add))
                link(dve.reciprocal(l[:, :, :], l[:, :, :]))
                link(dve.tensor_tensor(agg[:, :, :, :], srow[:, :, ACH:].rearrange("p t (h e) -> p t h e", e=EH),
                                       l[:, :, :].unsqueeze(3).to_broadcast([P, BT, GHEADS, EH]), ALU.mult))
                dve.sem_inc(s_read, 1)
                nxt = endt[:, BT:2 * BT] if isinstance(k, int) else endt[:, bass.ds((k + 1) * BT, BT)]
                dve.tensor_copy(ix[:, :], nxt).then_inc(s_ix, 1)
                link(dve.tensor_tensor(flat, flat, by_feature(0), ALU.add))
                link(dve.tensor_reduce(mu[:, :], flat, AX_X, ALU.add))
                link(dve.tensor_scalar(mu[:, :], mu[:, :], 1.0 / GDIM, None, ALU.mult))
                link(dve.tensor_tensor(flat, flat, by_token(mu[:, :]), ALU.subtract))
                link(dve.tensor_tensor(sq[:, :, :], flat, flat, ALU.mult))
                link(dve.tensor_reduce(var[:, :], sq[:, :, :], AX_X, ALU.add))
                link(dve.tensor_scalar(var[:, :], var[:, :], 1.0 / GDIM, EPS_TOKEN, ALU.mult, ALU.add))
                link(dve.tensor_scalar(nh[:, :].bitcast(I32), var[:, :].bitcast(I32), 1, None, ALU.logical_shift_right))
                link(dve.tensor_scalar(ny[:, :].bitcast(I32), nh[:, :].bitcast(I32), -1.0, float(0x5F3759DF), ALU.mult, ALU.add))
                for _ in range(4):
                    link(dve.tensor_tensor(nt[:, :], ny[:, :], ny[:, :], ALU.mult))
                    link(dve.scalar_tensor_tensor(out=nh[:, :], in0=nt[:, :], scalar=-0.5, in1=var[:, :], op0=ALU.mult, op1=ALU.mult))
                    link(dve.scalar_tensor_tensor(out=ny[:, :], in0=nh[:, :], scalar=1.5, in1=ny[:, :], op0=ALU.add, op1=ALU.mult))
                link(dve.tensor_tensor(flat, flat, by_token(ny[:, :]), ALU.mult))
                link(dve.tensor_tensor(flat, flat, by_feature(1), ALU.mult))
                link(dve.tensor_tensor(flat, flat, by_feature(2), ALU.add))
                link(dve.tensor_reduce(sc[:, :, :], agg[:, :, :, :].rearrange("p t h e -> p t e h"), AX_X, ALU.add))
                link(dve.tensor_scalar(sc[:, :, :], sc[:, :, :], 1.0 / GHEADS, None, ALU.mult))
                dve.memset(rank[:, :, :], 0.0)
                link(dve.tensor_reduce(mx[:, :], sc[:, :, :], AX_X, ALU.max))
                for u in range(EXPERTS):
                    for v in range(u + 1, EXPERTS):
                        link(dve.tensor_tensor(beat[:, :], sc[:, :, u], sc[:, :, v], ALU.is_ge))
                        dve.tensor_tensor(rank[:, :, v], rank[:, :, v], beat[:, :], ALU.add)
                        link(dve.scalar_tensor_tensor(out=rank[:, :, u], in0=rank[:, :, u], scalar=1.0, in1=beat[:, :],
                                                      op0=ALU.add, op1=ALU.subtract))
                link(dve.tensor_scalar(rank[:, :, :], rank[:, :, :], 2.0, None, ALU.is_lt))
                dve.tensor_tensor(gate[:, :, :], sc[:, :, :], by_token(mx[:, :], EXPERTS), ALU.subtract).then_inc(s_lo, 1)
                dve.wait_ge(s_ex, k + 1)
                link(dve.tensor_tensor(gate[:, :, :], gate[:, :, :], rank[:, :, :], ALU.mult))
                link(dve.tensor_reduce(mx[:, :], gate[:, :, :], AX_X, ALU.add))
                link(dve.reciprocal(mx[:, :], mx[:, :]))
                link(dve.tensor_tensor(gate[:, :, :], gate[:, :, :], by_token(mx[:, :], EXPERTS), ALU.mult))
                dve.sem_inc(s_gate, 1)
                assert n[0] == LINKS, n[0]
                for r in range(ROUNDS):
                    for b in range(BUFS):
                        use = k * ROUNDS + r
                        dve.wait_ge(s_ye[b], 16 * use + 16)
                        dve.wait_ge(s_xr[b], 16 * use + 16)
                        if not first_use(k, r):
                            dve.wait_ge(s_st[b], 16 * use)
                        tile0 = (r * BUFS + b) * TILES
                        for x in range(EXPERTS):
                            if x < BY_VECTOR:
                                for t in range(TILES):
                                    before = xr[b][:, t, :] if x == 0 else res[b][:, t, :]
                                    last = dve.scalar_tensor_tensor(out=res[b][:, t, :], in0=ye[b][:, t, x * P:(x + 1) * P],
                                                                    scalar=gate[:, tile0 + t, x:x + 1], in1=before,
                                                                    op0=ALU.mult, op1=ALU.add)
                            else:
                                if x == BY_VECTOR:
                                    dve.wait_ge(s_scaled, k * BATCH + r * BUFS + b + 1)
                                last = dve.tensor_tensor(res[b][:, :, :], res[b][:, :, :], ye[b][:, :, x * P:(x + 1) * P], ALU.add)
                            if x < EXPERTS - 1:
                                link(last)
                        last.then_inc(s_res, 1)

            batches(dve, body)


def window_attention_graph_experts(nc, x, w_qkv, b_qkv, w_o, b_o, w_gat, att_src, att_dst, b_gat,
                                   gamma, beta, w1, b1, w2, b2, edge_index, out):
    def dram(name, shape, dt=F32):
        return nc.dram_tensor(name, shape, dt, kind="Internal").ap()

    sorted_keys = dram("sorted_keys", (1 + SORTED, 1))
    x2_rows = dram("x2_rows", (IMAGES, TOKENS, P))
    tokens_t = dram("tokens_t", (IMAGES, P, TOKENS))
    node_rows = dram("node_rows", (IMAGES, TOKENS, NROW))
    state_rows = dram("state_rows", (SORTED + P, NROW))
    expert_out = dram("expert_out", (IMAGES, TOKENS // UNIT, UNIT, EXPERTS * P))
    last_state = dram("last_state", (P, NROW))
    first_start = dram("first_start", (P, 1))
    counts = dram("counts", (P, HI))
    end_rows = dram("end_rows", (P, HI), I32)

    with ExitStack() as ctx:
        keys = [ctx.enter_context(nc.sbuf_tensor(f"keys{i}", [P, COLS], F32)) for i in range(2)]
        sign = ctx.enter_context(nc.sbuf_tensor("sign", [P, PART_BITS], F32))
        attention(nc, x, w_qkv, b_qkv, w_o, b_o, w_gat, att_src, att_dst, edge_index, keys, sign,
                  x2_rows, tokens_t, node_rows)
        sort_partitions(nc, keys, sign, sorted_keys)
    edges(nc, sorted_keys.bitcast(I32), node_rows.rearrange("i t d -> (i t) d"), edge_index, tokens_t,
          w1, b1, w2, b2, state_rows, expert_out, last_state, first_start, counts)
    ends(nc, state_rows, last_state, first_start, counts, end_rows)
    combine(nc, state_rows, end_rows, expert_out, x2_rows, b_gat, gamma, beta, out)


INPUTS = ["x", "L0_conv_w_qkv", "L0_conv_b_qkv", "L0_conv_w_o", "L0_conv_b_o", "L0_ffn_W_gat", "L0_ffn_att_src",
          "L0_ffn_att_dst", "L0_ffn_b_gat", "L0_ffn_ln_gamma", "L0_ffn_ln_beta", "L0_ffn_W1", "L0_ffn_b1",
          "L0_ffn_W2", "L0_ffn_b2", "L0_ffn_edge_index"]


def kernel(**inputs):
    import numpy as np
    import concourse.bacc as bacc
    from concourse.bass_utils import run_bass_kernel_spmd

    nc = bacc.Bacc("TRN2", target_bir_lowering=False, num_devices=1)
    arrays, args = {}, []
    for name in INPUTS:
        a = np.ascontiguousarray(inputs[name])
        arrays["in_" + name] = a
        args.append(nc.dram_tensor("in_" + name, a.shape, mybir.dt.from_np(a.dtype), kind="ExternalInput").ap())
    out = nc.dram_tensor("out", (IMAGES, TOKENS, P), F32, kind="ExternalOutput").ap()
    window_attention_graph_experts(nc, *args, out)
    result = run_bass_kernel_spmd(nc, [arrays], core_ids=[0])
    return result.results[0]["out"].reshape(inputs["x"].shape)
```
